# Optimizing a Trainium2 kernel written in Bass

```python
import numpy as np
import jax
import jax.numpy as jnp

def _softmax(x, axis=-1):
    return jax.nn.softmax(x, axis=axis)

def _gelu(x):
    return jax.nn.gelu(x, approximate=True)

def _silu(x):
    return jax.nn.silu(x)

def _sigmoid(x):
    return jax.nn.sigmoid(x)

def _layernorm(x, axis=-1, eps=1e-05):
    m = jnp.mean(x, axis=axis, keepdims=True)
    v = jnp.var(x, axis=axis, keepdims=True)
    return (x - m) / jnp.sqrt(v + eps)

def _scatter_add(tgt, idx, src, axis=0):
    return tgt.at[idx].add(src)

def _segment_sum(src, seg, n):
    return jax.ops.segment_sum(src, seg, n)
kernel_name = 'mk_decoder_postln_d4_seqx_r4_2b7e84'

def setup_inputs(seed: int=0):
    np.random.seed(seed)
    _w = jnp.asarray

    def _rec_inputs():
        import jax
        import jax.numpy as jnp
        _rk = jax.random.key(seed)
        x = 7.22e-05 + 1 * jax.random.normal(jax.random.fold_in(_rk, 1), (4, 512, 512), jnp.float32)
        _lenS = 512 - jax.random.randint(jax.random.fold_in(_rk, 7), (4,), 0, max(1, 512 // 4) + 1, jnp.int32)
        _lenS2 = 512 - jax.random.randint(jax.random.fold_in(_rk, 8), (4,), 0, max(1, 512 // 4) + 1, jnp.int32)
        _ctx_512P = jax.random.normal(jax.random.fold_in(_rk, 11), (4, 16, 128), jnp.float32)
        _ctx_512c = jax.random.dirichlet(jax.random.fold_in(_rk, 511), 0.3 * jnp.ones((16,), jnp.float32), (4, 512))
        _ctx_512t = jnp.einsum('bsk,bkd->bsd', _ctx_512c, _ctx_512P)
        _ctx_512t = _ctx_512t * jax.lax.rsqrt(jnp.mean(jnp.square(_ctx_512t)) + 1e-12) * 0.953939
        ctx_512 = -0.000514642 + 1.00011 * (_ctx_512t + 0.3 * jax.random.normal(jax.random.fold_in(_rk, 611), (4, 512, 128), jnp.float32))
        return (x, ctx_512)
    x, ctx_512 = _rec_inputs()

    def _L0_attn_setup():
        import jax, jax.numpy as jnp
        import numpy as np
        BLOCK = 64
        EPS = 1e-06

        def _silu(x):
            return x * jax.nn.sigmoid(x)
        key = jax.random.key(seed)
        k1, k2, k3, k4 = jax.random.split(key, 4)
        embed_dim, hidden_dim = (512, 512)
        b, n, h = (2, 1024, 16)
        x = jax.random.normal(k1, (b, n, embed_dim), dtype=jnp.float32)
        slope_rate = jax.random.uniform(k2, (h, 1, 1), dtype=jnp.float32, minval=0.01, maxval=1.0)
        W_qkvu = jax.random.normal(k3, (4 * hidden_dim, embed_dim), dtype=jnp.float32) / np.sqrt(embed_dim)
        W_out = jax.random.normal(k4, (embed_dim, hidden_dim), dtype=jnp.float32) / np.sqrt(hidden_dim)
        return {'x': x, 'slope_rate': slope_rate, 'W_qkvu': W_qkvu, 'W_out': W_out}
    _L0_attn_all = _L0_attn_setup()
    _L0_attn_in = {k: v for k, v in _L0_attn_all.items() if k in ('slope_rate', 'W_qkvu', 'W_out')}
    del _L0_attn_all

    def _L0_xattn_setup():
        import jax, jax.numpy as jnp
        import numpy as np
        import math
        NUM_Q_HEADS = 32
        NUM_KV_HEADS = 8
        key = jax.random.key(seed)
        k1, k2, k3 = jax.random.split(key, 3)
        B, S, E = (2, 512, 512)
        kv_E = NUM_KV_HEADS * (E // NUM_Q_HEADS)
        q = jax.random.normal(k1, (B, S, E), dtype=jnp.float32)
        k = jax.random.normal(k2, (B, S, kv_E), dtype=jnp.float32)
        v = jax.random.normal(k3, (B, S, kv_E), dtype=jnp.float32)
        return {'q': q, 'k': k, 'v': v}
    _L0_xattn_all = _L0_xattn_setup()
    _L0_xattn_in = {k: v for k, v in _L0_xattn_all.items() if k in ()}
    del _L0_xattn_all

    def _L0_ffn_setup():
        import jax, jax.numpy as jnp
        import numpy as np
        HID = 512
        INTER = 2048
        NEXP = 8
        TOPK = 2
        EPS = 1e-05

        def _mock_fused_moe(x, selected_experts, routing_weights, expert_weight):
            y = jnp.einsum('bsh,hd->bsd', x, expert_weight)
            scale = routing_weights.sum(axis=-1, keepdims=True)
            return y * scale
        key = jax.random.key(seed)
        ks = jax.random.split(key, 6)
        s = lambda fan_in: 1.0 / np.sqrt(fan_in)
        return {'hidden_states': jax.random.normal(ks[0], (4, 1024, HID), dtype=jnp.float32), 'gate_w': jax.random.uniform(ks[1], (HID, NEXP), jnp.float32, -s(HID), s(HID)), 'up_w': jax.random.uniform(ks[2], (HID, INTER), jnp.float32, -s(HID), s(HID)), 'down_w': jax.random.uniform(ks[3], (INTER, HID), jnp.float32, -s(INTER), s(INTER)), 'expert_weight': jax.random.normal(ks[4], (HID, HID), dtype=jnp.float32), 'ln_gamma': jnp.ones((HID,), jnp.float32), 'ln_beta': jnp.zeros((HID,), jnp.float32)}
    _L0_ffn_all = _L0_ffn_setup()
    _L0_ffn_in = {k: v for k, v in _L0_ffn_all.items() if k in ('gate_w', 'up_w', 'down_w', 'expert_weight', 'ln_gamma', 'ln_beta')}
    del _L0_ffn_all

    def _L1_attn_setup():
        import jax, jax.numpy as jnp
        import numpy as np
        from jax import lax
        SPLIT = 8
        DIM = 16
        EPS = 1e-05

        def _branch(q, k, v, cw, cb, H_sp, W_sp, Hg, Wg):
            B, N, C = q.shape
            hd = C
            scale = hd ** (-0.5)
            wsz = H_sp * W_sp
            nh, nw = (Hg // H_sp, Wg // W_sp)

            def part(t):
                t = t.reshape(B, nh, H_sp, nw, W_sp, C).transpose(0, 1, 3, 2, 4, 5)
                return t.reshape(-1, wsz, 1, hd).transpose(0, 2, 1, 3)
            vimg = v.reshape(B, nh, H_sp, nw, W_sp, C).transpose(0, 1, 3, 5, 2, 4)
            vimg = vimg.reshape(-1, C, H_sp, W_sp)
            lepe = lax.conv_general_dilated(vimg, cw, (1, 1), [(1, 1), (1, 1)], dimension_numbers=('NCHW', 'OIHW', 'NCHW'), feature_group_count=C)
            lepe = lepe + cb[None, :, None, None]
            lepe = lepe.reshape(-1, 1, hd, wsz).transpose(0, 1, 3, 2)
            vw = vimg.reshape(-1, 1, hd, wsz).transpose(0, 1, 3, 2)
            attn = jax.nn.softmax(part(q) * scale @ jnp.swapaxes(part(k), -1, -2), axis=-1)
            out = attn @ vw + lepe
            out = out.transpose(0, 2, 1, 3).reshape(B, nh, nw, H_sp, W_sp, C)
            out = out.transpose(0, 1, 3, 2, 4, 5).reshape(B, N, C)
            return out
        key = jax.random.key(seed)
        ks = jax.random.split(key, 8)
        B, H, W = (8, 512, 512)
        d = DIM
        h = d // 2
        return {'x': jax.random.normal(ks[0], (B, H, W), jnp.float32), 'qkv_w': jax.random.normal(ks[1], (d, 3 * d), jnp.float32) * d ** (-0.5), 'conv_w0': jax.random.normal(ks[2], (h, 1, 3, 3), jnp.float32) * 0.3, 'conv_b0': jax.random.normal(ks[3], (h,), jnp.float32) * 0.02, 'conv_w1': jax.random.normal(ks[4], (h, 1, 3, 3), jnp.float32) * 0.3, 'conv_b1': jax.random.normal(ks[5], (h,), jnp.float32) * 0.02, 'proj_w': jax.random.normal(ks[6], (d, d), jnp.float32) * d ** (-0.5), 'proj_b': jax.random.normal(ks[7], (d,), jnp.float32) * 0.02, 'ln_w': jnp.ones((d,), jnp.float32), 'ln_b': jnp.zeros((d,), jnp.float32)}
    _L1_attn_all = _L1_attn_setup()
    _L1_attn_in = {k: v for k, v in _L1_attn_all.items() if k in ('qkv_w', 'conv_w0', 'conv_b0', 'conv_w1', 'conv_b1', 'proj_w', 'proj_b', 'ln_w', 'ln_b')}
    del _L1_attn_all

    def _L1_xattn_setup():
        import jax, jax.numpy as jnp
        import numpy as np
        B, N, D = (16, 512, 128)
        H = 4
        TOP_K_RATIO = 0.3
        key = jax.random.key(seed)
        k1, k2, k3, k4 = jax.random.split(key, 4)
        h = jax.random.normal(k1, (B, N, D), dtype=jnp.float32)
        adj_raw = jax.random.uniform(k2, (B, N, N), dtype=jnp.float32)
        lim = 1.0 / np.sqrt(D)
        Wq = jax.random.uniform(k3, (D, D), minval=-lim, maxval=lim, dtype=jnp.float32)
        Wk = jax.random.uniform(k4, (D, D), minval=-lim, maxval=lim, dtype=jnp.float32)
        gamma_raw = jnp.float32(-0.85)
        return {'h': h, 'adj_raw': adj_raw, 'Wq': Wq, 'Wk': Wk, 'gamma_raw': gamma_raw}
    _L1_xattn_all = _L1_xattn_setup()
    _L1_xattn_in = {k: v for k, v in _L1_xattn_all.items() if k in ('Wq', 'Wk', 'gamma_raw')}
    del _L1_xattn_all

    def _L1_ffn_setup():
        import jax, jax.numpy as jnp
        import numpy as np
        ACT_BITS = 8
        EPS = 1e-05

        def act_quant(x, bits=ACT_BITS):
            qb = float(2 ** (bits - 1))
            scale = qb / jnp.clip(jnp.max(jnp.abs(x), axis=-1, keepdims=True), EPS)
            xq = jnp.clip(jnp.round(x * scale), -qb, qb - 1) / scale
            return x + jax.lax.stop_gradient(xq - x)

        def weight_quant(w):
            scale = 1.0 / jnp.clip(jnp.mean(jnp.abs(w)), EPS)
            wq = jnp.clip(jnp.round(w * scale), -1.0, 1.0) / scale
            return w + jax.lax.stop_gradient(wq - w)

        def fwht(x):
            shape = x.shape
            n = shape[-1]
            x = x.reshape(-1, n)
            h = 1
            while h < n:
                x = x.reshape(-1, n // (2 * h), 2, h)
                a, b = (x[..., 0, :], x[..., 1, :])
                x = jnp.stack([a + b, a - b], axis=-2).reshape(-1, n)
                h *= 2
            return (x * (1.0 / np.sqrt(n)).astype(np.float32)).reshape(shape)

        def bitlinear(x, w):
            return jnp.einsum('bsh,oh->bso', act_quant(x), weight_quant(w))

        def h_bitlinear(x, w):
            return jnp.einsum('bsh,oh->bso', act_quant(fwht(x)), weight_quant(w))
        key = jax.random.key(seed)
        k1, k2, k3, k4 = jax.random.split(key, 4)
        H, I = (512, 2048)
        B, S = (4, 512)
        std_in = 1.0 / np.sqrt(H)
        std_mid = 1.0 / np.sqrt(I)
        return {'x': jax.random.normal(k1, (B, S, H), dtype=jnp.float32), 'w_gate': jax.random.normal(k2, (I, H), dtype=jnp.float32) * std_in, 'w_up': jax.random.normal(k3, (I, H), dtype=jnp.float32) * std_in, 'w_down': jax.random.normal(k4, (H, I), dtype=jnp.float32) * std_mid}
    _L1_ffn_all = _L1_ffn_setup()
    _L1_ffn_in = {k: v for k, v in _L1_ffn_all.items() if k in ('w_gate', 'w_up', 'w_down')}
    del _L1_ffn_all

    def _L2_attn_setup():
        import math
        import jax, jax.numpy as jnp
        import numpy as np
        B, S, H = (2, 512, 512)
        NH = 16
        HD = H // NH
        key = jax.random.key(seed)
        ks = jax.random.split(key, 9)
        scale = 1.0 / math.sqrt(H)
        return {'x': jax.random.normal(ks[0], (B, S, H), dtype=jnp.float32), 'WQ_w': jax.random.normal(ks[1], (H, H), dtype=jnp.float32) * scale, 'WQ_b': jax.random.normal(ks[2], (H,), dtype=jnp.float32) * 0.01, 'WK_w': jax.random.normal(ks[3], (H, H), dtype=jnp.float32) * scale, 'WK_b': jax.random.normal(ks[4], (H,), dtype=jnp.float32) * 0.01, 'WV_w': jax.random.normal(ks[5], (H, H), dtype=jnp.float32) * scale, 'WV_b': jax.random.normal(ks[6], (H,), dtype=jnp.float32) * 0.01, 'WO_w': jax.random.normal(ks[7], (H, H), dtype=jnp.float32) * scale, 'WO_b': jax.random.normal(ks[8], (H,), dtype=jnp.float32) * 0.01}
    _L2_attn_all = _L2_attn_setup()
    _L2_attn_in = {k: v for k, v in _L2_attn_all.items() if k in ('WQ_w', 'WQ_b', 'WK_w', 'WK_b', 'WV_w', 'WV_b', 'WO_w', 'WO_b')}
    del _L2_attn_all

    def _L2_xattn_setup():
        import jax, jax.numpy as jnp
        import numpy as np
        B, S, H, NH, L = (2, 512, 512, 16, 128)
        HD = H // NH
        key = jax.random.key(seed)
        k1, k2, k3, k4, k5 = jax.random.split(key, 5)
        scale = 0.02
        return {'q': jax.random.normal(k1, (B, S, H), dtype=jnp.float32), 'latent_kv': jax.random.normal(k2, (B, S, L), dtype=jnp.float32), 'Wq': jax.random.normal(k3, (H, H), dtype=jnp.float32) * scale, 'Wkv_expand': jax.random.normal(k4, (2 * H, L), dtype=jnp.float32) * scale, 'Wout': jax.random.normal(k5, (H, H), dtype=jnp.float32) * scale}
    _L2_xattn_all = _L2_xattn_setup()
    _L2_xattn_in = {k: v for k, v in _L2_xattn_all.items() if k in ('Wq', 'Wkv_expand', 'Wout')}
    del _L2_xattn_all

    def _L2_ffn_setup():
        import jax, jax.numpy as jnp
        import numpy as np
        B, S, H = (2, 512, 512)
        E, K, I = (64, 8, 192)

        def _moe_forward(hidden_states, gate_weight, w_gate, w_up, w_down):
            b, s, h = hidden_states.shape
            x = hidden_states.reshape(-1, h)
            logits = x.astype(jnp.float32) @ gate_weight.astype(jnp.float32).T
            scores = jax.nn.softmax(logits, axis=-1)
            topk_w, topk_idx = jax.lax.top_k(scores, K)
            topk_w = topk_w / jnp.sum(topk_w, axis=-1, keepdims=True)
            flat_ids = topk_idx.reshape(-1)
            expanded = jnp.repeat(x, K, axis=0)
            order = jnp.argsort(flat_ids)
            sorted_tokens = expanded[order]
            group_sizes = jnp.zeros((E,), jnp.int32).at[flat_ids].add(1)
            g = jax.lax.ragged_dot(sorted_tokens, w_gate, group_sizes)
            u = jax.lax.ragged_dot(sorted_tokens, w_up, group_sizes)
            out = jax.lax.ragged_dot(jax.nn.silu(g) * u, w_down, group_sizes)
            inv = jnp.argsort(order)
            outs = out[inv].reshape(-1, K, h)
            y = jnp.sum(outs * topk_w[:, :, None], axis=1)
            return y.reshape(b, s, h)
        key = jax.random.key(seed)
        k0, k1, k2, k3, k4 = jax.random.split(key, 5)
        hidden_states = jax.random.normal(k0, (B, S, H), dtype=jnp.float32)
        gate_weight = jax.random.normal(k1, (E, H), dtype=jnp.float32) * 0.02
        w_gate = jax.random.normal(k2, (E, H, I), dtype=jnp.float32) * 0.02
        w_up = jax.random.normal(k3, (E, H, I), dtype=jnp.float32) * 0.02
        w_down = jax.random.normal(k4, (E, I, H), dtype=jnp.float32) * 0.02
        return {'hidden_states': hidden_states, 'gate_weight': gate_weight, 'w_gate': w_gate, 'w_up': w_up, 'w_down': w_down}
    _L2_ffn_all = _L2_ffn_setup()
    _L2_ffn_in = {k: v for k, v in _L2_ffn_all.items() if k in ('gate_weight', 'w_gate', 'w_up', 'w_down')}
    del _L2_ffn_all

    def _L3_attn_setup():
        import jax, jax.numpy as jnp
        import numpy as np
        NUM_HEADS = 16
        B, S, E = (4, 512, 512)
        key = jax.random.key(seed)
        kx, kq, kk, kv, kc = jax.random.split(key, 5)
        sc = 1.0 / np.sqrt(E).astype(np.float32)
        return {'x': jax.random.normal(kx, (B, S, E), dtype=jnp.float32), 'Wq': jax.random.normal(kq, (E, E), dtype=jnp.float32) * sc, 'bq': jnp.zeros((E,), dtype=jnp.float32), 'Wk': jax.random.normal(kk, (E, E), dtype=jnp.float32) * sc, 'bk': jnp.zeros((E,), dtype=jnp.float32), 'Wv': jax.random.normal(kv, (E, E), dtype=jnp.float32) * sc, 'bv': jnp.zeros((E,), dtype=jnp.float32), 'Wc': jax.random.normal(kc, (E, E), dtype=jnp.float32) * sc, 'bc': jnp.zeros((E,), dtype=jnp.float32)}
    _L3_attn_all = _L3_attn_setup()
    _L3_attn_in = {k: v for k, v in _L3_attn_all.items() if k in ('Wq', 'bq', 'Wk', 'bk', 'Wv', 'bv', 'Wc', 'bc')}
    del _L3_attn_all

    def _L3_xattn_setup():
        import jax, jax.numpy as jnp
        import numpy as np
        EPS = 1e-06
        IMAGE_DIMS = 512
        key = jax.random.key(seed)
        k1, k2, k3 = jax.random.split(key, 3)
        B, I, J, D = (16, 512, 512, 128)
        p = jax.random.normal(k1, (B, I, J), dtype=jnp.float32)
        k_v = jax.random.normal(k2, (B, J, D), dtype=jnp.float32)
        W_k = jax.random.normal(k3, (D, D), dtype=jnp.float32) * (1.0 / np.sqrt(D))
        b_k = jnp.zeros((D,), dtype=jnp.float32)
        ln_gamma = jnp.ones((J,), dtype=jnp.float32)
        ln_beta = jnp.zeros((J,), dtype=jnp.float32)
        return {'p': p, 'k_v': k_v, 'W_k': W_k, 'b_k': b_k, 'ln_gamma': ln_gamma, 'ln_beta': ln_beta}
    _L3_xattn_all = _L3_xattn_setup()
    _L3_xattn_in = {k: v for k, v in _L3_xattn_all.items() if k in ('W_k', 'b_k', 'ln_gamma', 'ln_beta')}
    del _L3_xattn_all

    def _L3_ffn_setup():
        import jax, jax.numpy as jnp
        import numpy as np
        D_MODEL = 512
        D_FF = 2048

        def absmean_quant(w):
            scale = jnp.mean(jnp.abs(w))
            mask = (jnp.abs(w) >= scale * 0.7).astype(w.dtype)
            return jnp.sign(w) * mask
        key = jax.random.key(seed)
        k_x, k_w1, k_w2 = jax.random.split(key, 3)
        x = jax.random.normal(k_x, (4, 1024, D_MODEL), dtype=jnp.float32)
        w1 = jax.random.normal(k_w1, (D_FF, D_MODEL), dtype=jnp.float32)
        b1 = jnp.zeros((D_FF,), dtype=jnp.float32)
        w2 = jax.random.normal(k_w2, (D_MODEL, D_FF), dtype=jnp.float32)
        b2 = jnp.zeros((D_MODEL,), dtype=jnp.float32)
        return {'x': x, 'w1': w1, 'b1': b1, 'w2': w2, 'b2': b2}
    _L3_ffn_all = _L3_ffn_setup()
    _L3_ffn_in = {k: v for k, v in _L3_ffn_all.items() if k in ('w1', 'b1', 'w2', 'b2')}
    del _L3_ffn_all
    return {'x': x, 'ctx_512': ctx_512, 'L0_attn_slope_rate': _L0_attn_in['slope_rate'], 'L0_attn_W_qkvu': _L0_attn_in['W_qkvu'], 'L0_attn_W_out': _L0_attn_in['W_out'], 'L0_ffn_gate_w': _L0_ffn_in['gate_w'], 'L0_ffn_up_w': _L0_ffn_in['up_w'], 'L0_ffn_down_w': _L0_ffn_in['down_w'], 'L0_ffn_expert_weight': _L0_ffn_in['expert_weight'], 'L0_ffn_ln_gamma': _L0_ffn_in['ln_gamma'], 'L0_ffn_ln_beta': _L0_ffn_in['ln_beta'], 'L1_attn_qkv_w': _L1_attn_in['qkv_w'], 'L1_attn_conv_w0': _L1_attn_in['conv_w0'], 'L1_attn_conv_b0': _L1_attn_in['conv_b0'], 'L1_attn_conv_w1': _L1_attn_in['conv_w1'], 'L1_attn_conv_b1': _L1_attn_in['conv_b1'], 'L1_attn_proj_w': _L1_attn_in['proj_w'], 'L1_attn_proj_b': _L1_attn_in['proj_b'], 'L1_attn_ln_w': _L1_attn_in['ln_w'], 'L1_attn_ln_b': _L1_attn_in['ln_b'], 'L1_xattn_Wq': _L1_xattn_in['Wq'], 'L1_xattn_Wk': _L1_xattn_in['Wk'], 'L1_xattn_gamma_raw': _L1_xattn_in['gamma_raw'], 'L1_ffn_w_gate': _L1_ffn_in['w_gate'], 'L1_ffn_w_up': _L1_ffn_in['w_up'], 'L1_ffn_w_down': _L1_ffn_in['w_down'], 'L2_attn_WQ_w': _L2_attn_in['WQ_w'], 'L2_attn_WQ_b': _L2_attn_in['WQ_b'], 'L2_attn_WK_w': _L2_attn_in['WK_w'], 'L2_attn_WK_b': _L2_attn_in['WK_b'], 'L2_attn_WV_w': _L2_attn_in['WV_w'], 'L2_attn_WV_b': _L2_attn_in['WV_b'], 'L2_attn_WO_w': _L2_attn_in['WO_w'], 'L2_attn_WO_b': _L2_attn_in['WO_b'], 'L2_xattn_Wq': _L2_xattn_in['Wq'], 'L2_xattn_Wkv_expand': _L2_xattn_in['Wkv_expand'], 'L2_xattn_Wout': _L2_xattn_in['Wout'], 'L2_ffn_gate_weight': _L2_ffn_in['gate_weight'], 'L2_ffn_w_gate': _L2_ffn_in['w_gate'], 'L2_ffn_w_up': _L2_ffn_in['w_up'], 'L2_ffn_w_down': _L2_ffn_in['w_down'], 'L3_attn_Wq': _L3_attn_in['Wq'], 'L3_attn_bq': _L3_attn_in['bq'], 'L3_attn_Wk': _L3_attn_in['Wk'], 'L3_attn_bk': _L3_attn_in['bk'], 'L3_attn_Wv': _L3_attn_in['Wv'], 'L3_attn_bv': _L3_attn_in['bv'], 'L3_attn_Wc': _L3_attn_in['Wc'], 'L3_attn_bc': _L3_attn_in['bc'], 'L3_xattn_W_k': _L3_xattn_in['W_k'], 'L3_xattn_b_k': _L3_xattn_in['b_k'], 'L3_xattn_ln_gamma': _L3_xattn_in['ln_gamma'], 'L3_xattn_ln_beta': _L3_xattn_in['ln_beta'], 'L3_ffn_w1': _L3_ffn_in['w1'], 'L3_ffn_b1': _L3_ffn_in['b1'], 'L3_ffn_w2': _L3_ffn_in['w2'], 'L3_ffn_b2': _L3_ffn_in['b2']}

def reference(x, ctx_512, L0_attn_slope_rate, L0_attn_W_qkvu, L0_attn_W_out, L0_ffn_gate_w, L0_ffn_up_w, L0_ffn_down_w, L0_ffn_expert_weight, L0_ffn_ln_gamma, L0_ffn_ln_beta, L1_attn_qkv_w, L1_attn_conv_w0, L1_attn_conv_b0, L1_attn_conv_w1, L1_attn_conv_b1, L1_attn_proj_w, L1_attn_proj_b, L1_attn_ln_w, L1_attn_ln_b, L1_xattn_Wq, L1_xattn_Wk, L1_xattn_gamma_raw, L1_ffn_w_gate, L1_ffn_w_up, L1_ffn_w_down, L2_attn_WQ_w, L2_attn_WQ_b, L2_attn_WK_w, L2_attn_WK_b, L2_attn_WV_w, L2_attn_WV_b, L2_attn_WO_w, L2_attn_WO_b, L2_xattn_Wq, L2_xattn_Wkv_expand, L2_xattn_Wout, L2_ffn_gate_weight, L2_ffn_w_gate, L2_ffn_w_up, L2_ffn_w_down, L3_attn_Wq, L3_attn_bq, L3_attn_Wk, L3_attn_bk, L3_attn_Wv, L3_attn_bv, L3_attn_Wc, L3_attn_bc, L3_xattn_W_k, L3_xattn_b_k, L3_xattn_ln_gamma, L3_xattn_ln_beta, L3_ffn_w1, L3_ffn_b1, L3_ffn_w2, L3_ffn_b2):
    import jax
    import jax.numpy as jnp

    def _L0_attn_ref(x, slope_rate, W_qkvu, W_out):
        import jax, jax.numpy as jnp
        import numpy as np
        BLOCK = 64
        EPS = 1e-06

        def _silu(x):
            return x * jax.nn.sigmoid(x)
        b, n, embed_dim = x.shape
        h = slope_rate.shape[0]
        hidden_dim = W_qkvu.shape[0] // 4
        d = hidden_dim // h
        NB = n // BLOCK
        qkvu = x @ W_qkvu.T
        q, k, v, u = jnp.split(qkvu, 4, axis=-1)

        def to_heads(t):
            return t.reshape(b, n, h, d).transpose(0, 2, 1, 3)
        q = _silu(to_heads(q))
        k = _silu(to_heads(k))
        v = to_heads(v)
        s = slope_rate
        arr = jnp.arange(1, BLOCK + 1, dtype=x.dtype)
        q_decay = jnp.exp(-s * arr[:, None])
        k_decay = jnp.exp(-s * (BLOCK - arr[:, None]))
        idx = arr[:, None] - arr[None, :]
        diag_decay = jnp.exp(jnp.where(idx >= 0, -s * idx, -jnp.inf))
        block_decay = jnp.exp(-s * BLOCK)

        def blk(t):
            return t.reshape(b, h, NB, BLOCK, d).transpose(2, 0, 1, 3, 4)
        qb, kb, vb = (blk(q), blk(k), blk(v))

        def step(kv, inp):
            qi, ki, vi = inp
            qkv_none_diag = jnp.einsum('bhmd,bhde->bhme', qi * q_decay, kv)
            qk = jnp.einsum('bhmd,bhsd->bhms', qi, ki) * diag_decay
            qkv_diag = jnp.einsum('bhms,bhse->bhme', qk, vi)
            kv_new = block_decay * kv + jnp.einsum('bhsd,bhse->bhde', ki * k_decay, vi)
            return (kv_new, qkv_none_diag + qkv_diag)
        kv0 = jnp.zeros((b, h, d, d), dtype=jnp.float32)
        _, outs = jax.lax.scan(step, kv0, (qb, kb, vb))
        o = outs.transpose(1, 2, 0, 3, 4).reshape(b, h, n, d)
        o = o.transpose(0, 2, 1, 3).reshape(b, n, hidden_dim)
        o = o * jax.lax.rsqrt(jnp.mean(o * o, axis=-1, keepdims=True) + EPS)
        o = u * o
        return o @ W_out.T

    def _L0_xattn_ref(q, k, v):
        import jax, jax.numpy as jnp
        import numpy as np
        import math
        NUM_Q_HEADS = 32
        NUM_KV_HEADS = 8
        B, S, E = q.shape
        H, KV = (NUM_Q_HEADS, NUM_KV_HEADS)
        D = E // H
        G = H // KV
        scale = math.sqrt(D)
        qh = q.reshape(B, S, KV, G, D).transpose(0, 2, 3, 1, 4)
        kh = k.reshape(B, S, KV, D).transpose(0, 2, 1, 3)
        vh = v.reshape(B, S, KV, D).transpose(0, 2, 1, 3)
        scores = jnp.einsum('bkgsd,bktd->bkgst', qh, kh) / scale
        weights = jax.nn.softmax(scores, axis=-1)
        out = jnp.einsum('bkgst,bktd->bkgsd', weights, vh)
        return out.transpose(0, 3, 1, 2, 4).reshape(B, S, E)

    def _L0_ffn_ref(hidden_states, gate_w, up_w, down_w, expert_weight, ln_gamma, ln_beta):
        import jax, jax.numpy as jnp
        import numpy as np
        HID = 512
        INTER = 2048
        NEXP = 8
        TOPK = 2
        EPS = 1e-05

        def _mock_fused_moe(x, selected_experts, routing_weights, expert_weight):
            y = jnp.einsum('bsh,hd->bsd', x, expert_weight)
            scale = routing_weights.sum(axis=-1, keepdims=True)
            return y * scale
        residuals = hidden_states
        logits = jnp.einsum('bsh,he->bse', hidden_states, gate_w)
        routing_weights, selected_experts = jax.lax.top_k(logits, TOPK)
        h = jnp.einsum('bsh,hi->bsi', residuals, up_w)
        h = jnp.square(jax.nn.relu(h))
        shared_out = jnp.einsum('bsi,ih->bsh', h, down_w)
        moe_out = _mock_fused_moe(hidden_states, selected_experts, routing_weights, expert_weight)
        y = shared_out + moe_out
        mu = y.mean(axis=-1, keepdims=True)
        var = jnp.mean(jnp.square(y - mu), axis=-1, keepdims=True)
        return (y - mu) * jax.lax.rsqrt(var + EPS) * ln_gamma + ln_beta

    def _L1_attn_ref(x, qkv_w, conv_w0, conv_b0, conv_w1, conv_b1, proj_w, proj_b, ln_w, ln_b):
        import jax, jax.numpy as jnp
        import numpy as np
        from jax import lax
        SPLIT = 8
        DIM = 16
        EPS = 1e-05

        def _branch(q, k, v, cw, cb, H_sp, W_sp, Hg, Wg):
            B, N, C = q.shape
            hd = C
            scale = hd ** (-0.5)
            wsz = H_sp * W_sp
            nh, nw = (Hg // H_sp, Wg // W_sp)

            def part(t):
                t = t.reshape(B, nh, H_sp, nw, W_sp, C).transpose(0, 1, 3, 2, 4, 5)
                return t.reshape(-1, wsz, 1, hd).transpose(0, 2, 1, 3)
            vimg = v.reshape(B, nh, H_sp, nw, W_sp, C).transpose(0, 1, 3, 5, 2, 4)
            vimg = vimg.reshape(-1, C, H_sp, W_sp)
            lepe = lax.conv_general_dilated(vimg, cw, (1, 1), [(1, 1), (1, 1)], dimension_numbers=('NCHW', 'OIHW', 'NCHW'), feature_group_count=C)
            lepe = lepe + cb[None, :, None, None]
            lepe = lepe.reshape(-1, 1, hd, wsz).transpose(0, 1, 3, 2)
            vw = vimg.reshape(-1, 1, hd, wsz).transpose(0, 1, 3, 2)
            attn = jax.nn.softmax(part(q) * scale @ jnp.swapaxes(part(k), -1, -2), axis=-1)
            out = attn @ vw + lepe
            out = out.transpose(0, 2, 1, 3).reshape(B, nh, nw, H_sp, W_sp, C)
            out = out.transpose(0, 1, 3, 2, 4, 5).reshape(B, N, C)
            return out
        B, H, W = x.shape
        Hg, Wg = (H // 4, W // 4)
        C = DIM
        tok = x.reshape(B, H * W // C, C)
        qkv = (tok @ qkv_w).reshape(B, -1, 3, C)
        q, k, v = (qkv[:, :, 0], qkv[:, :, 1], qkv[:, :, 2])
        h = C // 2
        x1 = _branch(q[..., :h], k[..., :h], v[..., :h], conv_w0, conv_b0, 1, SPLIT, Hg, Wg)
        x2 = _branch(q[..., h:], k[..., h:], v[..., h:], conv_w1, conv_b1, SPLIT, 1, Hg, Wg)
        att = jnp.concatenate([x1, x2], axis=-1) @ proj_w + proj_b
        mu = att.mean(-1, keepdims=True)
        var = ((att - mu) ** 2).mean(-1, keepdims=True)
        normed = (att - mu) * lax.rsqrt(var + EPS) * ln_w + ln_b
        tok = tok + normed
        return jnp.transpose(tok, (0, 2, 1)).reshape(B, H, W)

    def _L1_xattn_ref(h, adj_raw, Wq, Wk, gamma_raw):
        import jax, jax.numpy as jnp
        import numpy as np
        B, N, D = (16, 512, 128)
        H = 4
        TOP_K_RATIO = 0.3
        b, n, dm = h.shape
        d = dm // H
        Q = (h @ Wq.T).reshape(b, n, H, d).transpose(0, 2, 1, 3)
        K = (h @ Wk.T).reshape(b, n, H, d).transpose(0, 2, 1, 3)
        sim = jnp.einsum('bhnd,bhmd->bnm', Q, K) / (jnp.sqrt(jnp.float32(d)) * H)
        k = max(1, int(n * TOP_K_RATIO))
        topk_vals = jax.lax.top_k(sim, k)[0]
        threshold = topk_vals[:, :, -1:]
        sparse_mask = (sim >= threshold).astype(sim.dtype)
        A_learned = jax.nn.sigmoid(sim) * sparse_mask
        A_learned = (A_learned + jnp.swapaxes(A_learned, -1, -2)) * 0.5
        gamma = jax.nn.sigmoid(gamma_raw)
        return (1.0 - gamma) * adj_raw + gamma * A_learned

    def _L1_ffn_ref(x, w_gate, w_up, w_down):
        import jax, jax.numpy as jnp
        import numpy as np
        ACT_BITS = 8
        EPS = 1e-05

        def act_quant(x, bits=ACT_BITS):
            qb = float(2 ** (bits - 1))
            scale = qb / jnp.clip(jnp.max(jnp.abs(x), axis=-1, keepdims=True), EPS)
            xq = jnp.clip(jnp.round(x * scale), -qb, qb - 1) / scale
            return x + jax.lax.stop_gradient(xq - x)

        def weight_quant(w):
            scale = 1.0 / jnp.clip(jnp.mean(jnp.abs(w)), EPS)
            wq = jnp.clip(jnp.round(w * scale), -1.0, 1.0) / scale
            return w + jax.lax.stop_gradient(wq - w)

        def fwht(x):
            shape = x.shape
            n = shape[-1]
            x = x.reshape(-1, n)
            h = 1
            while h < n:
                x = x.reshape(-1, n // (2 * h), 2, h)
                a, b = (x[..., 0, :], x[..., 1, :])
                x = jnp.stack([a + b, a - b], axis=-2).reshape(-1, n)
                h *= 2
            return (x * (1.0 / np.sqrt(n)).astype(np.float32)).reshape(shape)

        def bitlinear(x, w):
            return jnp.einsum('bsh,oh->bso', act_quant(x), weight_quant(w))

        def h_bitlinear(x, w):
            return jnp.einsum('bsh,oh->bso', act_quant(fwht(x)), weight_quant(w))
        gate = bitlinear(x, w_gate)
        up = bitlinear(x, w_up)
        intermediate = jax.nn.silu(gate) * up
        return h_bitlinear(intermediate, w_down)

    def _L2_attn_ref(x, WQ_w, WQ_b, WK_w, WK_b, WV_w, WV_b, WO_w, WO_b):
        import math
        import jax, jax.numpy as jnp
        import numpy as np
        B, S, H = (2, 512, 512)
        NH = 16
        HD = H // NH
        b, s, h = x.shape
        q = (x @ WQ_w.T + WQ_b).reshape(b, s, NH, HD).transpose(0, 2, 1, 3)
        k = (x @ WK_w.T + WK_b).reshape(b, s, NH, HD).transpose(0, 2, 1, 3)
        v = (x @ WV_w.T + WV_b).reshape(b, s, NH, HD).transpose(0, 2, 1, 3)
        scores = jnp.einsum('bhqd,bhkd->bhqk', q, k) * (1.0 / math.sqrt(HD))
        causal = jnp.triu(jnp.ones((s, s), dtype=bool), k=1)
        scores = jnp.where(causal, -jnp.inf, scores)
        attn = jax.nn.softmax(scores, axis=-1)
        out = jnp.einsum('bhqk,bhkd->bhqd', attn, v)
        out = out.transpose(0, 2, 1, 3).reshape(b, s, h)
        return out @ WO_w.T + WO_b

    def _L2_xattn_ref(q, latent_kv, Wq, Wkv_expand, Wout):
        import jax, jax.numpy as jnp
        import numpy as np
        B, S, H, NH, L = (2, 512, 512, 16, 128)
        HD = H // NH
        b, sq, _ = q.shape
        sk = latent_kv.shape[1]
        qp = q @ Wq.T
        kv = latent_kv @ Wkv_expand.T
        k, v = jnp.split(kv, 2, axis=-1)
        qh = qp.reshape(b, sq, NH, HD).transpose(0, 2, 1, 3)
        kh = k.reshape(b, sk, NH, HD).transpose(0, 2, 1, 3)
        vh = v.reshape(b, sk, NH, HD).transpose(0, 2, 1, 3)
        inv_sqrt_d = 1.0 / jnp.sqrt(jnp.float32(HD))
        scores = jnp.einsum('bhqd,bhkd->bhqk', qh, kh) * inv_sqrt_d
        causal = jnp.tril(jnp.ones((sq, sk), dtype=bool))
        scores = jnp.where(causal, scores, jnp.finfo(scores.dtype).min)
        attn = jax.nn.softmax(scores, axis=-1)
        out = jnp.einsum('bhqk,bhkd->bhqd', attn, vh)
        out = out.transpose(0, 2, 1, 3).reshape(b, sq, H)
        return out @ Wout.T

    def _L2_ffn_ref(hidden_states, gate_weight, w_gate, w_up, w_down):
        import jax, jax.numpy as jnp
        import numpy as np
        B, S, H = (2, 512, 512)
        E, K, I = (64, 8, 192)

        def _moe_forward(hidden_states, gate_weight, w_gate, w_up, w_down):
            b, s, h = hidden_states.shape
            x = hidden_states.reshape(-1, h)
            logits = x.astype(jnp.float32) @ gate_weight.astype(jnp.float32).T
            scores = jax.nn.softmax(logits, axis=-1)
            topk_w, topk_idx = jax.lax.top_k(scores, K)
            topk_w = topk_w / jnp.sum(topk_w, axis=-1, keepdims=True)
            flat_ids = topk_idx.reshape(-1)
            expanded = jnp.repeat(x, K, axis=0)
            order = jnp.argsort(flat_ids)
            sorted_tokens = expanded[order]
            group_sizes = jnp.zeros((E,), jnp.int32).at[flat_ids].add(1)
            g = jax.lax.ragged_dot(sorted_tokens, w_gate, group_sizes)
            u = jax.lax.ragged_dot(sorted_tokens, w_up, group_sizes)
            out = jax.lax.ragged_dot(jax.nn.silu(g) * u, w_down, group_sizes)
            inv = jnp.argsort(order)
            outs = out[inv].reshape(-1, K, h)
            y = jnp.sum(outs * topk_w[:, :, None], axis=1)
            return y.reshape(b, s, h)
        return _moe_forward(hidden_states, gate_weight, w_gate, w_up, w_down)

    def _L3_attn_ref(x, Wq, bq, Wk, bk, Wv, bv, Wc, bc):
        import jax, jax.numpy as jnp
        import numpy as np
        NUM_HEADS = 16
        B, S, E = x.shape
        H = NUM_HEADS
        d = E // H
        q = (x @ Wq + bq).reshape(B, S, H, d)
        k = (x @ Wk + bk).reshape(B, S, H, d)
        v = (x @ Wv + bv).reshape(B, S, H, d)
        att = jnp.einsum('bihd,bjhd->bhij', q, k) * (1.0 / np.sqrt(d).astype(np.float32))
        causal = jnp.tril(jnp.ones((S, S), dtype=bool))
        att = jnp.where(causal[None, None, :, :], att, -jnp.inf)
        att = jax.nn.softmax(att, axis=-1)
        y = jnp.einsum('bhij,bihd->bihd', att, v).reshape(B, S, E)
        return y @ Wc + bc

    def _L3_xattn_ref(p, k_v, W_k, b_k, ln_gamma, ln_beta):
        import jax, jax.numpy as jnp
        import numpy as np
        EPS = 1e-06
        IMAGE_DIMS = 512
        kv = k_v @ W_k.T + b_k
        out = jnp.einsum('bij,bjd->bid', p, kv)
        scale = IMAGE_DIMS ** (-0.5)
        sim = jnp.einsum('bid,bjd->bij', out, kv) * scale
        mu = jnp.mean(sim, axis=-1, keepdims=True)
        var = jnp.var(sim, axis=-1, keepdims=True)
        sim = (sim - mu) * jax.lax.rsqrt(var + EPS) * ln_gamma + ln_beta
        attn = jax.nn.softmax(sim, axis=-1)
        return attn

    def _L3_ffn_ref(x, w1, b1, w2, b2):
        import jax, jax.numpy as jnp
        import numpy as np
        D_MODEL = 512
        D_FF = 2048

        def absmean_quant(w):
            scale = jnp.mean(jnp.abs(w))
            mask = (jnp.abs(w) >= scale * 0.7).astype(w.dtype)
            return jnp.sign(w) * mask
        w1_q = absmean_quant(w1)
        w2_q = absmean_quant(w2)
        h = jnp.einsum('bsd,fd->bsf', x, w1_q) + b1
        h = jax.nn.gelu(h, approximate=False)
        out = jnp.einsum('bsf,df->bsd', h, w2_q) + b2
        return out
    x = _layernorm(x + _L0_attn_ref(x, L0_attn_slope_rate, L0_attn_W_qkvu, L0_attn_W_out), axis=-1)
    x = _layernorm(x + _L0_xattn_ref(x, ctx_512, ctx_512), axis=-1)
    x = _layernorm(x + _L0_ffn_ref(x, L0_ffn_gate_w, L0_ffn_up_w, L0_ffn_down_w, L0_ffn_expert_weight, L0_ffn_ln_gamma, L0_ffn_ln_beta), axis=-1)
    x = _layernorm(x + _L1_attn_ref(x, L1_attn_qkv_w, L1_attn_conv_w0, L1_attn_conv_b0, L1_attn_conv_w1, L1_attn_conv_b1, L1_attn_proj_w, L1_attn_proj_b, L1_attn_ln_w, L1_attn_ln_b), axis=-1)
    x = _layernorm(x + _L1_xattn_ref(ctx_512, x, L1_xattn_Wq, L1_xattn_Wk, L1_xattn_gamma_raw), axis=-1)
    x = _layernorm(x + _L1_ffn_ref(x, L1_ffn_w_gate, L1_ffn_w_up, L1_ffn_w_down), axis=-1)
    x = _layernorm(x + _L2_attn_ref(x, L2_attn_WQ_w, L2_attn_WQ_b, L2_attn_WK_w, L2_attn_WK_b, L2_attn_WV_w, L2_attn_WV_b, L2_attn_WO_w, L2_attn_WO_b), axis=-1)
    x = _layernorm(x + _L2_xattn_ref(x, ctx_512, L2_xattn_Wq, L2_xattn_Wkv_expand, L2_xattn_Wout), axis=-1)
    x = _layernorm(x + _L2_ffn_ref(x, L2_ffn_gate_weight, L2_ffn_w_gate, L2_ffn_w_up, L2_ffn_w_down), axis=-1)
    x = _layernorm(x + _L3_attn_ref(x, L3_attn_Wq, L3_attn_bq, L3_attn_Wk, L3_attn_bk, L3_attn_Wv, L3_attn_bv, L3_attn_Wc, L3_attn_bc), axis=-1)
    x = _layernorm(x + _L3_xattn_ref(x, ctx_512, L3_xattn_W_k, L3_xattn_b_k, L3_xattn_ln_gamma, L3_xattn_ln_beta), axis=-1)
    x = _layernorm(x + _L3_ffn_ref(x, L3_ffn_w1, L3_ffn_b1, L3_ffn_w2, L3_ffn_b2), axis=-1)
    return x

_drawn_inputs = setup_inputs


def setup_inputs(seed=0):
    import zlib

    import numpy as np

    out = dict(_drawn_inputs(seed))
    spreads = {'L0_ffn_ln_gamma': (1.0, 0.2),
     'L0_ffn_ln_beta': (0.0, 0.1),
     'L1_attn_ln_w': (1.0, 0.2),
     'L1_attn_ln_b': (0.0, 0.8),
     'L3_attn_bq': (0.0, 0.8),
     'L3_attn_bk': (0.0, 0.8),
     'L3_attn_bv': (0.0, 0.1),
     'L3_attn_bc': (0.0, 0.1),
     'L3_xattn_b_k': (0.0, 0.8),
     'L3_xattn_ln_gamma': (1.0, 0.6),
     'L3_xattn_ln_beta': (0.0, 0.8),
     'L3_ffn_b1': (0.0, 0.8),
     'L3_ffn_b2': (0.0, 0.8)}
    factors = {'L0_ffn_up_w': 2.964,
     'L0_ffn_down_w': 2.806,
     'L1_attn_conv_b0': 6.932,
     'L1_attn_conv_b1': 8.0,
     'L1_attn_proj_b': 8.0,
     'L2_attn_WQ_b': 8.0,
     'L2_attn_WK_b': 8.0,
     'L2_attn_WV_b': 5.965,
     'L2_attn_WO_b': 6.457,
     'L2_xattn_Wq': 8.0,
     'L2_ffn_gate_weight': 5.656,
     'L2_ffn_w_gate': 5.385,
     'L2_ffn_w_up': 5.289,
     'L2_ffn_w_down': 5.292,
     'L3_attn_Wq': 8.0,
     'L3_attn_Wk': 8.0,
     'L3_xattn_W_k': 8.0}
    for name, (base, spread) in spreads.items():
        noise = np.random.default_rng([zlib.crc32(name.encode()), seed]).standard_normal(out[name].shape)
        drawn = base * np.exp(spread * noise) if base else spread * noise
        out[name] = jnp.asarray(drawn.astype(out[name].dtype))
    for name, factor in factors.items():
        out[name] = (out[name] * factor).astype(out[name].dtype)
    return out
```

```python
import numpy as np
import concourse.bass as bass
from concourse import mybir

F32 = mybir.dt.float32
BF16 = mybir.dt.bfloat16
U32 = mybir.dt.uint32
ALU = mybir.AluOpType
ACT = mybir.ActivationFunctionType
AX = mybir.AxisListType
P = 128
NT = 16
D = 512
NEG = -1.0e30


class Eng:

    def __init__(self, nc, name, eng):
        self.nc, self.name, self.eng = nc, name, eng
        self.seen = {}
        self.last = None

    def phase(self, label):
        self.sem = self.nc.alloc_semaphore(f"{self.name}_{label}")
        self.count = 0

    def wait(self, *toks):
        for t in toks:
            if t is None:
                continue
            if isinstance(t, list):
                self.wait(*t)
                continue
            sem, val = t
            if self.seen.get(sem.name, 0) >= val:
                continue
            self.seen[sem.name] = val
            self.eng.wait_ge(sem, val)

    def sig(self, ins):
        ins.then_inc(self.sem, 1)
        self.count += 1
        self.last = (self.sem, self.count)
        return self.last


class Slot:
    def __init__(self, ring, i, ap, free):
        self.ring, self.i, self.ap, self.free = ring, i, ap, free

    def done(self, *toks):
        self.ring.free[self.i] = list(toks)
        self.ring.held[self.i] = False


class Ring:

    def __init__(self, bufs, free=None):
        self.bufs, self.n = bufs, 0
        self.free = [list(free or []) for _ in bufs]
        self.held = [False for _ in bufs]

    def take(self):
        i = self.n % len(self.bufs)
        self.n += 1
        assert not self.held[i], "a buffer is taken before its last user is named"
        self.held[i] = True
        return Slot(self, i, self.bufs[i], self.free[i])


class K:
    def __init__(self, nc, ins, out):
        self.nc, self.ins, self.out = nc, ins, out
        self.pe = Eng(nc, "pe", nc.tensor)
        self.act = Eng(nc, "act", nc.scalar)
        self.dve = Eng(nc, "dve", nc.vector)
        self.pool = Eng(nc, "pool", nc.gpsimd)
        self.sp = Eng(nc, "sp", nc.sync)
        self.NDS = 24
        self.dsem = [nc.alloc_semaphore(f"dma{i}") for i in range(self.NDS)]
        self.dcount = [0] * self.NDS
        self.dn = 0
        self.W = 51800
        self.arena = nc.alloc_sbuf_tensor("arena", [P, self.W], F32)
        self.ps = nc.alloc_psum_tensor("ps", [P, 8, 512], F32)
        self.off = 0
        self.fence_toks = []

    def alloc(self, shape, dt=F32):
        n = int(np.prod(shape))
        words = n if dt != BF16 else (n + 1) // 2
        o = self.off
        self.off += words
        assert self.off <= self.W, f"sbuf {self.off}"
        return self.view(o, shape, dt)

    def view(self, o, shape, dt=F32):
        n = int(np.prod(shape))
        words = n if dt != BF16 else n // 2
        a = self.arena[:, o:o + words]
        if dt != F32:
            a = a.bitcast(dt)
        if len(shape) > 1:
            names = "abcde"[:len(shape)]
            kw = {names[i]: shape[i] for i in range(1, len(shape))}
            a = a.rearrange(f"p ({' '.join(names)}) -> p {' '.join(names)}", **kw)
        return a

    def bank(self, i, n=1):
        return self.ps[:, i:i + n, :]

    def phase(self, label):
        toks = [e.last for e in (self.pe, self.act, self.dve, self.pool) if e.last]
        for i in range(self.NDS):
            if self.dcount[i]:
                toks.append((self.dsem[i], 16 * self.dcount[i]))
        for e in (self.pe, self.act, self.dve, self.pool, self.sp):
            e.wait(*toks)
        for e in (self.pe, self.act, self.dve, self.pool):
            e.phase(label)

    def dma(self, out, in_, *w, eng=None):
        eng = eng or self.sp
        i = self.dn % self.NDS
        self.dn += 1
        if self.dcount[i]:
            eng.wait((self.dsem[i], 16 * self.dcount[i]))
        eng.wait(*w)
        eng.eng.dma_start(out, in_).then_inc(self.dsem[i], 16)
        self.dcount[i] += 1
        return (self.dsem[i], 16 * self.dcount[i])

    def mm(self, out, lhsT, rhs, start, stop, *w, sig=False, skip=True):
        self.pe.wait(*w)
        i = self.nc.tensor.matmul(out, lhsT, rhs, start=start, stop=stop, skip_group_check=skip)
        return self.pe.sig(i) if sig else None

    def tr(self, out, in_, *w, sig=False):
        self.pe.wait(*w)
        ident = self.idb if in_.dtype == BF16 else self.idf
        n = in_.shape[0]
        i = self.nc.tensor.transpose(out, in_, ident[0:n, 0:n])
        return self.pe.sig(i) if sig else None

    def activ(self, out, in_, func, *w, bias=None, scale=1.0, accum=None):
        self.act.wait(*w)
        kw = {}
        if bias is not None:
            kw["bias"] = bias
        if accum is not None:
            kw["accum_out"] = accum
        return self.act.sig(self.nc.scalar.activation(out, in_, func, scale=scale, **kw))

    def acopy(self, out, in_, *w):
        return self.activ(out, in_, ACT.Copy, *w)

    def v_copy(self, out, in_, *w):
        self.dve.wait(*w)
        return self.dve.sig(self.nc.vector.tensor_copy(out, in_))

    def v_tt(self, out, a, b, op, *w):
        self.dve.wait(*w)
        return self.dve.sig(self.nc.vector.tensor_tensor(out, a, b, op))

    def v_ts(self, out, a, s1, s2, op0, op1, *w, accum=None):
        self.dve.wait(*w)
        kw = {"accum_out": accum} if accum is not None else {}
        if op1 is None:
            return self.dve.sig(self.nc.vector.tensor_scalar(out, a, s1, None, op0))
        return self.dve.sig(self.nc.vector.tensor_scalar(out, a, s1, s2, op0, op1, **kw))

    def v_stt(self, out, a, s, b, op0, op1, *w):
        self.dve.wait(*w)
        return self.dve.sig(self.nc.vector.scalar_tensor_tensor(out=out, in0=a, scalar=s, in1=b, op0=op0, op1=op1))

    def v_red(self, out, a, op, *w, negate=False, absolute=False):
        self.dve.wait(*w)
        return self.dve.sig(self.nc.vector.tensor_reduce(out, a, AX.X, op, negate=negate,
                                                         apply_absolute_value=absolute))

    def v_recip(self, out, a, *w):
        self.dve.wait(*w)
        return self.dve.sig(self.nc.vector.reciprocal(out, a))

    def g_tt(self, out, a, b, op, *w):
        self.pool.wait(*w)
        return self.pool.sig(self.nc.gpsimd.tensor_tensor(out, a, b, op))

    def g_ts(self, out, a, s1, s2, op0, op1, *w):
        self.pool.wait(*w)
        if op1 is None:
            return self.pool.sig(self.nc.gpsimd.tensor_scalar(out, a, s1, None, op0))
        return self.pool.sig(self.nc.gpsimd.tensor_scalar(out, a, s1, s2, op0, op1))

    def g_copy(self, out, a, *w):
        self.pool.wait(*w)
        return self.pool.sig(self.nc.gpsimd.tensor_copy(out, a))

    def start(self):
        nc = self.nc
        self.X = self.alloc([NT, D])
        self.idf = self.alloc([P])
        self.idb = self.alloc([P], BF16)
        self.mq = self.alloc([P], BF16)
        self.mk = self.alloc([P], BF16)
        self.nhalf = self.alloc([32])
        self.st = self.alloc([4, 8])
        self.mv = self.alloc([4, 4])
        self.zb = Ring([self.alloc([D]) for _ in range(4)])
        self.base = self.off
        for e in (self.pe, self.act, self.dve, self.pool, self.sp):
            e.phase("start")
        c = self.ins["c_masks"]
        tc = [self.dma(self.idf, self.ins["c_ident"])]
        tmp = self.view(self.base, [3, P])
        t = self.dma(tmp, c)
        tc.append(self.v_copy(self.idb, tmp[:, 0, :], t))
        tc.append(self.v_copy(self.mq, tmp[:, 1, :], t))
        tc.append(self.v_copy(self.mk, tmp[:, 2, :], t))
        self.pool.wait()
        tc.append(self.pool.sig(nc.gpsimd.memset(self.nhalf, -0.5)))
        tx = self.dma(self.X, self.ins["x"].rearrange("b (t p) d -> p (b t) d", p=P))
        self.xtok = [tx] * NT
        self.ln_n = 0
        self.ln_pending = []

    def ln_begin(self, i, add, *w):
        s = self.zb.take()
        n = self.ln_n % 4
        self.ln_n += 1
        tz = add(s.ap, *w, s.free)
        self.dve.wait(tz)
        tb = self.dve.sig(self.nc.vector.bn_stats(self.st[:, n, 0:6], s.ap))
        self.dve.wait(tb)
        ta = self.dve.sig(self.nc.vector.bn_aggr(self.mv[:, n, 0:2], self.st[:, n, 0:6]))
        t1 = self.g_ts(self.mv[:, n, 2:3], self.mv[:, n, 1:2], 1e-5, 1.0, ALU.add, ALU.mult, ta)
        t2 = self.g_tt(self.mv[:, n, 3:4], self.mv[:, n, 2:3], self.nhalf[:, 0:1], ALU.pow, t1)
        self.ln_pending.append((i, s, n, t2))

    def ln_end(self):
        i, s, n, t2 = self.ln_pending.pop(0)
        t = self.v_ts(self.X[:, i, :], s.ap, self.mv[:, n, 0:1], self.mv[:, n, 3:4],
                      ALU.subtract, ALU.mult, t2)
        s.done(t)
        self.xtok[i] = t
        return t

    def ln(self, i, add, *w, lag=1):
        self.ln_begin(i, add, *w)
        while len(self.ln_pending) > lag:
            self.ln_end()

    def ln_flush(self):
        while self.ln_pending:
            self.ln_end()

    def add_from(self, i, src, slot, *w):
        def add(z, *ww):
            t = self.v_tt(z, self.X[:, i, :], src, ALU.add, *ww, self.xtok[i])
            if slot is not None:
                slot.done(t)
            return t
        return add

    def x_to_xt(self, i, ring, dst, *w, eng=0):
        s = ring.take()
        b = s.ap.rearrange("p (k n) -> p k n", k=4)
        for k in range(4):
            t = self.tr(b[:, k, :], self.X[:, i, k * P:(k + 1) * P], s.free, self.xtok[i], sig=(k == 3))
        t = self.acopy(dst, b, t, *w) if eng == 0 else self.v_copy(dst, b, t, *w)
        s.done(t)
        return t


def pipeline(n, stages):
    top = max(lag for lag, _ in stages)
    for t in range(n + top):
        for lag, f in sorted(stages, key=lambda s: -s[0]):
            if 0 <= t - lag < n:
                f(t - lag)
def l0_attn(k):
    nc = k.nc
    k.phase("l0attn")
    k.off = k.base
    WQ = k.alloc([4, 2048])
    WO = k.alloc([4, 512])
    tw = [k.dma(WQ[:, :, 512 * j:512 * j + 512],
                k.ins["L0_attn_W_qkvu"].rearrange("(k p) n -> p k n", p=P)[:, :, 512 * j:512 * j + 512])
          for j in range(4)]
    two = k.dma(WO, k.ins["L0_attn_W_out"].rearrange("(k p) n -> p k n", p=P))
    SQ = k.alloc([4])
    SK = k.alloc([16])
    IO = k.alloc([3, P])
    DT = k.alloc([16, P])
    QD = k.alloc([4, P])
    KD = k.alloc([512])
    KD16 = k.alloc([16])
    EB = k.alloc([4, P])
    BM = k.alloc([P])
    eb1 = k.alloc([4])
    ts = [k.dma(SQ, k.ins["slope_q"]), k.dma(SK, k.ins["slope_k"]), k.dma(IO, k.ins["c_iota"]),
          k.dma(BM, k.ins["c_block"])]
    for h in range(16):
        td = k.v_ts(DT[:, h, :], IO[:, 1, :], SK[:, h:h + 1], -1.0, ALU.mult, ALU.mult, ts)
    for hg in range(4):
        td = k.v_ts(QD[:, hg, :], IO[:, 0, :], SQ[:, hg:hg + 1], -1.0, ALU.mult, ALU.mult)
    td = k.v_ts(KD16, SK, IO[:, 2, 0:1], -1.0, ALU.mult, ALU.mult)
    td = k.v_ts(eb1, SQ, -128.0, None, ALU.mult, None)
    t1 = k.activ(DT, DT, ACT.Exp, td)
    t2 = k.activ(QD, QD, ACT.Exp)
    t3 = k.activ(KD16, KD16, ACT.Exp)
    t4 = k.activ(eb1, eb1, ACT.Exp)
    t5 = k.v_copy(KD.rearrange("p (h d) -> p h d", d=32), KD16.unsqueeze(2).to_broadcast([P, 16, 32]), t3, td)
    for hg in range(4):
        t6 = k.v_ts(EB[:, hg, :], BM, eb1[:, hg:hg + 1], None, ALU.mult, None, t4, td)
    dec = [t1, t2, t5, t6]

    R = Ring([k.bank(j)[:, 0, :] for j in range(3)])
    S4 = Ring([k.bank(3 + j)[:, 0, :] for j in range(4)])
    OB = Ring([k.bank(7)[:, 0, :]])
    XT = Ring([k.alloc([4, P]) for _ in range(2)])
    Qr, Kr = (Ring([k.alloc([512]) for _ in range(1)]) for _ in range(2))
    Vr, Ur = (Ring([k.alloc([512]) for _ in range(3)]) for _ in range(2))
    QTr, KTr = (Ring([k.alloc([4, P]) for _ in range(2)]) for _ in range(2))
    QSr, KSr = (Ring([k.alloc([4, P]) for _ in range(3)]) for _ in range(2))
    PTr = Ring([k.alloc([16, P])])
    OTr = Ring([k.alloc([4, P]) for _ in range(2)])
    ONr = Ring([k.alloc([512]) for _ in range(2)])
    KV = k.alloc([4, P])
    KVt = k.alloc([4, P])
    rs = k.alloc([NT, 4])
    st = [dict() for _ in range(NT)]
    state = {"kv": None, "rd": None}

    def a0(i):
        s = st[i]
        s["xt"] = XT.take()
        s["txt"] = k.x_to_xt(i, R, s["xt"].ap, s["xt"].free, eng=i % 2)

    def a(i):
        s = st[i]
        for j, (name, ring) in enumerate((("q", Qr), ("k", Kr), ("v", Vr), ("u", Ur))):
            b = R.take()
            o = s[name] = ring.take()
            for kk in range(4):
                t = k.mm(b.ap, s["xt"].ap[:, kk, :], WQ[:, kk, 512 * j:512 * j + 512], kk == 0, kk == 3,
                         b.free, s["txt"], tw[j], sig=(kk == 3))
            if j < 2:
                t = k.activ(o.ap, b.ap, ACT.Silu, t, o.free)
            elif j == 2:
                t = k.v_copy(o.ap, b.ap, t, o.free)
            else:
                t = k.acopy(o.ap, b.ap, t, o.free)
            b.done(t)
            s["t" + name] = t
        s["xt"].done(k.pe.last)

    def b(i):
        s = st[i]
        for name, src, tsrc, ring in (("qt", s["q"], s["tq"], QTr), ("kt", s["k"], s["tk"], KTr)):
            bk = R.take()
            bb = bk.ap.rearrange("p (k n) -> p k n", k=4)
            o = s[name] = ring.take()
            for kk in range(4):
                t = k.tr(bb[:, kk, :], src.ap[:, kk * P:kk * P + P], bk.free, tsrc, sig=(kk == 3))
            t = (k.v_copy if name == "qt" else k.acopy)(o.ap, bb, t, o.free)
            bk.done(t)
            s["t" + name] = t
            if name == "qt":
                s["q"].done(k.pe.last)
            else:
                tkt = k.pe.last
        o = s["ks"] = KSr.take()
        s["tks"] = k.g_tt(o.ap.rearrange("p a b -> p (a b)"), s["k"].ap, KD, ALU.mult, s["tk"], o.free, dec)
        s["k"].done(s["tks"], tkt)
        o = s["qs"] = QSr.take()
        s["tqs"] = k.g_tt(o.ap, s["qt"].ap, QD, ALU.mult, s["tqt"], o.free)

    def c(i):
        s = st[i]
        first = i % 4 == 0
        pt = s["pt"] = PTr.take()
        banks = [S4.take() for _ in range(4)]
        for g in range(4):
            bb = banks[g].ap.rearrange("p (k n) -> p k n", k=4)
            for hg in range(4):
                t = k.mm(bb[:, hg, :], s["kt"].ap[32 * g:32 * g + 32, hg, :], s["qt"].ap[32 * g:32 * g + 32, hg, :],
                         True, True, banks[g].free, s["tqt"], s["tkt"], sig=(hg == 3))
            dv = DT.rearrange("p (hg g) n -> p g hg n", g=4)[:, g]
            pv = pt.ap.rearrange("p (hg g) n -> p g hg n", g=4)[:, g]
            t = k.v_tt(pv, bb, dv, ALU.mult, t, pt.free, dec)
            banks[g].done(t)
        s["tpt"] = t
        s["qt"].done(k.pe.last, s["tqs"])
        s["kt"].done(k.pe.last)

    def kvup(i):
        s = st[i]
        if i % 4 == 3:
            s["ks"].done(s["tks"])
            return
        bk = R.take()
        bb = bk.ap.rearrange("p (k n) -> p k n", k=4)
        for hg in range(4):
            t = k.mm(bb[:, hg, :], s["ks"].ap[:, hg, :], s["v"].ap[:, hg * P:hg * P + P], True, True,
                     bk.free, s["tks"], s["tv"], sig=(hg == 3))
        s["ks"].done(t)
        bm = BM.unsqueeze(1).to_broadcast([P, 4, P])
        if i % 4 == 0:
            t = t0 = k.v_tt(KV, bb, bm, ALU.mult, t, state["rd"])
        else:
            t0 = k.v_tt(KVt, bb, bm, ALU.mult, t, state["kv"])
            t1 = k.v_tt(KV, KV, EB, ALU.mult, state["kv"], state["rd"], t0)
            t = k.v_tt(KV, KV, KVt, ALU.add, t1)
        bk.done(t0)
        state["kv"] = t

    def dd(i):
        s = st[i]
        ob = OB.take()
        if i % 4:
            for hg in range(4):
                k.mm(ob.ap[:, hg * P:hg * P + P], s["qs"].ap[:, hg, :], KV[:, hg, :], hg == 0, False,
                     ob.free, s["tqs"], state["kv"], sig=(hg == 3))
            state["rd"] = k.pe.last
        kvup(i)
        s["qs"].done(k.pe.last, s["tqs"])
        for h in range(16):
            t = k.mm(ob.ap[:, h * 32:h * 32 + 32], s["pt"].ap[:, h, :], s["v"].ap[:, h * 32:h * 32 + 32],
                     i % 4 == 0 and h == 0, h == 15, ob.free, s["tpt"], s["tv"], sig=(h == 15))
        s["pt"].done(t)
        s["v"].done(t)
        on = s["on"] = ONr.take()
        t1 = k.activ(on.ap, ob.ap, ACT.Square, t, on.free, accum=rs[:, i, 0:1])
        t2 = k.g_ts(rs[:, i, 1:2], rs[:, i, 0:1], 1.0 / 512, 1e-6, ALU.mult, ALU.add, t1)
        t3 = k.g_tt(rs[:, i, 2:3], rs[:, i, 1:2], k.nhalf[:, 0:1], ALU.pow, t2)
        t4 = k.v_stt(on.ap, ob.ap, rs[:, i, 2:3], s["u"].ap, ALU.mult, ALU.mult, t3, s["tu"], t1)
        s["u"].done(t4)
        ob.done(t4)
        s["ton"] = t4

    def e(i):
        s = st[i]
        bk = R.take()
        bb = bk.ap.rearrange("p (k n) -> p k n", k=4)
        for kk in range(4):
            t = k.tr(bb[:, kk, :], s["on"].ap[:, kk * P:kk * P + P], bk.free, s["ton"], sig=(kk == 3))
        s["on"].done(t)
        ot = OTr.take()
        t = k.acopy(ot.ap, bb, t, ot.free)
        bk.done(t)
        b2 = R.take()
        for kk in range(4):
            t2 = k.mm(b2.ap, ot.ap[:, kk, :], WO[:, kk, :], kk == 0, kk == 3, b2.free, t, two, sig=(kk == 3))
        ot.done(t2)
        k.ln(i, k.add_from(i, b2.ap, b2), t2)

    pipeline(NT, [(0, a0), (1, a), (2, b), (3, c), (4, dd), (5, e)])
    k.ln_flush()


def split3(k, parts, x, res, *w):
    t = k.v_copy(parts[0], x, *w)
    t = k.v_tt(res, x, parts[0], ALU.subtract, t, *w)
    t = k.v_copy(parts[1], res, t)
    t = k.v_tt(res, res, parts[1], ALU.subtract, t)
    return k.v_copy(parts[2], res, t)


def l0_xattn(k):
    nc = k.nc
    k.phase("l0xattn")
    k.off = k.base
    CX = k.alloc([NT, P])
    tcx = [k.dma(CX[:, 4 * b:4 * b + 4, :], k.ins["ctx_512"][b].rearrange("(t p) d -> p t d", p=P)) for b in range(4)]
    KS = Ring([k.alloc([8, 512], BF16) for _ in range(2)])
    VA = Ring([k.alloc([4, 8, 17]) for _ in range(2)])
    kst = [k.alloc([8, P], BF16) for _ in range(1)]
    kres = k.alloc([P])
    qst = Ring([k.alloc([32, 96], BF16) for _ in range(1)])
    qsc = k.alloc([512])
    qres = k.alloc([512])
    QS = Ring([k.alloc([32, P], BF16) for _ in range(2)])
    MX = k.alloc([2, 32])
    mres = k.alloc([32])
    ms = k.alloc([96], BF16)
    MT = Ring([k.alloc([P], BF16) for _ in range(2)])
    PT = Ring([k.alloc([4, P]) for _ in range(4)])
    rz = k.alloc([2, 32])
    oa = Ring([k.alloc([512]) for _ in range(2)])
    S1 = Ring([k.bank(0, 2), k.bank(2, 2)])
    S2 = Ring([k.bank(4)[:, 0, :], k.bank(5)[:, 0, :]])
    OB = Ring([k.bank(6)[:, 0, 0:272].rearrange("p (h e) -> p h e", e=17),
               k.bank(7)[:, 0, 0:272].rearrange("p (h e) -> p h e", e=17)])
    st = [dict() for _ in range(NT)]
    kb = [dict() for _ in range(4)]
    KORD = (0, 1, 0, 1, 2, 0)
    QORD = (0, 0, 1, 1, 0, 2)
    k.tkst = None

    for buf in VA.bufs:
        k.pool.wait()
        tva = k.pool.sig(nc.gpsimd.memset(buf[:, :, :, 16:17], 1.0))
    tks0 = k.pool.sig(nc.gpsimd.memset(kst[0][:, :, 96:128], 0.0))
    k.pool.wait(tks0)
    tks0 = k.pool.sig(nc.gpsimd.memset(kst[0][:, :, 96:99], 1.0))
    k.tkst = [tks0]

    def prep(b, t4):
        s = kb[b]
        if t4 == 0:
            s["ks"] = KS.take()
            s["va"] = VA.take()
            s["tk"] = [None] * 4
            s["tv"] = [None] * 4
        src = CX[:, 4 * b + t4, :].rearrange("p (h d) -> p h d", d=16)
        va = s["va"].ap
        s["tv"][t4] = k.g_copy(va[:, t4, :, 0:16], src, tcx, s["va"].free)
        s["tva"] = tva
        buf = kst[0]
        kv = buf[:, :, 0:96].rearrange("p h (r d) -> p h r d", d=16)
        part = [kv[:, :, 0, :], kv[:, :, 1, :], kv[:, :, 4, :]]
        rr = kres.rearrange("p (h d) -> p h d", d=16)
        t = split3(k, part, src, rr, tcx, k.tkst, tks0)
        ta = k.g_copy(kv[:, :, 2, :], kv[:, :, 0, :], t)
        tb = k.g_copy(kv[:, :, 3, :], kv[:, :, 1, :])
        tc = k.g_copy(kv[:, :, 5, :], kv[:, :, 0, :])
        s1 = S1.take()
        bb = s1.ap[:, 0, :].bitcast(BF16).rearrange("p (h n) -> p h n", n=P)
        for h in range(8):
            t = k.tr(bb[:, h, :], buf[:, h, :], s1.free, tc, ta, tb, sig=(h == 7))
        k.tkst = [t]
        t = k.acopy(s["ks"].ap[:, :, t4 * P:t4 * P + P], bb, t, s["ks"].free)
        s1.done(t)
        s["tk"][t4] = t

    def qprep(i):
        s = st[i]
        q = s["q"] = QS.take()
        sc = qsc.rearrange("p (h d) -> p h d", d=16)
        b = qst.take()
        qv = b.ap.rearrange("p h (r d) -> p h r d", d=16)
        t0 = k.v_ts(qsc, k.X[:, i, :], 0.25, None, ALU.mult, None, k.xtok[i], k.dve.last)
        rr = qres.rearrange("p (h d) -> p h d", d=16)
        t = split3(k, [qv[:, :, 0, :], qv[:, :, 2, :], qv[:, :, 5, :]], sc, rr, t0, b.free)
        for dst, src in ((1, 0), (3, 2), (4, 0)):
            t = k.g_copy(qv[:, :, dst, :], qv[:, :, src, :], t)
        s["tq"] = []
        for h4 in range(2):
            s1 = S1.take()
            for j in range(2):
                bb = s1.ap[:, j, :].bitcast(BF16).rearrange("p (h n) -> p h n", n=P)
                for h in range(8):
                    t1 = k.tr(bb[0:96, h, :], b.ap[:, 16 * h4 + 8 * j + h, :], s1.free, t, sig=(h == 7))
                dst = q.ap[0:96, 16 * h4 + 8 * j:16 * h4 + 8 * j + 8, :]
                te = k.acopy(dst, bb[0:96], t1, q.free) if j == 0 else k.v_copy(dst, bb[0:96], t1, q.free)
                s["tq"].append(te)
            s1.done(*s["tq"][-2:])
        b.done(t1)

    def first(i, j):
        s = st[i]
        s1 = S1.take()
        for u in range(2):
            h = 2 * j + u
            t = k.mm(s1.ap[:, u, :], s["q"].ap[0:96, h, :], kb[i // 4]["ks"].ap[0:96, h // 4, :], True, True,
                     s1.free, s["tq"], kb[i // 4]["tk"], sig=(u == 1))
        t = k.v_red(MX[:, i % 2, 2 * j:2 * j + 2], s1.ap, ALU.max, t, s["mfree"], negate=True)
        s1.done(t)
        s["tmx"] = t

    def maxrows(i):
        s = st[i]
        parts = [ms.rearrange("p (r h) -> p r h", h=32)[:, r, :] for r in range(3)]
        t = split3(k, parts, MX[:, i % 2, :], mres, s["tmx"], k.msfree)
        s1 = S1.take()
        bb = s1.ap[:, 0, 0:64].bitcast(BF16)
        t = k.tr(bb[0:96, :], ms, s1.free, t, sig=True)
        k.msfree = t
        m = MT.take()
        t = k.v_copy(m.ap[0:96, :], bb[0:96, :], t, m.free)
        s1.done(t)
        t = k.dma(s["q"].ap[96:99, :, :], m.ap[0:96, :], t, s["q"].free)
        m.done(t)
        s["tmr"] = t

    k.msfree = None

    def second(i, h):
        s = st[i]
        kk = kb[i // 4]
        s2 = S2.take()
        bb = s2.ap.rearrange("p (t n) -> p t n", t=4)
        for t4 in range(4):
            t = k.mm(bb[:, t4, :], kk["ks"].ap[0:99, h // 4, t4 * P:t4 * P + P], s["q"].ap[0:99, h, :], True, True,
                     s2.free, s["tmr"], s["tq"], kk["tk"], sig=(t4 == 3))
        p = PT.take()
        t = k.activ(p.ap, bb, ACT.Exp, t, p.free)
        s2.done(t)
        s["p"].append((h, p, t))

    def pv(i):
        s = st[i]
        h, p, t = s["p"].pop(0)
        kk = kb[i // 4]
        if h % 16 == 0:
            s["ob"] = OB.take()
        ob = s["ob"]
        for t4 in range(4):
            t2 = k.mm(ob.ap[:, h % 16, :], p.ap[:, t4, :], kk["va"].ap[:, t4, h // 4, :], t4 == 0 and h % 16 == 0, t4 == 3,
                      ob.free, t, kk["tv"], kk["tva"], sig=(t4 == 3))
        p.done(t2)
        if h % 16 == 15:
            if h == 15:
                s["oa"] = oa.take()
                s["toa"] = []
            hh = h // 16
            r = rz[:, i % 2, 16 * hh:16 * hh + 16]
            t3 = k.v_recip(r.unsqueeze(2), ob.ap[:, :, 16:17], t2, s["mfree"])
            o = s["oa"].ap[:, 256 * hh:256 * hh + 256].rearrange("p (h d) -> p h d", d=16)
            t3 = k.v_tt(o, ob.ap[:, :, 0:16], r.unsqueeze(2).to_broadcast([P, 16, 16]), ALU.mult, t3, s["oa"].free)
            ob.done(t3)
            s["toa"].append(t3)
        if h == 31:
            s["q"].done(t2, k.pe.last)
            def add(z, *w):
                t = k.g_tt(z, k.X[:, i, :], s["oa"].ap, ALU.add, s["toa"], *w, k.xtok[i])
                s["oa"].done(t)
                return t
            k.ln(i, add)
            if i % 4 == 3:
                kk["ks"].done(k.pe.last)
                kk["va"].done(k.pe.last)

    for t4 in range(4):
        prep(0, t4)
    for i in range(NT + 1):
        if i < NT:
            st[i]["mfree"] = k.dve.last
            st[i]["p"] = []
            if i == 0:
                qprep(0)
        for j in range(16):
            if i < NT:
                first(i, j)
            if i >= 1:
                second(i - 1, 2 * j)
                if j > 0:
                    pv(i - 1)
                second(i - 1, 2 * j + 1)
                pv(i - 1)
            if i < NT and i % 4 == 3 and i // 4 < 3 and j in (3, 6, 9, 12):
                prep(i // 4 + 1, j // 3 - 1)
        if i >= 1:
            pv(i - 1)
        if i < NT:
            maxrows(i)
        if i + 1 < NT:
            qprep(i + 1)
    k.ln_flush()
def rows(ap):
    return ap.rearrange("(k p) n -> p k n", p=P)


def stats(k, z, st6, mv4, eps, *w):
    k.dve.wait(*w)
    t = k.dve.sig(k.nc.vector.bn_stats(st6, z))
    tr = t
    k.dve.wait(t)
    t = k.dve.sig(k.nc.vector.bn_aggr(mv4[:, 0:2], st6))
    t = k.g_ts(mv4[:, 2:3], mv4[:, 1:2], eps, 1.0, ALU.add, ALU.mult, t)
    return k.g_tt(mv4[:, 3:4], mv4[:, 2:3], k.nhalf[:, 0:1], ALU.pow, t), tr


def ffn(k, first_layer):
    nc = k.nc
    k.phase("ffn" + str(int(first_layer)))
    k.off = k.base
    W1 = k.alloc([4, 2048])
    W2 = k.alloc([16, 512])
    if first_layer:
        w1, w2 = rows(k.ins["L0_ffn_up_w"]), rows(k.ins["L0_ffn_down_w"])
        WE = k.alloc([4, 512])
        WG = k.alloc([4, 8])
        G = k.alloc([2, 512])
    else:
        w1, w2 = rows(k.ins["L3_ffn_w1"]), rows(k.ins["L3_ffn_w2"])
        B1 = k.alloc([16])
        B2 = k.alloc([512])
    tw1 = [k.dma(W1[:, kk, :], w1[:, kk, :]) for kk in range(4)]
    if first_layer:
        tc = [k.dma(WE, rows(k.ins["L0_ffn_expert_weight"])), k.dma(WG, rows(k.ins["L0_ffn_gate_w"])),
              k.dma(G, k.ins["L0_ffn_ln"])]
    else:
        tc = [k.dma(B1, k.ins["L3_ffn_b1"]), k.dma(B2, k.ins["L3_ffn_b2"])]
    tw2 = [k.dma(W2[:, 4 * j:4 * j + 4, :], w2[:, 4 * j:4 * j + 4, :]) for j in range(4)]
    XT = Ring([k.alloc([4, 512]) for _ in range(2)])
    HT = Ring([k.alloc([512]) for _ in range(4)])
    YS = Ring([k.alloc([512]) for _ in range(3)])
    ES = Ring([k.alloc([512]) for _ in range(2)])
    sm = k.alloc([NT, 24])
    YB = [k.bank(j)[:, 0, :] for j in range(4)]
    yfree = [[] for _ in range(4)]
    H = Ring([k.bank(4)[:, 0, :], k.bank(5)[:, 0, :]])
    R = Ring([k.bank(6)[:, 0, :], k.bank(7)[:, 0, :]])

    if not first_layer:
        cnt = 1.0 / (2048 * 512)
        part = k.alloc([8])
        thr = k.alloc([4])
        ones = k.alloc([P])
        tmp = Ring([k.alloc([2048]) for _ in range(2)])
        k.pool.wait()
        to = k.pool.sig(nc.gpsimd.memset(ones, 1.0))
        tq = []
        for n, (W, tw) in enumerate(((W1.rearrange("p a b -> p (a b)"), tw1), (W2.rearrange("p a b -> p (a b)"), tw2))):
            tp = [k.v_red(part[:, 4 * n + j:4 * n + j + 1], W[:, 2048 * j:2048 * j + 2048], ALU.add, tw[j],
                          absolute=True) for j in range(4)]
            t = k.v_red(thr[:, 2 * n:2 * n + 1], part[:, 4 * n:4 * n + 4], ALU.add, tp)
            b = R.take()
            t = k.mm(b.ap[:, 0:1], ones, thr[:, 2 * n:2 * n + 1], True, True, b.free, t, to, sig=True)
            t = k.v_ts(thr[:, 2 * n:2 * n + 1], b.ap[:, 0:1], cnt, 0.7, ALU.mult, ALU.mult, t)
            b.done(t)
            t = k.v_ts(thr[:, 2 * n + 1:2 * n + 2], thr[:, 2 * n:2 * n + 1], -1.0, None, ALU.mult, None, t)
            tj = []
            for j in range(4):
                s = tmp.take()
                w = W[:, 2048 * j:2048 * j + 2048]
                t2 = k.v_ts(s.ap, w, thr[:, 2 * n + 1:2 * n + 2], None, ALU.is_le, None, t, s.free)
                t2 = k.v_stt(w, w, thr[:, 2 * n:2 * n + 1], s.ap, ALU.is_ge, ALU.subtract, t2)
                s.done(t2)
                tj.append(t2)
            tq.append(tj)
        tw1, tw2 = tq

    def xt(b):
        s = XT.take()
        s.toks = []
        for t4 in range(4):
            s.toks.append(k.x_to_xt(4 * b + t4, R, s.ap[:, :, t4 * P:t4 * P + P], s.free, eng=t4 % 2))
        return s

    xs = {0: xt(0)}

    def up(b, m):
        h = H.take()
        for kk in range(4):
            t = k.mm(h.ap, W1[:, kk, m * P:m * P + P], xs[b].ap[:, kk, :], kk == 0, kk == 3, h.free, xs[b].toks,
                     tw1[kk], sig=(kk == 3))
        o = HT.take()
        if first_layer:
            t = k.activ(o.ap, h.ap, ACT.Relu, t, o.free)
            h.done(t)
            t = k.activ(o.ap, o.ap, ACT.Square, t) if m % 2 else k.v_tt(o.ap, o.ap, o.ap, ALU.mult, t)
        else:
            t = k.activ(o.ap, h.ap, ACT.Gelu, t, o.free, tc, bias=B1[:, m:m + 1])
            h.done(t)
        return o, t

    def down(b, m, ot):
        o, t = ot
        for t4 in range(4):
            td = k.mm(YB[t4], o.ap[:, t4 * P:t4 * P + P], W2[:, m, :], m == 0, m == 15, t, tw2[m // 4],
                      yfree[t4], sig=(m == 15 or t4 == 3))
            if m == 15:
                ydone[t4] = td
        o.done(td)

    def gate(i, t4):
        x = xs[i // 4]
        r = R.take()
        for kk in range(4):
            t = k.mm(r.ap[:, 0:8], x.ap[:, kk, t4 * P:t4 * P + P], WG[:, kk, :], kk == 0, kk == 3, r.free, x.toks, tc,
                     sig=(kk == 3))
        k.dve.wait(t)
        t = k.dve.sig(nc.vector.max(sm[:, i, 0:8], r.ap[:, 0:8]))
        r.done(t)
        ts = k.v_tt(sm[:, i, 8:9], sm[:, i, 0:1], sm[:, i, 1:2], ALU.add, t)
        r = R.take()
        for kk in range(4):
            t = k.mm(r.ap, x.ap[:, kk, t4 * P:t4 * P + P], WE[:, kk, :], kk == 0, kk == 3, r.free, sig=(kk == 3))
        e = ES.take()
        t = k.activ(e.ap, r.ap, ACT.Copy, t, ts, e.free, scale=sm[:, i, 8:9])
        r.done(t)
        return e, t

    def finish(i, t4):
        if first_layer:
            e, te = gate(i, t4)
            y = YS.take()
            ty = k.v_tt(y.ap, YB[t4], e.ap, ALU.add, ydone[t4], te, y.free)
            yfree[t4] = [ty]
            e.done(ty)
            ts, _ = stats(k, y.ap, sm[:, i, 9:15], sm[:, i, 16:20], 1e-5, ty)
            return y, ts, i
        y = YS.take()
        tx = k.g_tt(y.ap, k.X[:, i, :], B2, ALU.add, k.xtok[i], tc, y.free)

        def add(z, *w):
            t = k.v_tt(z, y.ap, YB[t4], ALU.add, tx, *w)
            yfree[t4] = [t]
            y.done(t)
            return t
        k.ln(i, add, ydone[t4])
        return None

    def finish2(v):
        y, ts, i = v
        t = k.v_ts(y.ap, y.ap, sm[:, i, 16:17], sm[:, i, 19:20], ALU.subtract, ALU.mult, ts)
        t = k.g_tt(y.ap, y.ap, G[:, 0, :], ALU.mult, t, tc)
        t = k.g_tt(y.ap, y.ap, G[:, 1, :], ALU.add, t)

        def add(z, *w):
            t2 = k.v_tt(z, y.ap, k.X[:, i, :], ALU.add, t, *w, k.xtok[i])
            y.done(t2)
            return t2
        k.ln(i, add)

    ydone = [None] * 4
    pend = []
    for b in range(4):
        q = []
        for m in range(16):
            q.append(up(b, m))
            if m >= 2:
                down(b, m - 2, q[m - 2])
            if m == 8 and b < 3:
                xs[b + 1] = xt(b + 1)
        down(b, 14, q[14])
        down(b, 15, q[15])
        for t4 in range(4):
            v = finish(4 * b + t4, t4)
            if v:
                pend.append(v)
                if len(pend) > 1:
                    finish2(pend.pop(0))
        xs[b].done(k.pe.last)
    while pend:
        finish2(pend.pop(0))
    k.ln_flush()


def l0_ffn(k):
    ffn(k, True)


def l3_ffn(k):
    ffn(k, False)


def attn(k, label, kind):
    nc = k.nc
    k.phase(label)
    k.off = k.base
    ins = k.ins
    lat = kind == 1
    SC = float(32) ** -0.5
    WQ = k.alloc([4, 512])
    nk = 1 if lat else 4
    WK, WV = k.alloc([nk, 512]), k.alloc([nk, 512])
    WO = k.alloc([4, 512])
    tw = [k.dma(w, rows(ins[label + n])) for w, n in ((WQ, "_q"), (WK, "_k"), (WV, "_v"), (WO, "_o"))]
    XT = Ring([k.alloc([4, P]) for _ in range(2)])
    if lat:
        CT = k.alloc([4, 512])
        tw.append(k.dma(CT, ins["ctx_T"]))
    else:
        BQ, BK, BV, BO = k.alloc([4]), k.alloc([4]), k.alloc([512]), k.alloc([512])
        tw += [k.dma(w, ins[label + n]) for w, n in ((BQ, "_bq"), (BK, "_bk"), (BV, "_bv"), (BO, "_bo"))]
    QT = Ring([k.alloc([4, P]) for _ in range(3)])
    KT = Ring([k.alloc([4, 512]) for _ in range(2)])
    if kind == 2:
        V = Ring([k.alloc([512]) for _ in range(3)])
        JK = Ring([k.alloc([512]) for _ in range(2)])
        SM = k.alloc([2, 4, 16])
    else:
        VA = Ring([k.alloc([4, 16, 33]) for _ in range(2)])
        k.pool.wait()
        for b in VA.bufs:
            tva = k.pool.sig(nc.gpsimd.memset(b[:, :, :, 32:33], 1.0))
        PT = Ring([k.alloc([2, 512]) for _ in range(4)])
        NS = k.alloc([4, 32], BF16)
        NM = Ring([k.alloc([P], BF16) for _ in range(2)])
        SEL = k.alloc([4, P], BF16)
        stg = k.alloc([4, P])
        t = k.dma(stg, ins["c_sel"])
        tsel = [k.v_copy(SEL, stg, t)]
        k.pool.wait()
        tsel.append(k.pool.sig(nc.gpsimd.memset(NS, 0.0)))
        mres = k.alloc([16])
        rz = k.alloc([2, 16])
    MX = k.alloc([2, 4, 4])
    ON = Ring([k.alloc([512]) for _ in range(2)])
    OT = Ring([k.alloc([4, P]) for _ in range(2)])
    XB = Ring([k.alloc([512]) for _ in range(2)])
    A = Ring([k.bank(0, 2), k.bank(2, 2)])
    S2 = Ring([k.bank(4, 2)])
    OB = Ring([k.bank(6)[:, 0, 0:264].rearrange("p (h e) -> p h e", e=33),
               k.bank(7)[:, 0, 0:264].rearrange("p (h e) -> p h e", e=33)])
    st = [dict() for _ in range(NT)]
    kb = [dict() for _ in range(4)]
    free = {"mx": [None, None], "ns": None, "rz": [None, None]}

    def v4(ap):
        return ap.rearrange("p (m n) -> p m n", m=4)

    def proj(i):
        s, b, t4 = st[i], kb[i // 4], i % 4
        if t4 == 0:
            b["kt"] = KT.take()
            b["tk"] = []
            if kind != 2:
                b["v"] = VA.take()
                b["tv"] = [tva]
        a = A.take()
        xt = XT.take()
        bb = v4(a.ap[:, 0, :])
        for kk in range(4):
            t = k.tr(bb[:, kk, :], k.X[:, i, kk * P:kk * P + P], a.free, k.xtok[i], sig=(kk == 3))
        txt = k.acopy(xt.ap, bb, t, xt.free)
        a.done(txt)
        a = A.take()
        q = s["q"] = QT.take()
        bb = v4(a.ap[:, 0, :])
        for m in range(4):
            for kk in range(4):
                t = k.mm(bb[:, m, :], WQ[:, kk, m * P:m * P + P], xt.ap[:, kk, :], kk == 0, kk == 3, a.free, tw, txt,
                         sig=(kk == 3 and m == 3))
        if lat:
            t1 = k.acopy(q.ap, bb, t, q.free)
        else:
            t1 = k.v_tt(q.ap, bb, BQ.unsqueeze(2).to_broadcast([P, 4, P]), ALU.add, t, q.free)
        s["tq"] = t1
        bb = v4(a.ap[:, 1, :])
        for m in range(4):
            for kk in range(nk):
                r = CT[:, i // 4, t4 * P:t4 * P + P] if lat else xt.ap[:, kk, :]
                t = k.mm(bb[:, m, :], WK[:, kk, m * P:m * P + P], r, kk == 0, kk == nk - 1, sig=(kk == nk - 1 and m == 3))
        dst = b["kt"].ap[:, :, t4 * P:t4 * P + P]
        if lat:
            t2 = k.acopy(dst, bb, t, b["kt"].free)
        else:
            t2 = k.v_tt(dst, bb, BK.unsqueeze(2).to_broadcast([P, 4, P]), ALU.add, t, b["kt"].free)
        a.done(t1, t2)
        b["tk"].append(t2)
        a = A.take()
        for kk in range(nk):
            l = CT[:, i // 4, t4 * P:t4 * P + P] if lat else xt.ap[:, kk, :]
            t = k.mm(a.ap[:, 0, :], l, WV[:, kk, :], kk == 0, kk == nk - 1, a.free, sig=(kk == nk - 1))
        xt.done(t)
        src = a.ap[:, 0, :].rearrange("p (h d) -> p h d", d=32)
        if kind == 2:
            v = s["v"] = V.take()
            t = s["tv"] = k.v_tt(v.ap, a.ap[:, 0, :], BV, ALU.add, t, v.free)
        elif lat:
            t = k.acopy(b["v"].ap[:, t4, :, 0:32], src, t, b["v"].free)
            b["tv"].append(t)
        else:
            t = k.v_tt(b["v"].ap[:, t4, :, 0:32], src, BV.rearrange("p (h d) -> p h d", d=32), ALU.add, t, b["v"].free)
            b["tv"].append(t)
        a.done(t)

    def first(i, hg, u):
        s, b, n = st[i], kb[i // 4], (i % 4 + 1) * P
        a = A.take()
        for g in range(2):
            r0 = 32 * (2 * u + g)
            k.mm(a.ap[:, g, 0:n], s["q"].ap[r0:r0 + 32, hg, :], b["kt"].ap[r0:r0 + 32, hg, 0:n], True, False,
                 a.free, s["tq"], b["tk"])
            t = k.mm(a.ap[:, g, n - P:n], k.idb, k.mq, False, True, sig=(g == 1))
        tm = k.v_red(MX[:, i % 2, 2 * u:2 * u + 2, hg], a.ap[:, :, 0:n], ALU.max, t, free["mx"][i % 2], negate=True)
        if kind == 2:
            for g in range(2):
                g4 = 2 * u + g
                j = JK.take()
                tb = k.v_ts(SM[:, i % 2, 0, 4 * hg + g4:4 * hg + g4 + 1], MX[:, i % 2, g4, hg:hg + 1], SC, None, ALU.mult,
                            None, tm, s["smfree"])
                t = k.activ(j.ap[:, 0:n], a.ap[:, g, 0:n], ACT.Exp, tb, j.free, s["smfree"],
                            bias=SM[:, i % 2, 0, 4 * hg + g4:4 * hg + g4 + 1], scale=SC,
                            accum=SM[:, i % 2, 1, 4 * hg + g4:4 * hg + g4 + 1])
                j.done(t)
            tm = t
        a.done(tm)
        s["tm"] = tm

    def maxrows(i):
        s = st[i]
        parts = [NS[:, :, 4 * r:4 * r + 4] for r in range(3)]
        t = split3(k, parts, MX[:, i % 2], mres.rearrange("p (a b) -> p a b", b=4), s["tm"], free["ns"], tsel)
        free["mx"][i % 2] = t
        a = A.take()
        bb = a.ap[:, 0, 0:64].bitcast(BF16)
        t = free["ns"] = k.tr(bb, NS.rearrange("p a b -> p (a b)"), a.free, t, sig=True)
        m = s["nm"] = NM.take()
        s["tnm"] = k.v_copy(m.ap, bb, t, m.free)
        a.done(s["tnm"])

    def second(i, hg, u):
        s, b, n = st[i], kb[i // 4], i % 4 + 1
        a = S2.take()
        for g in range(2):
            r0 = 32 * (2 * u + g)
            for kt in range(n):
                o = a.ap[:, g, kt * P:kt * P + P]
                k.mm(o, b["kt"].ap[r0:r0 + 32, hg, kt * P:kt * P + P], s["q"].ap[r0:r0 + 32, hg, :], True, False,
                     a.free, s["tq"], b["tk"], s["tnm"])
                if kt == n - 1:
                    k.mm(o, k.idb, k.mk, False, False)
                t = k.mm(o, SEL[r0:r0 + 12, hg, :], s["nm"].ap[r0:r0 + 12, :], False, True, tsel,
                         sig=(g == 1 and kt == n - 1))
        p = PT.take()
        t = k.activ(p.ap[:, :, 0:n * P], a.ap[:, :, 0:n * P], ACT.Exp, t, p.free, scale=SC)
        a.done(t)
        s["p"].append((hg, u, p, t))

    def pv(i):
        s, b, n = st[i], kb[i // 4], i % 4 + 1
        hg, u, p, t = s["p"].pop(0)
        if hg % 2 == 0 and u == 0:
            s["ob"] = OB.take()
        ob = s["ob"]
        for g in range(2):
            h8 = 4 * (hg % 2) + 2 * u + g
            for kt in range(n):
                t2 = k.mm(ob.ap[:, h8, :], p.ap[:, g, kt * P:kt * P + P], b["v"].ap[:, kt, 4 * hg + 2 * u + g, :],
                          kt == 0 and h8 == 0, kt == n - 1, ob.free, t, b["tv"], sig=(g == 1 and kt == n - 1))
        p.done(t2)
        if hg % 2 == 1 and u == 1:
            half = hg // 2
            if half == 0:
                s["on"] = ON.take()
                s["ton"] = []
            r = rz[:, i % 2, 8 * half:8 * half + 8].unsqueeze(2)
            t3 = k.v_recip(r, ob.ap[:, :, 32:33], t2, free["rz"][i % 2])
            o = s["on"].ap[:, 256 * half:256 * half + 256].rearrange("p (h d) -> p h d", d=32)
            t3 = k.v_tt(o, ob.ap[:, :, 0:32], r.to_broadcast([P, 8, 32]), ALU.mult, t3, s["on"].free)
            ob.done(t3)
            s["ton"].append(t3)
            if half == 1:
                free["rz"][i % 2] = t3
                s["q"].done(t2)
                s["nm"].done(t2)
                if i % 4 == 3:
                    b["kt"].done(t2)
                    b["v"].done(t2)

    def out(i):
        s = st[i]
        if kind == 2:
            if i % 4 == 3:
                kb[i // 4]["kt"].done(k.pe.last)
            s["q"].done(k.pe.last)
            on = s["on"] = ON.take()
            n, r, m = (SM[:, i % 2, j, :] for j in (1, 2, 3))
            t = k.v_recip(r, n, s["tm"])
            t = k.v_tt(m, n, r, ALU.mult, t)
            t = k.v_tt(on.ap.rearrange("p (h d) -> p h d", d=32), s["v"].ap.rearrange("p (h d) -> p h d", d=32),
                       m.unsqueeze(2).to_broadcast([P, 16, 32]), ALU.mult, t, s["tv"], on.free)
            s["v"].done(t)
            s["ton"] = [t]
            s["tsm"] = t
        a = A.take()
        bb = v4(a.ap[:, 0, :])
        for kk in range(4):
            t = k.tr(bb[:, kk, :], s["on"].ap[:, kk * P:kk * P + P], a.free, s["ton"], sig=(kk == 3))
        s["on"].done(t)
        o = OT.take()
        t = k.acopy(o.ap, bb, t, o.free)
        for kk in range(4):
            t2 = k.mm(a.ap[:, 1, :], o.ap[:, kk, :], WO[:, kk, :], kk == 0, kk == 3, t, sig=(kk == 3))
        o.done(t2)
        if lat:
            k.ln(i, k.add_from(i, a.ap[:, 1, :], a), t2)
            return
        xb = XB.take()
        tb = k.g_tt(xb.ap, k.X[:, i, :], BO, ALU.add, k.xtok[i], xb.free, tw)

        def add(z, *w):
            t = k.v_tt(z, xb.ap, a.ap[:, 1, :], ALU.add, tb, *w)
            a.done(t)
            xb.done(t)
            return t
        k.ln(i, add, t2)

    proj(0)
    for i in range(NT + 1):
        if i < NT:
            st[i]["p"] = []
            st[i]["smfree"] = st[i - 2]["tsm"] if kind == 2 and i >= 2 else None
        for j in range(8):
            if i < NT:
                first(i, j // 2, j % 2)
            if i >= 1 and kind != 2:
                second(i - 1, j // 2, j % 2)
                if j >= 1:
                    pv(i - 1)
            if j == 4 and i + 1 < NT:
                proj(i + 1)
        if kind != 2:
            if i < NT:
                maxrows(i)
            if i >= 1:
                pv(i - 1)
        if i >= 1:
            out(i - 1)
    k.ln_flush()


def l2_attn(k):
    attn(k, "L2_attn", 0)


def l2_xattn(k):
    attn(k, "L2_xattn", 1)


def l3_attn(k):
    attn(k, "L3_attn", 2)


def l3_xattn(k):
    nc = k.nc
    k.phase("l3xattn")
    k.off = k.base
    ins = k.ins
    CT = k.alloc([4, 512])
    WK = k.alloc([P])
    bk = k.alloc([1])
    GB = k.alloc([2, 512])
    KT = Ring([k.alloc([512]) for _ in range(2)])
    KV = Ring([k.alloc([4, P]) for _ in range(2)])
    XT = Ring([k.alloc([4, P]) for _ in range(2)])
    OT = Ring([k.alloc([P]) for _ in range(2)])
    ZZ = Ring([k.alloc([512]) for _ in range(4)])
    sm = k.alloc([NT, 16])
    R = Ring([k.bank(j)[:, 0, :] for j in range(8)])
    tc = [k.dma(CT, ins["ctx_T"]), k.dma(WK, ins["L3_xattn_W_k"]), k.dma(bk, ins["L3_xattn_b_k"]),
          k.dma(GB, ins["L3_xattn_ln"])]
    SC = float(512) ** -0.5
    kb = [dict() for _ in range(4)]
    st = [dict() for _ in range(NT)]

    def keys(b):
        s = kb[b]
        r = R.take()
        t = k.mm(r.ap, WK, CT[:, b, :], True, True, r.free, tc, sig=True)
        s["kt"], s["kv"] = KT.take(), KV.take()
        t = k.activ(s["kt"].ap, r.ap, ACT.Identity, t, s["kt"].free, bias=bk[:, 0:1])
        r.done(t)
        s["tk"] = t
        r = R.take()
        bb = r.ap.rearrange("p (m n) -> p m n", m=4)
        for m in range(4):
            t = k.tr(bb[:, m, :], s["kt"].ap[:, m * P:m * P + P], r.free, s["tk"], sig=(m == 3))
        s["tv"] = k.v_copy(s["kv"].ap, bb, t, s["kv"].free)
        r.done(s["tv"])

    def a(i):
        if i % 4 == 0:
            keys(i // 4)
        s = st[i]
        s["xt"] = XT.take()
        s["txt"] = k.x_to_xt(i, R, s["xt"].ap, s["xt"].free, eng=0)

    def b(i):
        s, b = st[i], kb[i // 4]
        r = R.take()
        for kk in range(4):
            t = k.mm(r.ap[:, 0:P], b["kv"].ap[:, kk, :], s["xt"].ap[:, kk, :], kk == 0, kk == 3, r.free, b["tv"], s["txt"],
                     sig=(kk == 3))
        s["xt"].done(t)
        o = OT.take()
        to = k.acopy(o.ap, r.ap[:, 0:P], t, o.free)
        r.done(to)
        r = R.take()
        t = k.mm(r.ap, o.ap, b["kt"].ap, True, True, r.free, to, b["tk"], sig=True)
        o.done(t)
        if i % 4 == 3:
            b["kt"].done(t)
            b["kv"].done(t)
        m = sm[:, i, :]
        k.dve.wait(t)
        t1 = k.dve.sig(nc.vector.bn_stats(m[:, 0:6], r.ap))
        k.dve.wait(t1)
        t1 = k.dve.sig(nc.vector.bn_aggr(m[:, 6:8], m[:, 0:6]))
        t1 = k.g_ts(m[:, 8:9], m[:, 7:8], SC * SC, 1e-6, ALU.mult, ALU.add, t1)
        t1 = k.g_tt(m[:, 9:10], m[:, 8:9], k.nhalf[:, 0:1], ALU.pow, t1)
        t1 = k.g_ts(m[:, 10:11], m[:, 9:10], SC, 1.0, ALU.mult, ALU.mult, t1)
        s["r"], s["t1"] = r, t1

    def c(i):
        s = st[i]
        m = sm[:, i, :]
        r = s["r"]
        z = ZZ.take()
        t = k.v_ts(z.ap, r.ap, m[:, 6:7], m[:, 10:11], ALU.subtract, ALU.mult, s["t1"], z.free)
        r.done(t)
        t = k.g_tt(z.ap, z.ap, GB[:, 0, :], ALU.mult, t, tc)
        s["tz"] = k.g_tt(z.ap, z.ap, GB[:, 1, :], ALU.add, t)
        s["z"] = z

    def d(i):
        s = st[i]
        m, z = sm[:, i, :], s["z"]
        t = k.v_red(m[:, 11:12], z.ap, ALU.max, s["tz"], negate=True)
        t = k.activ(z.ap, z.ap, ACT.Exp, t, bias=m[:, 11:12], accum=m[:, 12:13])
        t = k.v_recip(m[:, 13:14], m[:, 12:13], t)

        def add(zz, *w):
            t2 = k.v_stt(zz, z.ap, m[:, 13:14], k.X[:, i, :], ALU.mult, ALU.add, t, *w, k.xtok[i])
            z.done(t2)
            return t2
        k.ln(i, add)

    pipeline(NT, [(0, a), (1, b), (2, c), (3, d)])
    k.ln_flush()


def l1_xattn(k):
    nc = k.nc
    k.phase("l1xattn")
    k.off = k.base
    ins = k.ins
    CT = k.alloc([4, 512])
    W = k.alloc([2, P])
    gr = k.alloc([4])
    QT, KT = (Ring([k.alloc([512]) for _ in range(2)]) for _ in range(2))
    SS = Ring([k.alloc([512]) for _ in range(3)])
    WK = Ring([k.alloc([512]) for _ in range(2)])
    m8 = k.alloc([2, 8])
    AL = Ring([k.alloc([4, 512]) for _ in range(2)])
    BB = Ring([k.alloc([512]) for _ in range(2)])
    XS = Ring([k.alloc([512]) for _ in range(2)])
    R = Ring([k.bank(j)[:, 0, :] for j in range(8)])
    tc = [k.dma(CT, ins["ctx_T"]), k.dma(W, ins["L1_xattn_W"])]
    t = k.dma(gr[:, 0:1], ins["L1_gamma"])
    t = k.activ(gr[:, 1:2], gr[:, 0:1], ACT.Exp, t, scale=-1.0)
    t = k.v_ts(gr[:, 1:2], gr[:, 1:2], 1.0, None, ALU.add, None, t)
    t = k.v_recip(gr[:, 1:2], gr[:, 1:2], t)
    tg = [k.v_ts(gr[:, 2:3], gr[:, 1:2], -1.0, 2.0, ALU.mult, ALU.add, t),
          k.v_ts(gr[:, 3:4], gr[:, 1:2], 0.5, None, ALU.mult, None, t)]
    SC = 1.0 / (float(np.sqrt(np.float32(32))) * 4)
    kb = [dict() for _ in range(4)]

    def sims(b):
        s = kb[b]
        for j, (ring, n) in enumerate(((QT, "q"), (KT, "k"))):
            r = R.take()
            t = k.mm(r.ap, W[:, j, :], CT[:, b, :], True, True, r.free, tc, sig=True)
            s[n] = ring.take()
            if j == 0:
                t = k.activ(s[n].ap, r.ap, ACT.Copy, t, s[n].free, scale=SC)
            else:
                t = k.acopy(s[n].ap, r.ap, t, s[n].free)
            r.done(t)
            s["t" + n] = t
        s["al"] = AL.take()
        s["ta"] = []

    def topk(b, t4):
        s = kb[b]
        r = R.take()
        t = k.mm(r.ap, s["q"].ap[:, t4 * P:t4 * P + P], s["k"].ap, True, True, r.free, s["tq"], s["tk"], sig=True)
        if t4 == 3:
            s["q"].done(t)
            s["k"].done(t)
        o = SS.take()
        ts = k.acopy(o.ap, r.ap, t, o.free)
        r.done(ts)
        w = WK.take()
        m = m8[:, (4 * b + t4) % 2, :]
        k.dve.wait(ts, w.free)
        k.dve.wait(k.dve.last)
        t = k.dve.sig(nc.vector.max(m, o.ap))
        for n in range(19):
            k.dve.wait(t)
            t = k.dve.sig(nc.vector.match_replace(w.ap, m, o.ap if n == 0 else w.ap, -3.0e38))
            k.dve.wait(t)
            t = k.dve.sig(nc.vector.max(m, w.ap))
        w.done(t)
        te = k.activ(w.ap, o.ap, ACT.Exp, t, scale=-1.0)
        te = k.v_ts(w.ap, w.ap, 1.0, None, ALU.add, None, te)
        te = k.v_recip(w.ap, w.ap, te)
        al = s["al"]
        t = k.v_stt(al.ap[:, t4, :], o.ap, m[:, 0:1], w.ap, ALU.is_ge, ALU.mult, te, al.free)
        w.done(t)
        o.done(t)
        s["ta"].append(t)

    def mix(i):
        s, t4 = kb[i // 4], i % 4
        al = s["al"]
        r = R.take()
        bb = r.ap.rearrange("p (m n) -> p m n", m=4)
        for m in range(4):
            t = k.tr(bb[:, m, :], al.ap[:, m, t4 * P:t4 * P + P], r.free, s["ta"], sig=(m == 3))
        o = BB.take()
        x = XS.take()
        tx = k.activ(x.ap, k.X[:, i, :], ACT.Copy, x.free, k.xtok[i], tg, scale=gr[:, 2:3])
        t = k.v_tt(o.ap, al.ap[:, t4, :], r.ap, ALU.add, t, o.free)
        r.done(t)
        if t4 == 3:
            al.done(t)

        def add(z, *w):
            t2 = k.v_stt(z, o.ap, gr[:, 3:4], x.ap, ALU.mult, ALU.add, t, tx, *w)
            o.done(t2)
            x.done(t2)
            return t2
        k.ln(i, add)

    for b in range(4):
        sims(b)
        for t4 in range(4):
            topk(b, t4)
        for t4 in range(4):
            mix(4 * b + t4)
    k.ln_flush()


MAGIC = 12582912.0


def l1_ffn(k):
    nc = k.nc
    k.phase("l1ffn")
    k.off = k.base
    ins = k.ins
    WG, WU = k.alloc([4, 2048], BF16), k.alloc([4, 2048], BF16)
    WD = k.alloc([16, 512], BF16)
    H = k.alloc([P])
    part = k.alloc([16])
    sc = k.alloc([8])
    ones = k.alloc([P])
    keep = k.off
    stg = [k.alloc([8192]) for _ in range(2)]
    R = Ring([k.bank(j)[:, 0, :] for j in range(8)])
    th = k.dma(H, ins["c_hadamard"])
    k.pool.wait()
    to = k.pool.sig(nc.gpsimd.memset(ones, 1.0))
    cnt = 1.0 / (2048 * 512)
    tw, sfree = [], [[], []]
    for n, (name, W) in enumerate((("L1_ffn_w_gate", WG), ("L1_ffn_w_up", WU), ("L1_ffn_w_down", WD))):
        S = stg[n % 2]
        src = rows(ins[name])
        kk = src.shape[1] // 4
        tl = [k.dma(S[:, 2048 * j:2048 * j + 2048].rearrange("p (k n) -> p k n", k=kk),
                    src[:, kk * j:kk * j + kk, :], sfree[n % 2]) for j in range(4)]
        tp = [k.v_red(part[:, 4 * n + j:4 * n + j + 1], S[:, 2048 * j:2048 * j + 2048], ALU.add, tl[j], absolute=True)
              for j in range(4)]
        t = k.v_red(sc[:, n:n + 1], part[:, 4 * n:4 * n + 4], ALU.add, tp)
        b = R.take()
        t = k.mm(b.ap[:, 0:1], ones, sc[:, n:n + 1], True, True, b.free, t, to, sig=True)
        t = k.v_ts(sc[:, n:n + 1], b.ap[:, 0:1], cnt, 1e-5, ALU.mult, ALU.max, t)
        b.done(t)
        t = k.v_recip(sc[:, 4 + n:5 + n], sc[:, n:n + 1], t)
        Wf = W.rearrange("p a b -> p (a b)")
        tj = []
        for j in range(4):
            w = S[:, 2048 * j:2048 * j + 2048]
            t2 = k.v_ts(w, w, sc[:, 4 + n:5 + n], 1.0, ALU.mult, ALU.min, t)
            t2 = k.v_ts(w, w, -1.0, MAGIC, ALU.max, ALU.add, t2)
            t2 = k.v_ts(Wf[:, 2048 * j:2048 * j + 2048], w, MAGIC, None, ALU.subtract, None, t2)
            tj.append(t2)
        sfree[n % 2] = tj
        tw.append(tj)
    tstage = [x for y in sfree for x in y]
    k.off = keep
    XQ = Ring([k.alloc([512]) for _ in range(2)], tstage)
    XB = Ring([k.alloc([512], BF16) for _ in range(2)], tstage)
    XT = Ring([k.alloc([4, P], BF16) for _ in range(2)], tstage)
    IM = Ring([k.alloc([2048]) for _ in range(2)], tstage)
    IT = Ring([k.alloc([16, P]) for _ in range(1)], tstage)
    HA = Ring([k.alloc([2048]) for _ in range(2)], tstage)
    HB = Ring([k.alloc([2048]) for _ in range(2)], tstage)
    YB = Ring([k.alloc([2048], BF16) for _ in range(1)], tstage)
    YT = Ring([k.alloc([16, P], BF16) for _ in range(2)], tstage)
    SG = Ring([k.alloc([512]) for _ in range(3)], tstage)
    sm = k.alloc([NT, 12])
    st = [dict() for _ in range(NT)]
    HN = float(1.0 / np.sqrt(2048))

    def a(i):
        s, m = st[i], sm[:, i, :]
        x = XQ.take()
        t = k.v_red(m[:, 0:1], k.X[:, i, :], ALU.max, k.xtok[i], tstage, absolute=True)
        t = k.v_ts(m[:, 0:1], m[:, 0:1], 1e-5, 1.0 / 128, ALU.max, ALU.mult, t)
        tr = k.v_recip(m[:, 1:2], m[:, 0:1], t)
        s["tf"] = [k.v_ts(m[:, 2:3], m[:, 0:1], sc[:, 0:1], None, ALU.mult, None, tr),
                   k.v_ts(m[:, 3:4], m[:, 0:1], sc[:, 1:2], None, ALU.mult, None, tr)]
        t = k.v_ts(x.ap, k.X[:, i, :], m[:, 1:2], 127.0, ALU.mult, ALU.min, tr, x.free)
        t = k.v_ts(x.ap, x.ap, -128.0, MAGIC, ALU.max, ALU.add, t)
        xb = XB.take()
        t = k.v_ts(xb.ap, x.ap, MAGIC, None, ALU.subtract, None, t, xb.free)
        x.done(t)
        r = R.take()
        bb = r.ap.bitcast(BF16)[:, 0:512].rearrange("p (m n) -> p m n", m=4)
        for kk in range(4):
            t1 = k.tr(bb[:, kk, :], xb.ap[:, kk * P:kk * P + P], r.free, t, sig=(kk == 3))
        xb.done(t1)
        s["xt"] = XT.take()
        s["txt"] = k.acopy(s["xt"].ap, bb, t1, s["xt"].free)
        r.done(s["txt"])

    def b(i):
        s, m = st[i], sm[:, i, :]
        im = s["im"] = IM.take()
        s["tim"] = []
        for c in range(4):
            r, r2 = R.take(), R.take()
            for kk in range(4):
                t = k.mm(r.ap, s["xt"].ap[:, kk, :], WG[:, kk, 512 * c:512 * c + 512], kk == 0, kk == 3, r.free,
                         s["txt"], tw[0], sig=(kk == 3))
            for kk in range(4):
                t2 = k.mm(r2.ap, s["xt"].ap[:, kk, :], WU[:, kk, 512 * c:512 * c + 512], kk == 0, kk == 3, r2.free,
                          tw[1], sig=(kk == 3))
            g = SG.take()
            t = k.activ(g.ap, r.ap, ACT.Silu, t, s["tf"], g.free, scale=m[:, 2:3])
            r.done(t)
            t = k.v_stt(im.ap[:, 512 * c:512 * c + 512], r2.ap, m[:, 3:4], g.ap, ALU.mult, ALU.mult, t, t2, im.free)
            r2.done(t)
            g.done(t)
            s["tim"].append(t)
        s["xt"].done(k.pe.last)

    def c(i):
        s, m = st[i], sm[:, i, :]
        im, it = s["im"], IT.take()
        te = []
        for c in range(4):
            r = R.take()
            bb = r.ap.rearrange("p (m n) -> p m n", m=4)
            for j in range(4):
                t = k.tr(bb[:, j, :], im.ap[:, (4 * c + j) * P:(4 * c + j + 1) * P], r.free, s["tim"], sig=(j == 3))
            te.append(k.acopy(it.ap[:, 4 * c:4 * c + 4, :], bb, t, it.free))
            r.done(te[-1])
        im.done(t)
        ha, hb = HA.take(), HB.take()
        tc = []
        for c in range(4):
            r = R.take()
            for j in range(4):
                t = k.mm(r.ap[:, j * P:j * P + P], it.ap[:, 4 * c + j, :], H, True, True, r.free, te[c], th, sig=(j == 3))
            tc.append(k.acopy(ha.ap[:, 512 * c:512 * c + 512], r.ap, t, ha.free))
            r.done(tc[-1])
        it.done(t)
        cur, nxt, t = ha, hb, tc
        nfree = hb.free
        for lv in range(4):
            h = P << lv
            v = cur.ap.rearrange("p (a t n) -> p a t n", t=2, n=h)
            o = nxt.ap.rearrange("p (a t n) -> p a t n", t=2, n=h)
            f = k.v_tt if lv < 2 else k.g_tt
            t1 = f(o[:, :, 0, :], v[:, :, 0, :], v[:, :, 1, :], ALU.add, t, nfree)
            t2 = f(o[:, :, 1, :], v[:, :, 0, :], v[:, :, 1, :], ALU.subtract, t)
            cur, nxt, t, nfree = nxt, cur, [t1, t2], None
        s["ha"], s["hb"], s["th"] = ha, hb, t

    def d(i):
        s, m = st[i], sm[:, i, :]
        ha, hb = s["ha"], s["hb"]
        t = k.v_red(m[:, 4:5], ha.ap, ALU.max, s["th"], absolute=True)
        t = k.v_ts(m[:, 4:5], m[:, 4:5], HN, 1e-5, ALU.mult, ALU.max, t)
        t = k.v_ts(m[:, 4:5], m[:, 4:5], 1.0 / 128, None, ALU.mult, None, t)
        t = k.v_recip(m[:, 5:6], m[:, 4:5], t)
        t1 = k.v_ts(m[:, 5:6], m[:, 5:6], HN, None, ALU.mult, None, t)
        tf = k.v_ts(m[:, 6:7], m[:, 4:5], sc[:, 2:3], None, ALU.mult, None, t)
        t = k.v_ts(ha.ap, ha.ap, m[:, 5:6], 127.0, ALU.mult, ALU.min, t1)
        t = k.v_ts(ha.ap, ha.ap, -128.0, MAGIC, ALU.max, ALU.add, t)
        yb = YB.take()
        t = k.v_ts(yb.ap, ha.ap, MAGIC, None, ALU.subtract, None, t, yb.free)
        ha.done(t)
        hb.done(t, s["th"])
        yt = YT.take()
        te = []
        for c in range(2):
            r = R.take()
            bb = r.ap.bitcast(BF16).rearrange("p (m n) -> p m n", m=8)
            for j in range(8):
                t1 = k.tr(bb[:, j, :], yb.ap[:, (8 * c + j) * P:(8 * c + j + 1) * P], r.free, t, sig=(j == 7))
            te.append(k.acopy(yt.ap[:, 8 * c:8 * c + 8, :], bb, t1, yt.free))
            r.done(te[-1])
        yb.done(t1)
        r = R.take()
        for j in range(16):
            t1 = k.mm(r.ap, yt.ap[:, j, :], WD[:, j, :], j == 0, j == 15, r.free, te, tw[2], sig=(j == 15))
        yt.done(t1)

        def add(z, *w):
            t2 = k.v_stt(z, r.ap, m[:, 6:7], k.X[:, i, :], ALU.mult, ALU.add, tf, *w, k.xtok[i])
            r.done(t2)
            return t2
        k.ln(i, add, t1)

    pipeline(NT, [(0, a), (1, b), (2, c), (3, d)])
    k.ln_flush()


def l1_attn(k):
    nc = k.nc
    k.phase("l1attn")
    k.off = k.base
    ins = k.ins
    xt_off = k.off
    XT = k.alloc([4, 2048])
    YT1, YT2 = k.alloc([2, 2048]), k.alloc([2, 2048])
    BD = k.alloc([2, 192])
    BP = k.alloc([2, 256])
    PM = k.alloc([P])
    CW = k.alloc([2, 4, 8])
    LB = k.alloc([3, 512])
    mark = k.off
    Q = Ring([k.alloc([8, 8, 24]) for _ in range(2)])
    PR = Ring([k.alloc([4096]) for _ in range(2)])
    S = Ring([k.alloc([8, 8, 8]) for _ in range(2)])
    AA = Ring([k.alloc([8, 8, 8])])
    A2 = Ring([k.alloc([8, 16, 8]) for _ in range(1)])
    LE = Ring([k.alloc([2, 8, 8, 8]) for _ in range(1)])
    mz = Ring([k.alloc([3, 64]) for _ in range(2)])
    tc = [k.dma(BD, ins["L1_bd"]), k.dma(BP, ins["L1_bp"]), k.dma(CW, ins["L1_cw"]), k.dma(LB, ins["L1_lb"])]
    R = Ring([k.bank(j)[:, 0, :] for j in range(4)])
    R4 = Ring([k.bank(4, 4)])
    SCL = float(8) ** -0.5

    tpm = k.dma(PM, ins["c_perm"])
    XV = XT.rearrange("p k (l r) -> p (k l) r", l=4)
    for i in range(NT):
        r = R.take()
        for c in range(4):
            t = k.mm(r.ap[:, c * P:c * P + P], k.X[:, i, c * P:c * P + P], PM, True, True, r.free, k.xtok[i], tpm,
                     sig=(c == 3))
        col = 256 * (i // 8) + 64 * (i // 4 % 2) + 16 * (i % 4)
        dst = XV[:, :, col:col + 144].rearrange("p m (h n) -> p m h n", n=16)[:, :, 0:9:8]
        src = r.ap.rearrange("p (m h n) -> p m h n", h=2, n=16)
        t = (k.acopy if i % 2 else k.v_copy)(dst, src, t)
        r.done(t)
    txt = [k.act.last, k.dve.last]

    def group(sset, il):
        return 4 * (il % 4) + 2 * sset + il // 4

    def window(q, tq, dst, br, n):
        s, pr, mm = S.take(), PR.take(), mz.take()
        pv = pr.ap.rearrange("p (w i j c) -> p w i j c", w=8, i=8, j=8)
        tp = []
        for w in range(8):
            a = q[:, w, :, 0:8].unsqueeze(2).to_broadcast([P, 8, 8, 8])
            b = q[:, w, :, 8:16].unsqueeze(1).to_broadcast([P, 8, 8, 8])
            tp.append((k.v_tt if w % 3 else k.g_tt)(pv[:, w], a, b, ALU.mult, tq, pr.free))
        sf = s.ap.rearrange("p w i j -> p (w i) j")
        t = k.v_red(s.ap.rearrange("p w i j -> p (w i j)"), pr.ap.rearrange("p (s c) -> p s c", c=8), ALU.add, tp, s.free)
        m, z, r = (mm.ap[:, j, :] for j in range(3))
        t = k.v_red(m, sf, ALU.max, t, mm.free)
        t = k.v_tt(sf, sf, m.unsqueeze(2).to_broadcast([P, 64, 8]), ALU.subtract, t)
        te = k.activ(sf, sf, ACT.Exp, t, scale=SCL)
        t = k.v_red(z, sf, ALU.add, te)
        tr = k.v_recip(r, z, t)
        pv = pr.ap.rearrange("p (w i c j) -> p w i c j", w=8, i=8, c=8)
        tp = []
        for w in range(8):
            a = s.ap[:, w].unsqueeze(2).to_broadcast([P, 8, 8, 8])
            b = q[:, w, :, 16:24].rearrange("p j c -> p c j").unsqueeze(1).to_broadcast([P, 8, 8, 8])
            tp.append((k.v_tt if w % 3 else k.g_tt)(pv[:, w], a, b, ALU.mult, te, t))
        s.done(tr, tp)
        aa = AA.take()
        t = k.v_red(aa.ap.rearrange("p w i c -> p (w i c)"), pr.ap.rearrange("p (s c) -> p s c", c=8), ALU.add, tp, aa.free)
        pr.done(t)
        t = k.v_tt(aa.ap.rearrange("p w i c -> p (w i) c"), aa.ap.rearrange("p w i c -> p (w i) c"),
                   r.unsqueeze(2).to_broadcast([P, 64, 8]), ALU.mult, t, tr)
        mm.done(t)
        le = LE.take()
        l0, l1 = le.ap[:, 0], le.ap[:, 1]
        v = q[:, :, :, 16:24]

        def cw(j, ni):
            return CW[:, br, j, :].unsqueeze(1).unsqueeze(1).to_broadcast([P, 1, ni, 8])

        tl = []
        for w in range(8):
            t1 = k.g_tt(l0[:, w:w + 1], v[:, w:w + 1], cw(1, 8), ALU.mult, tq, le.free, tc)
        g = t1
        tl = []
        for w in range(8):
            tl.append(k.g_tt(l1[:, w:w + 1, 1:8], v[:, w:w + 1, 0:7], cw(0, 7), ALU.mult, tq, le.free))
        t1 = k.g_tt(l0[:, :, 1:8], l0[:, :, 1:8], l1[:, :, 1:8], ALU.add, tl, g)
        tl = []
        for w in range(8):
            tl.append(k.g_tt(l1[:, w:w + 1, 0:7], v[:, w:w + 1, 1:8], cw(2, 7), ALU.mult, t1))
        t1 = k.g_tt(l0[:, :, 0:7], l0[:, :, 0:7], l1[:, :, 0:7], ALU.add, tl, t1)
        for w in range(8):
            t2 = k.g_tt(l1[:, w:w + 1], aa.ap[:, w:w + 1], cw(3, 8), ALU.add, t, t1)
        aa.done(t2)
        t3 = k.g_tt(dst, l0 if n is None else l0.rearrange("p w i c -> p i w c"),
                    l1 if n is None else l1.rearrange("p w i c -> p i w c"), ALU.add, t2, t1)
        le.done(t3)
        return t3

    ty = []
    for u in range(8):
        q = Q.take()
        tq = []
        for t2 in range(2):
            i = 2 * u + t2
            for c2 in range(2):
                r = R.take()
                for c in range(2):
                    t = k.mm(r.ap[:, 192 * c:192 * c + 192], XT[:, 2 * c2 + c, i * P:i * P + P], BD[:, 0, :], True, True,
                             r.free, txt, tc, sig=(c == 1))
                w0 = 4 * t2 + 2 * c2
                tq.append(k.acopy(q.ap[:, w0:w0 + 2], r.ap[:, 0:384].rearrange("p (w i c) -> p w i c", w=2, i=8), t, q.free))
                r.done(tq[-1])
        a2 = A2.take()
        dst = a2.ap.rearrange("p a b c -> p (a b c)")[:, 0:512].rearrange("p (w i c) -> p w i c", w=8, i=8)
        td = window(q.ap, tq, dst, 0, None)
        q.done(td, k.dve.last)
        for t2 in range(2):
            i = 2 * u + t2
            r = R.take()
            for h in range(2):
                t = k.tr(r.ap[:, h * P:h * P + P], a2.ap.rearrange("p a b c -> p (a b c)")[:, 256 * t2 + 128 * h:256 * t2 + 128 * h + 128],
                         r.free, td, sig=(h == 1))
            te = k.acopy(YT1[:, :, i * P:i * P + P], r.ap[:, 0:256].rearrange("p (h n) -> p h n", h=2), t)
            r.done(te)
            ty.append(te)
        a2.done(t)
    for sset in range(2):
        for half in range(2):
            a2 = A2.take()
            for c2 in range(2):
                c = 2 * half + c2
                q = Q.take()
                r = R4.take()
                tq = []
                for il in range(8):
                    gi = group(sset, il) * P
                    col = XT[:, c, gi:gi + P]
                    t = k.mm(r.ap[:, il // 2, 192 * (il % 2):192 * (il % 2) + 192], col, BD[:, 1, :], True, True,
                             r.free, txt, tc, sig=(il % 2 == 1))
                    if il % 2:
                        src = r.ap[:, il // 2, 0:384].rearrange("p (i w c) -> p w i c", i=2, w=8)
                        tq.append(k.acopy(q.ap[:, :, il - 1:il + 1, :].rearrange("p w i c -> p i w c"),
                                          src.rearrange("p w i c -> p i w c"), t, q.free))
                r.done(*tq)
                dst = a2.ap[:, :, 8 * c2:8 * c2 + 8, :]
                td = window(q.ap, tq, dst, 1, 1)
                q.done(td, k.dve.last)
            for q4 in range(2):
                r = R.take()
                for j in range(4):
                    il = 4 * q4 + j
                    t = k.tr(r.ap[:, j * P:j * P + P], a2.ap[:, il].rearrange("p w c -> p (w c)"), r.free, td, sig=(j == 3))
                gi = group(sset, 4 * q4) * P
                te = k.acopy(YT2[:, half, :].rearrange("p (l n) -> p l n", l=4)[:, :, gi:gi + P],
                             r.ap.rearrange("p (l n) -> p l n", l=4), t)
                ty.append(te)
                r.done(te)
            a2.done(t)
    k.off = mark
    start = [k.dve.last, k.act.last, k.pool.last, k.pe.last]
    TN = k.alloc([16, 16, 32])
    Y = Ring([k.alloc([512]) for _ in range(3)], start)
    Z = Ring([k.alloc([512]) for _ in range(3)], start)
    sm = Ring([k.alloc([4, 32]) for _ in range(3)], start)
    RB = Ring([k.bank(j, 2) for j in (0, 2, 4, 6)])
    for s in RB.free:
        s.extend(start)
    tn = []
    st = [dict() for _ in range(16)]

    def a(rl):
        s = st[rl]
        r = s["r"] = RB.take()
        c0 = 512 * (rl // 4) + rl % 4
        c1 = c0 + 509
        for h in range(2):
            o = r.ap[:, 0, 256 * h:256 * h + 256]
            k.mm(o, YT1[:, h, c0:c1:4], BP[:, 0, :], True, False, r.free, ty)
            t = k.mm(o, YT2[:, h, c0:c1:4], BP[:, 1, :], False, True, sig=(h == 1))
        for c in range(4):
            tt = k.tr(r.ap[:, 1, c * P:c * P + P], XT[:, c, c0:c1:4], sig=(c == 3))
        y, z, m = Y.take(), Z.take(), sm.take()
        s["y"], s["z"], s["m"] = y, z, m
        y3 = y.ap.rearrange("p (x c) -> p x c", c=16)
        z3 = z.ap.rearrange("p (x c) -> p x c", c=16)
        t = k.v_tt(y.ap, r.ap[:, 0, :], LB[:, 0, :], ALU.add, t, y.free)
        t = k.v_red(m.ap[:, 0, :], y3, ALU.add, t, m.free)
        t = k.v_ts(m.ap[:, 0, :], m.ap[:, 0, :], 1.0 / 16, None, ALU.mult, None, t)
        t = k.v_tt(y3, y3, m.ap[:, 0, :].unsqueeze(2).to_broadcast([P, 32, 16]), ALU.subtract, t)
        t = k.activ(z.ap, y.ap, ACT.Square, t, z.free)
        t = k.v_red(m.ap[:, 1, :], z3, ALU.add, t)
        t = k.g_ts(m.ap[:, 2, :], m.ap[:, 1, :], 1.0 / 16, 1e-5, ALU.mult, ALU.add, t)
        s["t"] = k.g_tt(m.ap[:, 3, :], m.ap[:, 2, :], k.nhalf, ALU.pow, t)
        s["tt"] = tt

    def b(rl):
        s = st[rl]
        y, z, m, r = s["y"], s["z"], s["m"], s["r"]
        y3 = y.ap.rearrange("p (x c) -> p x c", c=16)
        t = k.v_tt(y3, y3, m.ap[:, 3, :].unsqueeze(2).to_broadcast([P, 32, 16]), ALU.mult, s["t"])
        m.done(t)
        t = k.g_tt(y.ap, y.ap, LB[:, 1, :], ALU.mult, t)
        t = k.g_tt(z.ap, y.ap, LB[:, 2, :], ALU.add, t)
        y.done(t)
        t = k.v_tt(TN[:, :, rl, :].rearrange("p c x -> p x c"), z.ap.rearrange("p (x c) -> p x c", c=16),
                   r.ap[:, 1, :].rearrange("p (x c) -> p x c", c=16), ALU.add, t, s["tt"])
        z.done(t)
        r.done(t)
        tn.append(t)

    pipeline(16, [(0, a), (1, b)])
    OUT = k.view(xt_off, [NT, 512])
    td = []
    for p8 in range(8):
        sset, lh, b2 = p8 // 4, p8 // 2 % 2, p8 % 2
        bb = 2 * sset + b2
        for c4 in range(4):
            src = TN[16 * p8:16 * p8 + 16].rearrange("p (t c) r x -> p c t (r x)", c=4)[:, c4]
            p0 = 32 * c4 + lh
            td.append(k.dma(OUT[p0:p0 + 31:2, 4 * bb:4 * bb + 4, :], src, tn, k.pe.last))
    for i in range(NT):
        k.ln(i, k.add_from(i, OUT[:, i, :], None), td)
    k.ln_flush()


def l2_ffn(k):
    nc = k.nc
    k.phase("l2ffn")
    k.off = k.base
    ins = k.ins
    XT = k.alloc([4, 2048])
    Y = k.alloc([NT, 512])
    WR = k.alloc([4, 64])
    GU = Ring([k.alloc([4, 384]) for _ in range(3)])
    DN = Ring([k.alloc([2, 512]) for _ in range(3)])
    RW = k.alloc([NT, 64])
    R = Ring([k.bank(j)[:, 0, :] for j in range(8)])
    SG = Ring([k.alloc([192]) for _ in range(3)])
    HH = Ring([k.alloc([192]) for _ in range(3)])
    HT = Ring([k.alloc([2, P]) for _ in range(3)])
    sc = k.alloc([4, 64])
    sm = k.alloc([NT, 16])
    twr = k.dma(WR, rows(ins["L2_ffn_gate_weight"]))
    wg = ins["L2_ffn_gu"].rearrange("e (k p) n -> e p k n", p=P)
    wd = ins["L2_ffn_w_down"].rearrange("e (k p) n -> e p k n", p=96)

    def load(e):
        g, d = GU.take(), DN.take()
        return g, k.dma(g.ap, wg[e], g.free), d, k.dma(d.ap[0:96], wd[e], d.free)

    ld = {0: load(0), 1: load(1)}
    for i in range(NT):
        k.x_to_xt(i, R, XT[:, :, i * P:i * P + P], eng=i % 2)
        txt = [k.act.last, k.dve.last]
        r = R.take()
        for kk in range(4):
            t = k.mm(r.ap[:, 0:64], XT[:, kk, i * P:i * P + P], WR[:, kk, :], kk == 0, kk == 3, r.free, txt, twr, sig=(kk == 3))
        m = sm[:, i, :]
        t = k.v_red(m[:, 0:1], r.ap[:, 0:64], ALU.max, t, negate=True)
        t = k.activ(sc[:, 0, :], r.ap[:, 0:64], ACT.Exp, t, bias=m[:, 0:1], accum=m[:, 1:2])
        r.done(t)
        t = k.v_recip(m[:, 2:3], m[:, 1:2], t)
        t = k.v_ts(sc[:, 1, :], sc[:, 0, :], m[:, 2:3], None, ALU.mult, None, t)
        k.dve.wait(t)
        t = k.dve.sig(nc.vector.max(m[:, 3:11], sc[:, 1, :]))
        k.dve.wait(t)
        t = k.dve.sig(nc.vector.match_replace(sc[:, 2, :], m[:, 3:11], sc[:, 1, :], -1.0))
        t = k.v_red(m[:, 11:12], m[:, 3:11], ALU.add, t)
        t = k.v_recip(m[:, 12:13], m[:, 11:12], t)
        t = k.v_tt(sc[:, 3, :], sc[:, 2, :], sc[:, 1, :], ALU.not_equal, t)
        t = k.v_tt(sc[:, 3, :], sc[:, 3, :], sc[:, 1, :], ALU.mult, t)
        trw = k.v_ts(RW[:, i, :], sc[:, 3, :], m[:, 12:13], None, ALU.mult, None, t)
        k.act.wait(trw)
    st = {}

    def a(n):
        e, i = divmod(n, NT)
        if i == 0 and e + 2 < 64:
            ld[e + 2] = None
        g, tg, d, td = ld[e]
        r = R.take()
        for kk in range(4):
            t = k.mm(r.ap[:, 0:384], XT[:, kk, i * P:i * P + P], g.ap[:, kk, :], kk == 0, kk == 3, r.free, tg, txt, sig=(kk == 3))
        if i == NT - 1:
            g.done(t)
        s = SG.take()
        t1 = k.activ(s.ap, r.ap[:, 0:192], ACT.Silu, t, s.free)
        h = HH.take()
        t2 = k.v_stt(h.ap, r.ap[:, 192:384], RW[:, i, e:e + 1], s.ap, ALU.mult, ALU.mult, t1, h.free, trw)
        s.done(t2)
        r.done(t2)
        st[n] = [h, t2]

    def b(n):
        e, i = divmod(n, NT)
        h, t = st[n]
        r = R.take()
        for c in range(2):
            t1 = k.tr(r.ap[0:96, c * P:c * P + P], h.ap[:, 96 * c:96 * c + 96], r.free, t, sig=(c == 1))
        h.done(t1)
        ht = HT.take()
        t = k.acopy(ht.ap[0:96], r.ap[0:96, 0:256].rearrange("p (c n) -> p c n", c=2), t1, ht.free)
        r.done(t)
        st[n] = [ht, t]

    def c(n):
        e, i = divmod(n, NT)
        g, tg, d, td = ld[e]
        ht, t = st.pop(n)
        r = R.take()
        for c in range(2):
            t1 = k.mm(r.ap, ht.ap[0:96, c, :], d.ap[0:96, c, :], c == 0, c == 1, r.free, t, td, sig=(c == 1))
        ht.done(t1)
        if i == NT - 1:
            d.done(t1)
            if e + 3 < 64 or ld.get(e + 2, 1) is None:
                pass
        if e == 0:
            t2 = k.v_copy(Y[:, i, :], r.ap, t1)
        else:
            t2 = k.v_tt(Y[:, i, :], Y[:, i, :], r.ap, ALU.add, t1, ty[i])
        ty[i] = t2
        r.done(t2)
        if i == 4 and e + 2 < 64:
            ld[e + 2] = load(e + 2)

    ty = [None] * NT
    pipeline(64 * NT, [(0, a), (1, b), (2, c)])
    for i in range(NT):
        k.ln(i, k.add_from(i, Y[:, i, :], None), ty[i])
    k.ln_flush()


def layout_rest(a, d, T, rep, f):
    for n in ("L0_ffn_up_w", "L0_ffn_down_w", "L0_ffn_expert_weight", "L0_ffn_gate_w", "L3_attn_Wq"):
        d[n] = np.asarray(a[n])
    d["L0_ffn_ln"] = rep(np.stack([np.asarray(a["L0_ffn_ln_gamma"]), np.asarray(a["L0_ffn_ln_beta"])]), P, 2, 512)
    d["L3_ffn_w1"], d["L3_ffn_w2"] = T(a["L3_ffn_w1"]), T(a["L3_ffn_w2"])
    d["L3_ffn_b1"] = T(np.asarray(a["L3_ffn_b1"]).reshape(16, P))
    d["L3_ffn_b2"] = rep(a["L3_ffn_b2"], P, 512)
    for n in ("gate", "up", "down"):
        d["L1_ffn_w_" + n] = T(a["L1_ffn_w_" + n])
    h = np.ones((1, 1), f)
    while len(h) < P:
        h = np.block([[h, h], [h, -h]]).astype(f)
    d["c_hadamard"] = h
    sel = np.zeros((P, 4, P), f)
    for g in range(4):
        for r in range(3):
            for hg in range(4):
                sel[32 * g + 4 * r + hg, hg, :] = 1
    d["c_sel"] = sel
    for lab, names, tr in (("L2_attn", ("WQ", "WK", "WV", "WO"), True), ("L3_attn", ("q", "k", "v", "c"), False)):
        for n, o in zip(names, "qkvo"):
            w, b = (f"{lab}_{n}_w", f"{lab}_{n}_b") if tr else (f"{lab}_W{n}", f"{lab}_b{n}")
            d[f"{lab}_{o}"] = T(a[w]) if tr else np.asarray(a[w])
            d[f"{lab}_b{o}"] = T(np.asarray(a[b]).reshape(4, P)) if o in "qk" else rep(a[b], P, 512)
    d["L2_xattn_q"], d["L2_xattn_o"] = T(a["L2_xattn_Wq"]), T(a["L2_xattn_Wout"])
    kv = T(a["L2_xattn_Wkv_expand"])
    d["L2_xattn_k"], d["L2_xattn_v"] = kv[:, :512], kv[:, 512:]
    d["ctx_T"] = np.ascontiguousarray(np.asarray(a["ctx_512"]).transpose(2, 0, 1))
    d["L3_xattn_W_k"] = T(a["L3_xattn_W_k"])
    d["L3_xattn_b_k"] = np.asarray(a["L3_xattn_b_k"]).reshape(P, 1)
    d["L3_xattn_ln"] = rep(np.stack([np.asarray(a["L3_xattn_ln_gamma"]), np.asarray(a["L3_xattn_ln_beta"])]), P, 2, 512)
    d["L1_xattn_W"] = np.stack([T(a["L1_xattn_Wq"]), T(a["L1_xattn_Wk"])], 1)
    pm = np.zeros((P, P), f)
    q = np.arange(P)
    pm[q, 32 * (q // 4 % 4) + 16 * (q // 16 % 2) + 4 * (q // 32) + q % 4] = 1
    d["c_perm"] = pm
    d["L1_gamma"] = rep(np.asarray(a["L1_xattn_gamma_raw"]).reshape(1, 1), P, 1)
    w = np.asarray(a["L1_attn_qkv_w"])
    bd = np.zeros((8, 16, 2, 8, 24), f)
    pw = np.asarray(a["L1_attn_proj_w"])
    bp = np.zeros((16, 8, 2, 16, 16), f)
    for br in range(2):
        for x in range(8):
            for j in range(3):
                bd[x, :, br, x, 8 * j:8 * j + 8] = w[:, 16 * j + 8 * br:16 * j + 8 * br + 8]
        for x in range(16):
            bp[x, :, br, x, :] = pw[8 * br:8 * br + 8]
    d["L1_bd"] = bd.reshape(P, 2, 192)
    d["L1_bp"] = bp.reshape(P, 2, 256)
    c0, c1 = np.asarray(a["L1_attn_conv_w0"])[:, 0], np.asarray(a["L1_attn_conv_w1"])[:, 0]
    cw = np.stack([np.stack([c0[:, 1, 0], c0[:, 1, 1], c0[:, 1, 2], np.asarray(a["L1_attn_conv_b0"])]),
                   np.stack([c1[:, 0, 1], c1[:, 1, 1], c1[:, 2, 1], np.asarray(a["L1_attn_conv_b1"])])])
    d["L1_cw"] = rep(cw, P, 2, 4, 8)
    lb = np.stack([np.tile(np.asarray(a["L1_attn_" + n]), 32) for n in ("proj_b", "ln_w", "ln_b")])
    d["L1_lb"] = rep(lb, P, 3, 512)
    d["L2_ffn_gate_weight"] = T(a["L2_ffn_gate_weight"])
    d["L2_ffn_gu"] = np.concatenate([np.asarray(a["L2_ffn_w_gate"]), np.asarray(a["L2_ffn_w_up"])], axis=2)
    d["L2_ffn_w_down"] = np.asarray(a["L2_ffn_w_down"])
    for n in ("L3_attn_Wq",):
        d.pop(n)
def build(nc, ins, out, layers):
    k = K(nc, ins, out)
    k.start()
    table = [l0_attn, l0_xattn, l0_ffn, l1_attn, l1_xattn, l1_ffn, l2_attn, l2_xattn, l2_ffn,
             l3_attn, l3_xattn, l3_ffn]
    for n in layers:
        table[n](k)
    o = out.rearrange("b (t p) d -> p (b t) d", p=P)
    ts = [k.dma(o[:, 4 * b:4 * b + 4, :], k.X[:, 4 * b:4 * b + 4, :], k.xtok) for b in range(4)]
    k.sp.wait(ts)


def layout(a):
    f = np.float32

    def T(x):
        return np.ascontiguousarray(np.asarray(x).T)

    def rep(x, *shape):
        return np.ascontiguousarray(np.broadcast_to(np.asarray(x), shape))

    d = {}
    d["x"] = np.asarray(a["x"])
    d["ctx_512"] = np.asarray(a["ctx_512"])
    ident = np.eye(P, dtype=f)
    i, j = np.arange(P)[None, :], np.arange(P)[:, None]
    d["c_ident"] = ident
    d["c_masks"] = np.stack([ident, np.where(i > j, f(NEG), f(0)), np.where(j > i, f(NEG), f(0))], 1).astype(f)
    d["c_iota"] = np.stack([i + 1 + 0 * j, np.where(i >= j, i - j, 1e30), 127 - j + 0 * i], 1).astype(f)
    d["c_block"] = (i // 32 == j // 32).astype(f)
    s = np.asarray(a["L0_attn_slope_rate"]).reshape(16)
    d["slope_k"] = rep(s, P, 16)
    d["slope_q"] = np.ascontiguousarray(np.repeat(s.reshape(4, 4).T, 32, axis=0))
    for n in ("L0_attn_W_qkvu", "L0_attn_W_out"):
        d[n] = T(a[n])
    layout_rest(a, d, T, rep, f)
    return d


def kernel(**inputs):
    import concourse.bacc as _bacc
    from concourse.bass_utils import run_bass_kernel_spmd as _run

    nc = _bacc.Bacc("TRN2", target_bir_lowering=False, num_devices=1)
    arrays, ins = {}, {}
    for name, v in layout(inputs).items():
        v = np.ascontiguousarray(v)
        arrays[f"in_{name}"] = v
        ins[name] = nc.dram_tensor(f"in_{name}", v.shape, mybir.dt.from_np(v.dtype), kind="ExternalInput").ap()
    out = nc.dram_tensor("out_0", (4, 512, 512), F32, kind="ExternalOutput").ap()
    build(nc, ins, out, range(12))
    r = _run(nc, [arrays], core_ids=[0])
    return r.results[0]["out_0"]
```

```python
import numpy as np
import concourse.bass as bass
from concourse import mybir

F32 = mybir.dt.float32
BF16 = mybir.dt.bfloat16
U32 = mybir.dt.uint32
I32 = mybir.dt.int32
ALU = mybir.AluOpType
ACT = mybir.ActivationFunctionType
AX = mybir.AxisListType
P = 128
NT = 16
D = 512
NEG = -1.0e30


class Eng:

    def __init__(self, nc, name, eng):
        self.nc, self.name, self.eng = nc, name, eng
        self.seen = {}
        self.last = None

    def phase(self, label):
        self.sem = self.nc.alloc_semaphore(f"{self.name}_{label}")
        self.count = 0

    def wait(self, *toks):
        for t in toks:
            if t is None:
                continue
            if isinstance(t, list):
                self.wait(*t)
                continue
            sem, val = t
            if self.seen.get(sem.name, 0) >= val:
                continue
            self.seen[sem.name] = val
            self.eng.wait_ge(sem, val)

    def sig(self, ins):
        ins.then_inc(self.sem, 1)
        self.count += 1
        self.last = (self.sem, self.count)
        return self.last


class Slot:
    def __init__(self, ring, i, ap, free):
        self.ring, self.i, self.ap, self.free = ring, i, ap, free

    def done(self, *toks):
        self.ring.free[self.i] = list(toks)
        self.ring.held[self.i] = False


class Ring:

    def __init__(self, bufs, free=None):
        self.bufs, self.n = bufs, 0
        self.free = [list(free or []) for _ in bufs]
        self.held = [False for _ in bufs]

    def take(self):
        i = self.n % len(self.bufs)
        self.n += 1
        assert not self.held[i], "a buffer is taken before its last user is named"
        self.held[i] = True
        return Slot(self, i, self.bufs[i], self.free[i])


class K:
    def __init__(self, nc, ins, out):
        self.nc, self.ins, self.out = nc, ins, out
        self.pe = Eng(nc, "pe", nc.tensor)
        self.act = Eng(nc, "act", nc.scalar)
        self.dve = Eng(nc, "dve", nc.vector)
        self.pool = Eng(nc, "pool", nc.gpsimd)
        self.sp = Eng(nc, "sp", nc.sync)
        self.NDS = 24
        self.dsem = [nc.alloc_semaphore(f"dma{i}") for i in range(self.NDS)]
        self.dcount = [0] * self.NDS
        self.dn = 0
        self.W = 51800
        self.arena = nc.alloc_sbuf_tensor("arena", [P, self.W], F32)
        self.ps = nc.alloc_psum_tensor("ps", [P, 8, 512], F32)
        self.off = 0
        self.fence_toks = []

    def alloc(self, shape, dt=F32):
        n = int(np.prod(shape))
        words = (n + 1) // 2 if dt == BF16 else n
        o = self.off
        self.off += words
        assert self.off <= self.W, f"sbuf {self.off}"
        return self.view(o, shape, dt)

    def view(self, o, shape, dt=F32):
        n = int(np.prod(shape))
        words = n if dt != BF16 else n // 2
        a = self.arena[:, o:o + words]
        if dt != F32:
            a = a.bitcast(dt)
        if len(shape) > 1:
            names = "abcde"[:len(shape)]
            kw = {names[i]: shape[i] for i in range(1, len(shape))}
            a = a.rearrange(f"p ({' '.join(names)}) -> p {' '.join(names)}", **kw)
        return a

    def bank(self, i, n=1):
        return self.ps[:, i:i + n, :]

    def phase(self, label):
        toks = [e.last for e in (self.pe, self.act, self.dve, self.pool) if e.last]
        for i in range(self.NDS):
            if self.dcount[i]:
                toks.append((self.dsem[i], 16 * self.dcount[i]))
        for e in (self.pe, self.act, self.dve, self.pool, self.sp):
            e.wait(*toks)
        for e in (self.pe, self.act, self.dve, self.pool):
            e.phase(label)

    def dma(self, out, in_, *w, eng=None):
        eng = eng or self.sp
        i = self.dn % self.NDS
        self.dn += 1
        if self.dcount[i]:
            eng.wait((self.dsem[i], 16 * self.dcount[i]))
        eng.wait(*w)
        eng.eng.dma_start(out, in_).then_inc(self.dsem[i], 16)
        self.dcount[i] += 1
        return (self.dsem[i], 16 * self.dcount[i])

    def mm(self, out, lhsT, rhs, start, stop, *w, sig=False, skip=True):
        self.pe.wait(*w)
        i = self.nc.tensor.matmul(out, lhsT, rhs, start=start, stop=stop, skip_group_check=skip)
        return self.pe.sig(i) if sig else None

    def tr(self, out, in_, *w, sig=False):
        self.pe.wait(*w)
        ident = self.idb if in_.dtype == BF16 else self.idf
        n = in_.shape[0]
        i = self.nc.tensor.transpose(out, in_, ident[0:n, 0:n])
        return self.pe.sig(i) if sig else None

    def activ(self, out, in_, func, *w, bias=None, scale=1.0, accum=None):
        self.act.wait(*w)
        kw = {}
        if bias is not None:
            kw["bias"] = bias
        if accum is not None:
            kw["accum_out"] = accum
        return self.act.sig(self.nc.scalar.activation(out, in_, func, scale=scale, **kw))

    def acopy(self, out, in_, *w):
        return self.activ(out, in_, ACT.Copy, *w)

    def v_copy(self, out, in_, *w):
        self.dve.wait(*w)
        return self.dve.sig(self.nc.vector.tensor_copy(out, in_))

    def v_tt(self, out, a, b, op, *w):
        self.dve.wait(*w)
        return self.dve.sig(self.nc.vector.tensor_tensor(out, a, b, op))

    def v_ts(self, out, a, s1, s2, op0, op1, *w, accum=None):
        self.dve.wait(*w)
        kw = {"accum_out": accum} if accum is not None else {}
        if op1 is None:
            return self.dve.sig(self.nc.vector.tensor_scalar(out, a, s1, None, op0))
        return self.dve.sig(self.nc.vector.tensor_scalar(out, a, s1, s2, op0, op1, **kw))

    def v_stt(self, out, a, s, b, op0, op1, *w):
        self.dve.wait(*w)
        return self.dve.sig(self.nc.vector.scalar_tensor_tensor(out=out, in0=a, scalar=s, in1=b, op0=op0, op1=op1))

    def v_red(self, out, a, op, *w, negate=False, absolute=False):
        self.dve.wait(*w)
        return self.dve.sig(self.nc.vector.tensor_reduce(out, a, AX.X, op, negate=negate,
                                                         apply_absolute_value=absolute))

    def v_recip(self, out, a, *w):
        self.dve.wait(*w)
        return self.dve.sig(self.nc.vector.reciprocal(out, a))

    def g_tt(self, out, a, b, op, *w):
        self.pool.wait(*w)
        return self.pool.sig(self.nc.gpsimd.tensor_tensor(out, a, b, op))

    def g_ts(self, out, a, s1, s2, op0, op1, *w):
        self.pool.wait(*w)
        if op1 is None:
            return self.pool.sig(self.nc.gpsimd.tensor_scalar(out, a, s1, None, op0))
        return self.pool.sig(self.nc.gpsimd.tensor_scalar(out, a, s1, s2, op0, op1))

    def g_copy(self, out, a, *w):
        self.pool.wait(*w)
        return self.pool.sig(self.nc.gpsimd.tensor_copy(out, a))

    def start(self):
        nc = self.nc
        self.X = self.alloc([NT, D])
        self.idf = self.alloc([P])
        self.idb = self.alloc([P], BF16)
        self.mq = self.alloc([P], BF16)
        self.mk = self.alloc([P], BF16)
        self.nhalf = self.alloc([32])
        self.st = self.alloc([4, 8])
        self.mv = self.alloc([4, 4])
        self.zb = Ring([self.alloc([D]) for _ in range(4)])
        self.base = self.off
        for e in (self.pe, self.act, self.dve, self.pool, self.sp):
            e.phase("start")
        c = self.ins["c_masks"]
        tc = [self.dma(self.idf, self.ins["c_ident"])]
        tmp = self.view(self.base, [3, P])
        t = self.dma(tmp, c)
        tc.append(self.v_copy(self.idb, tmp[:, 0, :], t))
        tc.append(self.v_copy(self.mq, tmp[:, 1, :], t))
        tc.append(self.v_copy(self.mk, tmp[:, 2, :], t))
        self.pool.wait()
        tc.append(self.pool.sig(nc.gpsimd.memset(self.nhalf, -0.5)))
        tx = self.dma(self.X, self.ins["x"].rearrange("b (t p) d -> p (b t) d", p=P))
        self.xtok = [tx] * NT
        self.ln_n = 0
        self.ln_pending = []

    def ln_begin(self, i, add, *w):
        s = self.zb.take()
        n = self.ln_n % 4
        self.ln_n += 1
        tz = add(s.ap, *w, s.free)
        self.dve.wait(tz)
        tb = self.dve.sig(self.nc.vector.bn_stats(self.st[:, n, 0:6], s.ap))
        self.dve.wait(tb)
        ta = self.dve.sig(self.nc.vector.bn_aggr(self.mv[:, n, 0:2], self.st[:, n, 0:6]))
        t1 = self.g_ts(self.mv[:, n, 2:3], self.mv[:, n, 1:2], 1e-5, 1.0, ALU.add, ALU.mult, ta)
        t2 = self.g_tt(self.mv[:, n, 3:4], self.mv[:, n, 2:3], self.nhalf[:, 0:1], ALU.pow, t1)
        self.ln_pending.append((i, s, n, t2))

    def ln_end(self):
        i, s, n, t2 = self.ln_pending.pop(0)
        t = self.v_ts(self.X[:, i, :], s.ap, self.mv[:, n, 0:1], self.mv[:, n, 3:4],
                      ALU.subtract, ALU.mult, t2)
        s.done(t)
        self.xtok[i] = t
        return t

    def ln(self, i, add, *w, lag=1):
        self.ln_begin(i, add, *w)
        while len(self.ln_pending) > lag:
            self.ln_end()

    def ln_flush(self):
        while self.ln_pending:
            self.ln_end()

    def add_from(self, i, src, slot, *w):
        def add(z, *ww):
            t = self.v_tt(z, self.X[:, i, :], src, ALU.add, *ww, self.xtok[i])
            if slot is not None:
                slot.done(t)
            return t
        return add

    def x_to_xt(self, i, ring, dst, *w, eng=0):
        s = ring.take()
        b = s.ap.rearrange("p (k n) -> p k n", k=4)
        for k in range(4):
            t = self.tr(b[:, k, :], self.X[:, i, k * P:(k + 1) * P], s.free, self.xtok[i], sig=(k == 3))
        t = self.acopy(dst, b, t, *w) if eng == 0 else self.v_copy(dst, b, t, *w)
        s.done(t)
        return t


def pipeline(n, stages):
    top = max(lag for lag, _ in stages)
    for t in range(n + top):
        for lag, f in sorted(stages, key=lambda s: -s[0]):
            if 0 <= t - lag < n:
                f(t - lag)
def l0_attn(k):
    nc = k.nc
    k.phase("l0attn")
    k.off = k.base
    WQ = k.alloc([4, 2048])
    WO = k.alloc([4, 512])
    tw = [k.dma(WQ[:, :, 512 * j:512 * j + 512],
                k.ins["L0_attn_W_qkvu"].rearrange("(k p) n -> p k n", p=P)[:, :, 512 * j:512 * j + 512])
          for j in range(4)]
    two = k.dma(WO, k.ins["L0_attn_W_out"].rearrange("(k p) n -> p k n", p=P))
    SQ = k.alloc([4])
    SK = k.alloc([16])
    IO = k.alloc([3, P])
    DT = k.alloc([16, P])
    QD = k.alloc([4, P])
    KD = k.alloc([512])
    KD16 = k.alloc([16])
    EB = k.alloc([4, P])
    BM = k.alloc([P])
    eb1 = k.alloc([4])
    ts = [k.dma(SQ, k.ins["slope_q"]), k.dma(SK, k.ins["slope_k"]), k.dma(IO, k.ins["c_iota"]),
          k.dma(BM, k.ins["c_block"])]
    for h in range(16):
        td = k.v_ts(DT[:, h, :], IO[:, 1, :], SK[:, h:h + 1], -1.0, ALU.mult, ALU.mult, ts)
    for hg in range(4):
        td = k.v_ts(QD[:, hg, :], IO[:, 0, :], SQ[:, hg:hg + 1], -1.0, ALU.mult, ALU.mult)
    td = k.v_ts(KD16, SK, IO[:, 2, 0:1], -1.0, ALU.mult, ALU.mult)
    td = k.v_ts(eb1, SQ, -128.0, None, ALU.mult, None)
    t1 = k.activ(DT, DT, ACT.Exp, td)
    t2 = k.activ(QD, QD, ACT.Exp)
    t3 = k.activ(KD16, KD16, ACT.Exp)
    t4 = k.activ(eb1, eb1, ACT.Exp)
    t5 = k.v_copy(KD.rearrange("p (h d) -> p h d", d=32), KD16.unsqueeze(2).to_broadcast([P, 16, 32]), t3, td)
    for hg in range(4):
        t6 = k.v_ts(EB[:, hg, :], BM, eb1[:, hg:hg + 1], None, ALU.mult, None, t4, td)
    dec = [t1, t2, t5, t6]

    R = Ring([k.bank(j)[:, 0, :] for j in range(3)])
    S4 = Ring([k.bank(3 + j)[:, 0, :] for j in range(4)])
    OB = Ring([k.bank(7)[:, 0, :]])
    XT = Ring([k.alloc([4, P]) for _ in range(2)])
    Qr, Kr = (Ring([k.alloc([512]) for _ in range(1)]) for _ in range(2))
    Vr, Ur = (Ring([k.alloc([512]) for _ in range(3)]) for _ in range(2))
    QTr = Ring([k.alloc([4, 4, P]) for _ in range(2)])
    KTr = Ring([k.alloc([4, P]) for _ in range(2)])
    for b in QTr.bufs:
        k.pool.wait(k.pool.last)
        tqz = k.pool.sig(nc.gpsimd.memset(b, 0.0))
    QSr, KSr = (Ring([k.alloc([4, P]) for _ in range(3)]) for _ in range(2))
    PTr = Ring([k.alloc([16, P])])
    OTr = Ring([k.alloc([4, P]) for _ in range(2)])
    ONr = Ring([k.alloc([512]) for _ in range(2)])
    KV = k.alloc([4, P])
    KVt = k.alloc([4, P])
    rs = k.alloc([NT, 4])
    st = [dict() for _ in range(NT)]
    state = {"kv": None, "rd": None}

    def a0(i):
        s = st[i]
        s["xt"] = XT.take()
        s["txt"] = k.x_to_xt(i, R, s["xt"].ap, s["xt"].free, eng=i % 2)

    def a(i):
        s = st[i]
        for j, (name, ring) in enumerate((("q", Qr), ("k", Kr), ("v", Vr), ("u", Ur))):
            b = R.take()
            o = s[name] = ring.take()
            for kk in range(4):
                t = k.mm(b.ap, s["xt"].ap[:, kk, :], WQ[:, kk, 512 * j:512 * j + 512], kk == 0, kk == 3,
                         b.free, s["txt"], tw[j], sig=(kk == 3))
            if j < 2:
                t = k.activ(o.ap, b.ap, ACT.Silu, t, o.free)
            elif j == 2:
                t = k.v_copy(o.ap, b.ap, t, o.free)
            else:
                t = k.acopy(o.ap, b.ap, t, o.free)
            b.done(t)
            s["t" + name] = t
        s["xt"].done(k.pe.last)

    def b(i):
        s = st[i]
        for name, src, tsrc, ring in (("qt", s["q"], s["tq"], QTr), ("kt", s["k"], s["tk"], KTr)):
            bk = R.take()
            bb = bk.ap.rearrange("p (k n) -> p k n", k=4)
            o = s[name] = ring.take()
            for kk in range(4):
                t = k.tr(bb[:, kk, :], src.ap[:, kk * P:kk * P + P], bk.free, tsrc, sig=(kk == 3))
            if name == "qt":
                t = [(k.v_copy if g % 2 else k.acopy)(o.ap[32 * g:32 * g + 32, g], bb[32 * g:32 * g + 32], t, o.free, tqz)
                     for g in range(4)] + [tqz]
                s["qs"] = QSr.take()
                s["tqs"] = k.v_tt(s["qs"].ap, bb, QD, ALU.mult, t, s["qs"].free, dec)
                t.append(s["tqs"])
            else:
                t = [k.acopy(o.ap, bb, t, o.free)]
            bk.done(*t)
            s["t" + name] = t
            if name == "qt":
                s["q"].done(k.pe.last)
            else:
                tkt = k.pe.last
        o = s["ks"] = KSr.take()
        s["tks"] = k.g_tt(o.ap.rearrange("p a b -> p (a b)"), s["k"].ap, KD, ALU.mult, s["tk"], o.free, dec)
        s["k"].done(s["tks"], tkt)

    def c(i):
        s = st[i]
        first = i % 4 == 0
        pt = s["pt"] = PTr.take()
        banks = [S4.take() for _ in range(4)]
        for g in range(4):
            bb = banks[g].ap.rearrange("p (k n) -> p k n", k=4)
            for hg in range(4):
                t = k.mm(bb[:, hg, :], s["kt"].ap[:, hg, :], s["qt"].ap[:, g, hg, :],
                         True, True, banks[g].free, s["tqt"], s["tkt"], sig=(hg == 3))
            dv = DT.rearrange("p (hg g) n -> p g hg n", g=4)[:, g]
            pv = pt.ap.rearrange("p (hg g) n -> p g hg n", g=4)[:, g]
            t = k.v_tt(pv, bb, dv, ALU.mult, t, pt.free, dec)
            banks[g].done(t)
        s["tpt"] = t
        s["qt"].done(k.pe.last, s["tqs"])
        s["kt"].done(k.pe.last)

    def kvup(i):
        s = st[i]
        if i % 4 == 3:
            s["ks"].done(s["tks"])
            return
        bk = R.take()
        bb = bk.ap.rearrange("p (k n) -> p k n", k=4)
        for hg in range(4):
            t = k.mm(bb[:, hg, :], s["ks"].ap[:, hg, :], s["v"].ap[:, hg * P:hg * P + P], True, True,
                     bk.free, s["tks"], s["tv"], sig=(hg == 3))
        s["ks"].done(t)
        bm = BM.unsqueeze(1).to_broadcast([P, 4, P])
        if i % 4 == 0:
            t = t0 = k.v_tt(KV, bb, bm, ALU.mult, t, state["rd"])
        else:
            t0 = k.v_tt(KVt, bb, bm, ALU.mult, t, state["kv"])
            t1 = k.v_tt(KV, KV, EB, ALU.mult, state["kv"], state["rd"], t0)
            t = k.v_tt(KV, KV, KVt, ALU.add, t1)
        bk.done(t0)
        state["kv"] = t

    def dd(i):
        s = st[i]
        ob = OB.take()
        if i % 4:
            for hg in range(4):
                k.mm(ob.ap[:, hg * P:hg * P + P], s["qs"].ap[:, hg, :], KV[:, hg, :], hg == 0, False,
                     ob.free, s["tqs"], state["kv"], sig=(hg == 3))
            state["rd"] = k.pe.last
        kvup(i)
        s["qs"].done(k.pe.last, s["tqs"])
        for h in range(16):
            t = k.mm(ob.ap[:, h * 32:h * 32 + 32], s["pt"].ap[:, h, :], s["v"].ap[:, h * 32:h * 32 + 32],
                     i % 4 == 0 and h == 0, h == 15, ob.free, s["tpt"], s["tv"], sig=(h == 15))
        s["pt"].done(t)
        s["v"].done(t)
        on = s["on"] = ONr.take()
        t1 = k.activ(on.ap, ob.ap, ACT.Square, t, on.free, accum=rs[:, i, 0:1])
        t2 = k.g_ts(rs[:, i, 1:2], rs[:, i, 0:1], 1.0 / 512, 1e-6, ALU.mult, ALU.add, t1)
        t3 = k.g_tt(rs[:, i, 2:3], rs[:, i, 1:2], k.nhalf[:, 0:1], ALU.pow, t2)
        t4 = k.v_stt(on.ap, ob.ap, rs[:, i, 2:3], s["u"].ap, ALU.mult, ALU.mult, t3, s["tu"], t1)
        s["u"].done(t4)
        ob.done(t4)
        s["ton"] = t4

    def e(i):
        s = st[i]
        bk = R.take()
        bb = bk.ap.rearrange("p (k n) -> p k n", k=4)
        for kk in range(4):
            t = k.tr(bb[:, kk, :], s["on"].ap[:, kk * P:kk * P + P], bk.free, s["ton"], sig=(kk == 3))
        s["on"].done(t)
        ot = OTr.take()
        t = k.acopy(ot.ap, bb, t, ot.free)
        bk.done(t)
        b2 = R.take()
        for kk in range(4):
            t2 = k.mm(b2.ap, ot.ap[:, kk, :], WO[:, kk, :], kk == 0, kk == 3, b2.free, t, two, sig=(kk == 3))
        ot.done(t2)
        k.ln(i, k.add_from(i, b2.ap, b2), t2)

    pipeline(NT, [(0, a0), (1, a), (2, b), (3, c), (4, dd), (5, e)])
    k.ln_flush()


def split3(k, parts, x, res, *w):
    t = k.v_copy(parts[0], x, *w)
    t = k.v_tt(res, x, parts[0], ALU.subtract, t, *w)
    t = k.v_copy(parts[1], res, t)
    t = k.v_tt(res, res, parts[1], ALU.subtract, t)
    return k.v_copy(parts[2], res, t)


def l0_xattn(k):
    nc = k.nc
    k.phase("l0xattn")
    k.off = k.base
    CX = k.alloc([NT, P])
    tcx = [k.dma(CX[:, 4 * b:4 * b + 4, :], k.ins["ctx_512"][b].rearrange("(t p) d -> p t d", p=P)) for b in range(4)]
    KS = Ring([k.alloc([8, 512], BF16) for _ in range(2)])
    VA = Ring([k.alloc([4, 8, 32]) for _ in range(2)])
    kst = [k.alloc([8, P], BF16) for _ in range(1)]
    kres = k.alloc([P])
    qst = Ring([k.alloc([32, 96], BF16) for _ in range(1)])
    qsc = k.alloc([512])
    qres = k.alloc([512])
    QS = Ring([k.alloc([32, P], BF16) for _ in range(3)])
    MX = k.alloc([2, 32])
    mres = k.alloc([32])
    ms = k.alloc([96], BF16)
    MT = Ring([k.alloc([P], BF16) for _ in range(2)])
    PT = Ring([k.alloc([4, 4, P]) for _ in range(3)])
    OT = Ring([k.alloc([4, P]) for _ in range(2)])
    rz = k.alloc([2, 32])
    oa = Ring([k.alloc([512]) for _ in range(2)])
    S1 = Ring([k.bank(0, 2), k.bank(2, 2)])
    S2 = Ring([k.bank(4)[:, 0, :], k.bank(5)[:, 0, :]])
    OB = Ring([k.bank(6)[:, 0, :], k.bank(7)[:, 0, :]])
    st = [dict() for _ in range(NT)]
    kb = [dict() for _ in range(4)]
    KORD = (0, 1, 0, 1, 2, 0)
    QORD = (0, 0, 1, 1, 0, 2)
    k.tkst = None

    for buf in VA.bufs:
        k.pool.wait()
        tva = k.pool.sig(nc.gpsimd.memset(buf[:, :, :, 16:32], 1.0))
    tks0 = k.pool.sig(nc.gpsimd.memset(kst[0][:, :, 96:128], 0.0))
    k.pool.wait(tks0)
    tks0 = k.pool.sig(nc.gpsimd.memset(kst[0][:, :, 96:99], 1.0))
    k.tkst = [tks0]
    for buf in QS.bufs:
        k.pool.wait(k.pool.last)
        tqz = k.pool.sig(nc.gpsimd.memset(buf[96:128, :, :], 0.0))
    k.pool.wait(tqz)

    def prep(b, t4):
        s = kb[b]
        if t4 == 0:
            s["ks"] = KS.take()
            s["va"] = VA.take()
            s["tk"] = [None] * 4
            s["tv"] = [None] * 4
        src = CX[:, 4 * b + t4, :].rearrange("p (h d) -> p h d", d=16)
        va = s["va"].ap
        s["tv"][t4] = k.g_copy(va[:, t4, :, 0:16], src, tcx, s["va"].free)
        s["tva"] = tva
        buf = kst[0]
        kv = buf[:, :, 0:96].rearrange("p h (r d) -> p h r d", d=16)
        part = [kv[:, :, 0, :], kv[:, :, 1, :], kv[:, :, 4, :]]
        rr = kres.rearrange("p (h d) -> p h d", d=16)
        t = split3(k, part, src, rr, tcx, k.tkst, tks0)
        ta = k.g_copy(kv[:, :, 2, :], kv[:, :, 0, :], t)
        tb = k.g_copy(kv[:, :, 3, :], kv[:, :, 1, :])
        tc = k.g_copy(kv[:, :, 5, :], kv[:, :, 0, :])
        s1 = S1.take()
        bb = s1.ap[:, 0, :].bitcast(BF16).rearrange("p (h n) -> p h n", n=P)
        for h in range(8):
            t = k.tr(bb[:, h, :], buf[:, h, :], s1.free, tc, ta, tb, sig=(h == 7))
        k.tkst = [t]
        t = k.acopy(s["ks"].ap[:, :, t4 * P:t4 * P + P], bb, t, s["ks"].free)
        s1.done(t)
        s["tk"][t4] = t

    def qsplit(i):
        s = st[i]
        sc = qsc.rearrange("p (h d) -> p h d", d=16)
        b = s["qst"] = qst.take()
        qv = b.ap.rearrange("p h (r d) -> p h r d", d=16)
        t0 = k.v_ts(qsc, k.X[:, i, :], 0.25, None, ALU.mult, None, k.xtok[i], k.dve.last)
        rr = qres.rearrange("p (h d) -> p h d", d=16)
        t = split3(k, [qv[:, :, 0, :], qv[:, :, 2, :], qv[:, :, 5, :]], sc, rr, t0, b.free)
        for dst, src in ((1, 0), (3, 2), (4, 0)):
            t = k.g_copy(qv[:, :, dst, :], qv[:, :, src, :], t)
        s["tqv"] = t

    def qt(i, h4):
        s = st[i]
        if h4 == 0:
            s["q"] = QS.take()
            s["tq"] = []
        q, b = s["q"], s["qst"]
        s1 = S1.take()
        for j in range(2):
            bb = s1.ap[:, j, :].bitcast(BF16).rearrange("p (h n) -> p h n", n=P)
            for h in range(8):
                t1 = k.tr(bb[0:96, h, :], b.ap[:, 16 * h4 + 8 * j + h, :], s1.free, s["tqv"], sig=(h == 7))
            dst = q.ap[0:96, 16 * h4 + 8 * j:16 * h4 + 8 * j + 8, :]
            te = k.acopy(dst, bb[0:96], t1, q.free)
            s["tq"].append(te)
        s1.done(te)
        if h4 == 1:
            b.done(t1)

    def first(i, j):
        s = st[i]
        s1 = S1.take()
        for u in range(2):
            h = 2 * j + u
            t = k.mm(s1.ap[:, u, :], s["q"].ap[0:96, h, :], kb[i // 4]["ks"].ap[0:96, h // 4, :], True, True,
                     s1.free, s["tq"], kb[i // 4]["tk"], sig=(u == 1))
        t = k.v_red(MX[:, i % 2, 2 * j:2 * j + 2], s1.ap, ALU.max, t, s["mfree"], negate=True)
        s1.done(t)
        s["tmx"] = t

    def maxparts(i):
        parts = [ms.rearrange("p (r h) -> p r h", h=32)[:, r, :] for r in range(3)]
        st[i]["tms"] = split3(k, parts, MX[:, i % 2, :], mres, st[i]["tmx"], k.msfree)

    def maxrows(i):
        s = st[i]
        s1 = S1.take()
        bb = s1.ap[:, 0, 0:64].bitcast(BF16)
        t = k.tr(bb[0:96, :], ms, s1.free, s["tms"], sig=True)
        k.msfree = t
        m = MT.take()
        t = k.v_copy(m.ap[0:96, :], bb[0:96, :], t, m.free)
        s1.done(t)
        t = k.dma(s["q"].ap[96:99, :, :], m.ap[0:96, :], t, s["q"].free, tqz)
        m.done(t)
        s["tmr"] = t

    k.msfree = None

    def second(i, h):
        s = st[i]
        kk = kb[i // 4]
        s2 = S2.take()
        bb = s2.ap.rearrange("p (t n) -> p t n", t=4)
        for t4 in range(4):
            t = k.mm(bb[:, t4, :], kk["ks"].ap[:, h // 4, t4 * P:t4 * P + P], s["q"].ap[:, h, :], True, True,
                     s2.free, s["tmr"], s["tq"], kk["tk"], sig=(t4 == 3))
        if h % 4 == 0:
            s["pt"] = PT.take()
        p = s["pt"]
        t = k.activ(p.ap[:, :, h % 4, :], bb, ACT.Exp, t, p.free)
        s2.done(t)
        if h % 4 == 3:
            s["p"].append((h // 4, p, t))

    def pv(i):
        s = st[i]
        kv, p, t = s["p"].pop(0)
        kk = kb[i // 4]
        if kv % 4 == 0:
            s["ob"] = OB.take()
        ob = s["ob"]
        r0 = 32 * (kv % 4)
        for t4 in range(4):
            t2 = k.mm(ob.ap[r0:r0 + 32, :], kk["va"].ap[:, t4, kv, :], p.ap[:, t4].rearrange("p h n -> p (h n)"),
                      t4 == 0, t4 == 3, ob.free, t, kk["tv"], kk["tva"], sig=(t4 == 3))
        p.done(t2)
        if kv % 4 == 3:
            o = OT.take()
            t3 = k.acopy(o.ap.rearrange("p a b -> p (a b)"), ob.ap, t2, o.free)
            ob.done(t3)
            s["ot"].append((kv // 4, o, t3))
        if kv == 7:
            s["q"].done(t2, k.pe.last)
            if i % 4 == 3:
                kk["ks"].done(k.pe.last)
                kk["va"].done(k.pe.last)

    def back(i):
        s = st[i]
        half, o, t = s["ot"].pop(0)
        s1 = S1.take()
        bb = s1.ap[:, 0, :].rearrange("p (g n) -> p g n", g=4)
        for g in range(4):
            t2 = k.tr(bb[:, g, :], o.ap[:, g, :], s1.free, t, sig=(g == 3))
        o.done(t2)
        if half == 0:
            s["oa"] = oa.take()
            s["toa"] = []
        b4 = bb.rearrange("p g (v e) -> p v g e", e=32)
        r = rz[:, i % 2, 16 * half:16 * half + 16].rearrange("p (v g) -> p v g", g=4).unsqueeze(3)
        t3 = k.v_recip(r, b4[:, :, :, 16:17], t2, s["mfree"])
        dst = s["oa"].ap[:, 256 * half:256 * half + 256].rearrange("p (v g d) -> p v g d", g=4, d=16)
        for v in range(4):
            t4 = k.v_tt(dst[:, v], b4[:, v, :, 0:16], r[:, v].to_broadcast([P, 4, 16]), ALU.mult, t3, s["oa"].free)
        s1.done(t4)
        s["toa"].append(t4)
        if half == 1:
            def add(z, *w):
                t = k.g_tt(z, k.X[:, i, :], s["oa"].ap, ALU.add, s["toa"], *w, k.xtok[i])
                s["oa"].done(t)
                return t
            k.ln(i, add)

    for t4 in range(4):
        prep(0, t4)
    LAG = 19
    qsplit(0)
    qt(0, 0)
    qt(0, 1)
    for n in range(16 * NT + LAG + 9):
        def at(lag, j=None):
            i, jj = divmod(n - lag, 16)
            return (i, jj) if 0 <= i < NT and (j is None or jj == j) else None
        v = at(0)
        if v:
            i, j = v
            if j == 0:
                st[i]["mfree"] = k.dve.last
                st[i]["p"], st[i]["ot"] = [], []
            first(i, j)
            if i + 1 < NT:
                if j == 3:
                    qsplit(i + 1)
                if j in (13, 14):
                    qt(i + 1, j - 13)
            if i % 4 == 3 and i // 4 < 3 and j in (3, 6, 9, 12):
                prep(i // 4 + 1, j // 3 - 1)
            if j == 15:
                maxparts(i)
        if at(16, 0):
            maxrows(at(16, 0)[0])
        v = at(LAG)
        if v:
            second(v[0], 2 * v[1])
            second(v[0], 2 * v[1] + 1)
        v = at(LAG + 1)
        if v and v[1] % 2 == 1:
            pv(v[0])
        for lag, j in ((LAG + 3, 7), (LAG + 3, 15)):
            if at(lag, j):
                back(at(lag, j)[0])
    k.ln_flush()
def rows(ap):
    return ap.rearrange("(k p) n -> p k n", p=P)


def stats(k, z, st6, mv4, eps, *w):
    k.dve.wait(*w)
    t = k.dve.sig(k.nc.vector.bn_stats(st6, z))
    tr = t
    k.dve.wait(t)
    t = k.dve.sig(k.nc.vector.bn_aggr(mv4[:, 0:2], st6))
    t = k.g_ts(mv4[:, 2:3], mv4[:, 1:2], eps, 1.0, ALU.add, ALU.mult, t)
    return k.g_tt(mv4[:, 3:4], mv4[:, 2:3], k.nhalf[:, 0:1], ALU.pow, t), tr


def ffn(k, first_layer):
    nc = k.nc
    k.phase("ffn" + str(int(first_layer)))
    k.off = k.base
    W1 = k.alloc([4, 2048])
    W2 = k.alloc([16, 512])
    if first_layer:
        w1, w2 = rows(k.ins["L0_ffn_up_w"]), rows(k.ins["L0_ffn_down_w"])
        WE = k.alloc([4, 512])
        WG = k.alloc([4, 8])
        G = k.alloc([2, 512])
    else:
        w1, w2 = rows(k.ins["L3_ffn_w1"]), rows(k.ins["L3_ffn_w2"])
        B1 = k.alloc([16])
        B2 = k.alloc([512])
    tw1 = [k.dma(W1[:, kk, :], w1[:, kk, :]) for kk in range(4)]
    if first_layer:
        tc = [k.dma(WE, rows(k.ins["L0_ffn_expert_weight"])), k.dma(WG, rows(k.ins["L0_ffn_gate_w"])),
              k.dma(G, k.ins["L0_ffn_ln"])]
    else:
        tc = [k.dma(B1, k.ins["L3_ffn_b1"]), k.dma(B2, k.ins["L3_ffn_b2"])]
    tw2 = [k.dma(W2[:, 4 * j:4 * j + 4, :], w2[:, 4 * j:4 * j + 4, :]) for j in range(4)]
    XT = Ring([k.alloc([4, 512]) for _ in range(2)])
    HT = Ring([k.alloc([512]) for _ in range(4)])
    YS = Ring([k.alloc([512]) for _ in range(3)])
    ES = Ring([k.alloc([512]) for _ in range(2)])
    sm = k.alloc([NT, 24])
    YB = [k.bank(j)[:, 0, :] for j in range(4)]
    yfree = [[] for _ in range(4)]
    H = Ring([k.bank(4)[:, 0, :], k.bank(5)[:, 0, :]])
    R = Ring([k.bank(6)[:, 0, :], k.bank(7)[:, 0, :]])

    if not first_layer:
        cnt = 1.0 / (2048 * 512)
        part = k.alloc([8])
        thr = k.alloc([4])
        ones = k.alloc([P])
        tmp = Ring([k.alloc([2048]) for _ in range(2)])
        k.pool.wait()
        to = k.pool.sig(nc.gpsimd.memset(ones, 1.0))
        tq = []
        for n, (W, tw) in enumerate(((W1.rearrange("p a b -> p (a b)"), tw1), (W2.rearrange("p a b -> p (a b)"), tw2))):
            tp = [k.v_red(part[:, 4 * n + j:4 * n + j + 1], W[:, 2048 * j:2048 * j + 2048], ALU.add, tw[j],
                          absolute=True) for j in range(4)]
            t = k.v_red(thr[:, 2 * n:2 * n + 1], part[:, 4 * n:4 * n + 4], ALU.add, tp)
            b = R.take()
            t = k.mm(b.ap[:, 0:1], ones, thr[:, 2 * n:2 * n + 1], True, True, b.free, t, to, sig=True)
            t = k.v_ts(thr[:, 2 * n:2 * n + 1], b.ap[:, 0:1], cnt, 0.7, ALU.mult, ALU.mult, t)
            b.done(t)
            t = k.v_ts(thr[:, 2 * n + 1:2 * n + 2], thr[:, 2 * n:2 * n + 1], -1.0, None, ALU.mult, None, t)
            tj = []
            for j in range(4):
                s = tmp.take()
                w = W[:, 2048 * j:2048 * j + 2048]
                t2 = k.v_ts(s.ap, w, thr[:, 2 * n + 1:2 * n + 2], None, ALU.is_le, None, t, s.free)
                t2 = k.v_stt(w, w, thr[:, 2 * n:2 * n + 1], s.ap, ALU.is_ge, ALU.subtract, t2)
                s.done(t2)
                tj.append(t2)
            tq.append(tj)
        tw1, tw2 = tq

    def xt(b):
        s = XT.take()
        s.toks = []
        for t4 in range(4):
            s.toks.append(k.x_to_xt(4 * b + t4, R, s.ap[:, :, t4 * P:t4 * P + P], s.free, eng=t4 % 2))
        return s

    xs = {0: xt(0)}

    def up(b, m):
        h = H.take()
        for kk in range(4):
            t = k.mm(h.ap, W1[:, kk, m * P:m * P + P], xs[b].ap[:, kk, :], kk == 0, kk == 3, h.free, xs[b].toks,
                     tw1[kk], sig=(kk == 3))
        o = HT.take()
        if first_layer:
            t = k.activ(o.ap, h.ap, ACT.Relu, t, o.free)
            h.done(t)
            t = k.activ(o.ap, o.ap, ACT.Square, t) if m % 2 else k.v_tt(o.ap, o.ap, o.ap, ALU.mult, t)
        else:
            t = k.activ(o.ap, h.ap, ACT.Gelu, t, o.free, tc, bias=B1[:, m:m + 1])
            h.done(t)
        return o, t

    def down(b, m, ot):
        o, t = ot
        for t4 in range(4):
            td = k.mm(YB[t4], o.ap[:, t4 * P:t4 * P + P], W2[:, m, :], m == 0, m == 15, t, tw2[m // 4],
                      yfree[t4], sig=(m == 15 or t4 == 3))
            if m == 15:
                ydone[t4] = td
        o.done(td)

    def gate(i, t4):
        x = xs[i // 4]
        r = R.take()
        for kk in range(4):
            t = k.mm(r.ap[:, 0:8], x.ap[:, kk, t4 * P:t4 * P + P], WG[:, kk, :], kk == 0, kk == 3, r.free, x.toks, tc,
                     sig=(kk == 3))
        k.dve.wait(t)
        t = k.dve.sig(nc.vector.max(sm[:, i, 0:8], r.ap[:, 0:8]))
        r.done(t)
        ts = k.v_tt(sm[:, i, 8:9], sm[:, i, 0:1], sm[:, i, 1:2], ALU.add, t)
        r = R.take()
        for kk in range(4):
            t = k.mm(r.ap, x.ap[:, kk, t4 * P:t4 * P + P], WE[:, kk, :], kk == 0, kk == 3, r.free, sig=(kk == 3))
        e = ES.take()
        t = k.activ(e.ap, r.ap, ACT.Copy, t, ts, e.free, scale=sm[:, i, 8:9])
        r.done(t)
        return e, t

    def finish(i, t4):
        if first_layer:
            e, te = gate(i, t4)
            y = YS.take()
            ty = k.v_tt(y.ap, YB[t4], e.ap, ALU.add, ydone[t4], te, y.free)
            yfree[t4] = [ty]
            e.done(ty)
            ts, _ = stats(k, y.ap, sm[:, i, 9:15], sm[:, i, 16:20], 1e-5, ty)
            return y, ts, i
        y = YS.take()
        tx = k.g_tt(y.ap, k.X[:, i, :], B2, ALU.add, k.xtok[i], tc, y.free)

        def add(z, *w):
            t = k.v_tt(z, y.ap, YB[t4], ALU.add, tx, *w)
            yfree[t4] = [t]
            y.done(t)
            return t
        k.ln(i, add, ydone[t4])
        return None

    def finish2(v):
        y, ts, i = v
        t = k.v_ts(y.ap, y.ap, sm[:, i, 16:17], sm[:, i, 19:20], ALU.subtract, ALU.mult, ts)
        t = k.g_tt(y.ap, y.ap, G[:, 0, :], ALU.mult, t, tc)
        t = k.g_tt(y.ap, y.ap, G[:, 1, :], ALU.add, t)

        def add(z, *w):
            t2 = k.v_tt(z, y.ap, k.X[:, i, :], ALU.add, t, *w, k.xtok[i])
            y.done(t2)
            return t2
        k.ln(i, add)

    ydone = [None] * 4
    pend = []
    for b in range(4):
        q = []
        for m in range(16):
            q.append(up(b, m))
            if m >= 2:
                down(b, m - 2, q[m - 2])
            if m == 8 and b < 3:
                xs[b + 1] = xt(b + 1)
        down(b, 14, q[14])
        down(b, 15, q[15])
        for t4 in range(4):
            v = finish(4 * b + t4, t4)
            if v:
                pend.append(v)
                if len(pend) > 1:
                    finish2(pend.pop(0))
        xs[b].done(k.pe.last)
    while pend:
        finish2(pend.pop(0))
    k.ln_flush()


def l0_ffn(k):
    ffn(k, True)


def l3_ffn(k):
    ffn(k, False)


def attn(k, label, kind):
    nc = k.nc
    k.phase(label)
    k.off = k.base
    ins = k.ins
    lat = kind == 1
    SC = float(32) ** -0.5
    WQ = k.alloc([4, 512])
    nk = 1 if lat else 4
    WK, WV = k.alloc([nk, 512]), k.alloc([nk, 512])
    WO = k.alloc([4, 512])
    tw = [k.dma(w, rows(ins[label + n])) for w, n in ((WQ, "_q"), (WK, "_k"), (WV, "_v"), (WO, "_o"))]
    XT = Ring([k.alloc([4, P]) for _ in range(2)])
    if lat:
        CT = k.alloc([4, 512])
        tw.append(k.dma(CT, ins["ctx_T"]))
    else:
        BQ, BK, BV, BO = k.alloc([4]), k.alloc([4]), k.alloc([512]), k.alloc([512])
        tw += [k.dma(w, ins[label + n]) for w, n in ((BQ, "_bq"), (BK, "_bk"), (BV, "_bv"), (BO, "_bo"))]
    QT = Ring([k.alloc([4, 4, P]) for _ in range(3)])
    for b in QT.bufs:
        k.pool.wait()
        tqz = k.pool.sig(nc.gpsimd.memset(b, 0.0))
    KT = Ring([k.alloc([4, 512]) for _ in range(2)])
    if kind == 2:
        V = Ring([k.alloc([512]) for _ in range(3)])
        JK = Ring([k.alloc([512]) for _ in range(2)])
        SM = k.alloc([2, 4, 16])
    else:
        VA = Ring([k.alloc([4, 8, 4, 32]) for _ in range(2)])
        k.pool.wait()
        for b in VA.bufs:
            tva = k.pool.sig(nc.gpsimd.memset(b[:, :, :, 1:3, :], 1.0))
        PT = Ring([k.alloc([2, 512]) for _ in range(4)])
        NS = k.alloc([4, 32], BF16)
        NM = Ring([k.alloc([P], BF16) for _ in range(2)])
        SEL = k.alloc([4, 4, P], BF16)
        stg = k.alloc([4, 4, P])
        t = k.dma(stg, ins["c_sel"])
        tsel = [k.v_copy(SEL, stg, t)]
        k.pool.wait()
        tsel.append(k.pool.sig(nc.gpsimd.memset(NS, 0.0)))
        mres = k.alloc([16])
        RZ = k.alloc([2, 512])
    MX = k.alloc([2, 4, 4])
    ON = Ring([k.alloc([512]) for _ in range(2)])
    OT = Ring([k.alloc([4, P]) for _ in range(2)])
    XB = Ring([k.alloc([512]) for _ in range(2)])
    A = Ring([k.bank(0, 2), k.bank(2, 2)])
    S2 = Ring([k.bank(4, 2)])
    OB = Ring([k.bank(6, 2)])
    LAG = 10
    st = [dict() for _ in range(NT)]
    kb = [dict() for _ in range(4)]
    free = {"mx": [None, None], "ns": None, "rz": None}

    def v4(ap):
        return ap.rearrange("p (m n) -> p m n", m=4)

    def proj(i):
        s, b, t4 = st[i], kb[i // 4], i % 4
        if t4 == 0:
            b["kt"] = KT.take()
            b["tk"] = []
            if kind != 2:
                b["v"] = VA.take()
                b["tv"] = [tva]
        a = A.take()
        xt = XT.take()
        bb = v4(a.ap[:, 0, :])
        for kk in range(4):
            t = k.tr(bb[:, kk, :], k.X[:, i, kk * P:kk * P + P], a.free, k.xtok[i], sig=(kk == 3))
        txt = k.acopy(xt.ap, bb, t, xt.free)
        a.done(txt)
        a = A.take()
        q = s["q"] = QT.take()
        bb = v4(a.ap[:, 0, :])
        for m in range(4):
            for kk in range(4):
                t = k.mm(bb[:, m, :], WQ[:, kk, m * P:m * P + P], xt.ap[:, kk, :], kk == 0, kk == 3, a.free, tw, txt,
                         sig=(kk == 3 and m == 3))
        s["tq"] = [tqz]
        for g in range(4):
            r = slice(32 * g, 32 * g + 32)
            if lat:
                t1 = k.acopy(q.ap[r, g], bb[r], t, q.free, tqz)
            else:
                t1 = k.v_tt(q.ap[r, g], bb[r], BQ[r].unsqueeze(2).to_broadcast([32, 4, P]), ALU.add, t, q.free, tqz)
            s["tq"].append(t1)
        bb = v4(a.ap[:, 1, :])
        for m in range(4):
            for kk in range(nk):
                r = CT[:, i // 4, t4 * P:t4 * P + P] if lat else xt.ap[:, kk, :]
                t = k.mm(bb[:, m, :], WK[:, kk, m * P:m * P + P], r, kk == 0, kk == nk - 1, sig=(kk == nk - 1 and m == 3))
        dst = b["kt"].ap[:, :, t4 * P:t4 * P + P]
        if lat:
            t2 = k.acopy(dst, bb, t, b["kt"].free)
        else:
            t2 = k.v_tt(dst, bb, BK.unsqueeze(2).to_broadcast([P, 4, P]), ALU.add, t, b["kt"].free)
        a.done(t1, t2)
        b["tk"].append(t2)
        a = A.take()
        for kk in range(nk):
            l = CT[:, i // 4, t4 * P:t4 * P + P] if lat else xt.ap[:, kk, :]
            t = k.mm(a.ap[:, 0, :], l, WV[:, kk, :], kk == 0, kk == nk - 1, a.free, sig=(kk == nk - 1))
        xt.done(t)
        src = a.ap[:, 0, :].rearrange("p (h w d) -> p h w d", w=2, d=32)
        if kind == 2:
            v = s["v"] = V.take()
            t = s["tv"] = k.v_tt(v.ap, a.ap[:, 0, :], BV, ALU.add, t, v.free)
        elif lat:
            t = k.acopy(b["v"].ap[:, t4, :, 0:4:3, :], src, t, b["v"].free)
            b["tv"].append(t)
        else:
            t = k.v_tt(b["v"].ap[:, t4, :, 0:4:3, :], src, BV.rearrange("p (h w d) -> p h w d", w=2, d=32), ALU.add, t,
                       b["v"].free)
            b["tv"].append(t)
        a.done(t)

    def first(i, hg, u):
        s, b, n = st[i], kb[i // 4], (i % 4 + 1) * P
        a = A.take()
        for g in range(2):
            k.mm(a.ap[:, g, 0:n], s["q"].ap[:, 2 * u + g, hg, :], b["kt"].ap[:, hg, 0:n], True, False,
                 a.free, s["tq"], b["tk"])
            t = k.mm(a.ap[:, g, n - P:n], k.idb, k.mq, False, True, sig=(g == 1))
        tm = k.v_red(MX[:, i % 2, 2 * u:2 * u + 2, hg], a.ap[:, :, 0:n], ALU.max, t, free["mx"][i % 2], negate=True)
        if kind == 2:
            for g in range(2):
                g4 = 2 * u + g
                j = JK.take()
                tb = k.v_ts(SM[:, i % 2, 0, 4 * hg + g4:4 * hg + g4 + 1], MX[:, i % 2, g4, hg:hg + 1], SC, None, ALU.mult,
                            None, tm, s["smfree"])
                t = k.activ(j.ap[:, 0:n], a.ap[:, g, 0:n], ACT.Exp, tb, j.free, s["smfree"],
                            bias=SM[:, i % 2, 0, 4 * hg + g4:4 * hg + g4 + 1], scale=SC,
                            accum=SM[:, i % 2, 1, 4 * hg + g4:4 * hg + g4 + 1])
                j.done(t)
            tm = t
        a.done(tm)
        s["tm"] = tm

    def maxparts(i):
        s = st[i]
        parts = [NS[:, :, 4 * r:4 * r + 4] for r in range(3)]
        t = split3(k, parts, MX[:, i % 2], mres.rearrange("p (a b) -> p a b", b=4), s["tm"], free["ns"], tsel)
        free["mx"][i % 2] = s["tns"] = t

    def maxrows(i):
        s = st[i]
        a = A.take()
        bb = a.ap[:, 0, 0:64].bitcast(BF16)
        t = free["ns"] = k.tr(bb, NS.rearrange("p a b -> p (a b)"), a.free, s["tns"], sig=True)
        m = s["nm"] = NM.take()
        s["tnm"] = k.v_copy(m.ap, bb, t, m.free)
        a.done(s["tnm"])

    def second(i, hg, u):
        s, b, n = st[i], kb[i // 4], i % 4 + 1
        a = S2.take()
        for g in range(2):
            for kt in range(n):
                o = a.ap[:, g, kt * P:kt * P + P]
                k.mm(o, b["kt"].ap[:, hg, kt * P:kt * P + P], s["q"].ap[:, 2 * u + g, hg, :], True, False,
                     a.free, s["tq"], b["tk"], s["tnm"])
                if kt == n - 1:
                    k.mm(o, k.idb, k.mk, False, False)
                t = k.mm(o, SEL[:, 2 * u + g, hg, :], s["nm"].ap, False, True, tsel,
                         sig=(g == 1 and kt == n - 1))
        p = PT.take()
        t = k.activ(p.ap[:, :, 0:n * P], a.ap[:, :, 0:n * P], ACT.Exp, t, p.free, scale=SC)
        a.done(t)
        s["p"].append((hg, u, p, t))

    def pv(i):
        s, b, n = st[i], kb[i // 4], i % 4 + 1
        hg, u, p, t = s["p"].pop(0)
        if hg == 0 and u == 0:
            s["ob"] = OB.take()
        ob = s["ob"]
        for g in range(2):
            for kt in range(n):
                v = b["v"].ap[:, kt, 2 * hg + u, 2 * g:2 * g + 2, :].rearrange("p w d -> p (w d)")
                t2 = k.mm(ob.ap[64 * u:64 * u + 64, g, hg * P:hg * P + P], v, p.ap[:, g, kt * P:kt * P + P],
                          kt == 0, kt == n - 1, ob.free, t, b["tv"], sig=(g == 1 and kt == n - 1))
        p.done(t2)
        if hg == 3 and u == 1:
            o = s["ot"] = OT.take()
            s["tot"] = []
            tz = [k.v_recip(RZ[:, g, :], ob.ap[:, g, :], t2, free["rz"]) for g in range(2)]
            for g4 in range(4):
                r0, z0, g = 32 * g4, 32 * (g4 ^ 1), g4 % 2
                t3 = k.v_tt(o.ap[r0:r0 + 32].rearrange("p a b -> p (a b)"), ob.ap[r0:r0 + 32, g, :],
                            RZ[z0:z0 + 32, g, :], ALU.mult, tz[g], o.free)
                s["tot"].append(t3)
            free["rz"] = s["tot"]
            ob.done(*s["tot"])
            s["q"].done(t2)
            s["nm"].done(t2)
            if i % 4 == 3:
                b["kt"].done(t2)
                b["v"].done(t2)

    def out(i):
        s = st[i]
        if kind == 2:
            if i % 4 == 3:
                kb[i // 4]["kt"].done(k.pe.last)
            s["q"].done(k.pe.last)
            on = s["on"] = ON.take()
            n, r, m = (SM[:, i % 2, j, :] for j in (1, 2, 3))
            t = k.v_recip(r, n, s["tm"])
            t = k.v_tt(m, n, r, ALU.mult, t)
            t = k.v_tt(on.ap.rearrange("p (h d) -> p h d", d=32), s["v"].ap.rearrange("p (h d) -> p h d", d=32),
                       m.unsqueeze(2).to_broadcast([P, 16, 32]), ALU.mult, t, s["tv"], on.free)
            s["v"].done(t)
            s["ton"] = [t]
            s["tsm"] = t
        a = A.take()
        if kind == 2:
            bb = v4(a.ap[:, 0, :])
            for kk in range(4):
                t = k.tr(bb[:, kk, :], s["on"].ap[:, kk * P:kk * P + P], a.free, s["ton"], sig=(kk == 3))
            s["on"].done(t)
            o = OT.take()
            t = k.acopy(o.ap, bb, t, o.free)
        else:
            o, t = s["ot"], [s["tot"], a.free]
        for kk in range(4):
            t2 = k.mm(a.ap[:, 1, :], o.ap[:, kk, :], WO[:, kk, :], kk == 0, kk == 3, t, sig=(kk == 3))
        o.done(t2)
        if lat:
            k.ln(i, k.add_from(i, a.ap[:, 1, :], a), t2)
            return
        xb = XB.take()
        tb = k.g_tt(xb.ap, k.X[:, i, :], BO, ALU.add, k.xtok[i], xb.free, tw)

        def add(z, *w):
            t = k.v_tt(z, xb.ap, a.ap[:, 1, :], ALU.add, tb, *w)
            a.done(t)
            xb.done(t)
            return t
        k.ln(i, add, t2)

    proj(0)
    for n in range(8 * NT + 22):
        def at(lag, j=None):
            i, jj = divmod(n - lag, 8)
            return (i, jj) if 0 <= i < NT and (j is None or jj == j) else None
        v = at(0)
        if v:
            if v[1] == 0:
                st[v[0]]["p"] = []
                st[v[0]]["smfree"] = st[v[0] - 2]["tsm"] if kind == 2 and v[0] >= 2 else None
            first(v[0], v[1] // 2, v[1] % 2)
            if v[1] == 4 and v[0] + 1 < NT:
                proj(v[0] + 1)
        if kind == 2:
            v = at(2, 7)
            if v:
                out(v[0])
            continue
        if at(0, 7):
            maxparts(at(0, 7)[0])
        if at(2, 7):
            maxrows(at(2, 7)[0])
        v = at(LAG)
        if v:
            second(v[0], v[1] // 2, v[1] % 2)
        v = at(LAG + 1)
        if v:
            pv(v[0])
        if at(LAG + 4, 7):
            out(at(LAG + 4, 7)[0])
    k.ln_flush()


def l2_attn(k):
    attn(k, "L2_attn", 0)


def l2_xattn(k):
    attn(k, "L2_xattn", 1)


def l3_attn(k):
    attn(k, "L3_attn", 2)


def l3_xattn(k):
    nc = k.nc
    k.phase("l3xattn")
    k.off = k.base
    ins = k.ins
    CT = k.alloc([4, 512])
    WK = k.alloc([P])
    bk = k.alloc([1])
    GB = k.alloc([2, 512])
    KT = Ring([k.alloc([512]) for _ in range(2)])
    KV = Ring([k.alloc([4, P]) for _ in range(2)])
    XT = Ring([k.alloc([4, P]) for _ in range(2)])
    OT = Ring([k.alloc([P]) for _ in range(2)])
    ZZ = Ring([k.alloc([512]) for _ in range(4)])
    sm = k.alloc([NT, 16])
    R = Ring([k.bank(j)[:, 0, :] for j in range(8)])
    tc = [k.dma(CT, ins["ctx_T"]), k.dma(WK, ins["L3_xattn_W_k"]), k.dma(bk, ins["L3_xattn_b_k"]),
          k.dma(GB, ins["L3_xattn_ln"])]
    SC = float(512) ** -0.5
    kb = [dict() for _ in range(4)]
    st = [dict() for _ in range(NT)]

    def keys(b):
        s = kb[b]
        r = R.take()
        t = k.mm(r.ap, WK, CT[:, b, :], True, True, r.free, tc, sig=True)
        s["kt"], s["kv"] = KT.take(), KV.take()
        t = k.activ(s["kt"].ap, r.ap, ACT.Identity, t, s["kt"].free, bias=bk[:, 0:1])
        r.done(t)
        s["tk"] = t
        r = R.take()
        bb = r.ap.rearrange("p (m n) -> p m n", m=4)
        for m in range(4):
            t = k.tr(bb[:, m, :], s["kt"].ap[:, m * P:m * P + P], r.free, s["tk"], sig=(m == 3))
        s["tv"] = k.v_copy(s["kv"].ap, bb, t, s["kv"].free)
        r.done(s["tv"])

    def a(i):
        if i % 4 == 0:
            keys(i // 4)
        s = st[i]
        s["xt"] = XT.take()
        s["txt"] = k.x_to_xt(i, R, s["xt"].ap, s["xt"].free, eng=0)

    def b(i):
        s, b = st[i], kb[i // 4]
        r = R.take()
        for kk in range(4):
            t = k.mm(r.ap[:, 0:P], b["kv"].ap[:, kk, :], s["xt"].ap[:, kk, :], kk == 0, kk == 3, r.free, b["tv"], s["txt"],
                     sig=(kk == 3))
        s["xt"].done(t)
        o = OT.take()
        to = k.acopy(o.ap, r.ap[:, 0:P], t, o.free)
        r.done(to)
        r = R.take()
        t = k.mm(r.ap, o.ap, b["kt"].ap, True, True, r.free, to, b["tk"], sig=True)
        o.done(t)
        if i % 4 == 3:
            b["kt"].done(t)
            b["kv"].done(t)
        m = sm[:, i, :]
        k.dve.wait(t)
        t1 = k.dve.sig(nc.vector.bn_stats(m[:, 0:6], r.ap))
        k.dve.wait(t1)
        t1 = k.dve.sig(nc.vector.bn_aggr(m[:, 6:8], m[:, 0:6]))
        t1 = k.g_ts(m[:, 8:9], m[:, 7:8], SC * SC, 1e-6, ALU.mult, ALU.add, t1)
        t1 = k.g_tt(m[:, 9:10], m[:, 8:9], k.nhalf[:, 0:1], ALU.pow, t1)
        t1 = k.g_ts(m[:, 10:11], m[:, 9:10], SC, 1.0, ALU.mult, ALU.mult, t1)
        s["r"], s["t1"] = r, t1

    def c(i):
        s = st[i]
        m = sm[:, i, :]
        r = s["r"]
        z = ZZ.take()
        t = k.v_ts(z.ap, r.ap, m[:, 6:7], m[:, 10:11], ALU.subtract, ALU.mult, s["t1"], z.free)
        r.done(t)
        t = k.g_tt(z.ap, z.ap, GB[:, 0, :], ALU.mult, t, tc)
        s["tz"] = k.g_tt(z.ap, z.ap, GB[:, 1, :], ALU.add, t)
        s["z"] = z

    def d(i):
        s = st[i]
        m, z = sm[:, i, :], s["z"]
        t = k.v_red(m[:, 11:12], z.ap, ALU.max, s["tz"], negate=True)
        t = k.activ(z.ap, z.ap, ACT.Exp, t, bias=m[:, 11:12], accum=m[:, 12:13])
        t = k.v_recip(m[:, 13:14], m[:, 12:13], t)

        def add(zz, *w):
            t2 = k.v_stt(zz, z.ap, m[:, 13:14], k.X[:, i, :], ALU.mult, ALU.add, t, *w, k.xtok[i])
            z.done(t2)
            return t2
        k.ln(i, add)

    pipeline(NT, [(0, a), (1, b), (2, c), (3, d)])
    k.ln_flush()


def l1_xattn(k):
    nc = k.nc
    k.phase("l1xattn")
    k.off = k.base
    ins = k.ins
    CT = k.alloc([4, 512])
    W = k.alloc([2, P])
    gr = k.alloc([4])
    QT, KT = (Ring([k.alloc([512]) for _ in range(2)]) for _ in range(2))
    SS = Ring([k.alloc([512]) for _ in range(3)])
    WK = Ring([k.alloc([512]) for _ in range(2)])
    m8 = k.alloc([2, 8])
    AL = Ring([k.alloc([4, 512]) for _ in range(2)])
    BB = Ring([k.alloc([512]) for _ in range(2)])
    XS = Ring([k.alloc([512]) for _ in range(2)])
    R = Ring([k.bank(j)[:, 0, :] for j in range(8)])
    tc = [k.dma(CT, ins["ctx_T"]), k.dma(W, ins["L1_xattn_W"])]
    t = k.dma(gr[:, 0:1], ins["L1_gamma"])
    t = k.activ(gr[:, 1:2], gr[:, 0:1], ACT.Exp, t, scale=-1.0)
    t = k.v_ts(gr[:, 1:2], gr[:, 1:2], 1.0, None, ALU.add, None, t)
    t = k.v_recip(gr[:, 1:2], gr[:, 1:2], t)
    tg = [k.v_ts(gr[:, 2:3], gr[:, 1:2], -1.0, 2.0, ALU.mult, ALU.add, t),
          k.v_ts(gr[:, 3:4], gr[:, 1:2], 0.5, None, ALU.mult, None, t)]
    SC = 1.0 / (float(np.sqrt(np.float32(32))) * 4)
    kb = [dict() for _ in range(4)]

    def sims(b):
        s = kb[b]
        for j, (ring, n) in enumerate(((QT, "q"), (KT, "k"))):
            r = R.take()
            t = k.mm(r.ap, W[:, j, :], CT[:, b, :], True, True, r.free, tc, sig=True)
            s[n] = ring.take()
            if j == 0:
                t = k.activ(s[n].ap, r.ap, ACT.Copy, t, s[n].free, scale=SC)
            else:
                t = k.acopy(s[n].ap, r.ap, t, s[n].free)
            r.done(t)
            s["t" + n] = t
        s["al"] = AL.take()
        s["ta"] = []

    def topk(b, t4):
        s = kb[b]
        r = R.take()
        t = k.mm(r.ap, s["q"].ap[:, t4 * P:t4 * P + P], s["k"].ap, True, True, r.free, s["tq"], s["tk"], sig=True)
        if t4 == 3:
            s["q"].done(t)
            s["k"].done(t)
        o = SS.take()
        ts = k.acopy(o.ap, r.ap, t, o.free)
        r.done(ts)
        w = WK.take()
        m = m8[:, (4 * b + t4) % 2, :]
        k.dve.wait(ts, w.free)
        k.dve.wait(k.dve.last)
        t = k.dve.sig(nc.vector.max(m, o.ap))
        for n in range(19):
            k.dve.wait(t)
            t = k.dve.sig(nc.vector.match_replace(w.ap, m, o.ap if n == 0 else w.ap, -3.0e38))
            k.dve.wait(t)
            t = k.dve.sig(nc.vector.max(m, w.ap))
        w.done(t)
        te = k.activ(w.ap, o.ap, ACT.Exp, t, scale=-1.0)
        te = k.v_ts(w.ap, w.ap, 1.0, None, ALU.add, None, te)
        te = k.v_recip(w.ap, w.ap, te)
        al = s["al"]
        t = k.v_stt(al.ap[:, t4, :], o.ap, m[:, 0:1], w.ap, ALU.is_ge, ALU.mult, te, al.free)
        w.done(t)
        o.done(t)
        s["ta"].append(t)

    def mix(i):
        s, t4 = kb[i // 4], i % 4
        al = s["al"]
        r = R.take()
        bb = r.ap.rearrange("p (m n) -> p m n", m=4)
        for m in range(4):
            t = k.tr(bb[:, m, :], al.ap[:, m, t4 * P:t4 * P + P], r.free, s["ta"], sig=(m == 3))
        o = BB.take()
        x = XS.take()
        tx = k.activ(x.ap, k.X[:, i, :], ACT.Copy, x.free, k.xtok[i], tg, scale=gr[:, 2:3])
        t = k.v_tt(o.ap, al.ap[:, t4, :], r.ap, ALU.add, t, o.free)
        r.done(t)
        if t4 == 3:
            al.done(t)

        def add(z, *w):
            t2 = k.v_stt(z, o.ap, gr[:, 3:4], x.ap, ALU.mult, ALU.add, t, tx, *w)
            o.done(t2)
            x.done(t2)
            return t2
        k.ln(i, add)

    for b in range(4):
        sims(b)
        for t4 in range(4):
            topk(b, t4)
        for t4 in range(4):
            mix(4 * b + t4)
    k.ln_flush()


MAGIC = 12582912.0


def l1_ffn(k):
    nc = k.nc
    k.phase("l1ffn")
    k.off = k.base
    ins = k.ins
    WG, WU = k.alloc([4, 2048], BF16), k.alloc([4, 2048], BF16)
    WD = k.alloc([16, 512], BF16)
    H = k.alloc([P])
    part = k.alloc([16])
    sc = k.alloc([8])
    ones = k.alloc([P])
    keep = k.off
    stg = [k.alloc([8192]) for _ in range(2)]
    R = Ring([k.bank(j)[:, 0, :] for j in range(8)])
    th = k.dma(H, ins["c_hadamard"])
    k.pool.wait()
    to = k.pool.sig(nc.gpsimd.memset(ones, 1.0))
    cnt = 1.0 / (2048 * 512)
    tw, sfree = [], [[], []]
    for n, (name, W) in enumerate((("L1_ffn_w_gate", WG), ("L1_ffn_w_up", WU), ("L1_ffn_w_down", WD))):
        S = stg[n % 2]
        src = rows(ins[name])
        kk = src.shape[1] // 4
        tl = [k.dma(S[:, 2048 * j:2048 * j + 2048].rearrange("p (k n) -> p k n", k=kk),
                    src[:, kk * j:kk * j + kk, :], sfree[n % 2]) for j in range(4)]
        tp = [k.v_red(part[:, 4 * n + j:4 * n + j + 1], S[:, 2048 * j:2048 * j + 2048], ALU.add, tl[j], absolute=True)
              for j in range(4)]
        t = k.v_red(sc[:, n:n + 1], part[:, 4 * n:4 * n + 4], ALU.add, tp)
        b = R.take()
        t = k.mm(b.ap[:, 0:1], ones, sc[:, n:n + 1], True, True, b.free, t, to, sig=True)
        t = k.v_ts(sc[:, n:n + 1], b.ap[:, 0:1], cnt, 1e-5, ALU.mult, ALU.max, t)
        b.done(t)
        t = k.v_recip(sc[:, 4 + n:5 + n], sc[:, n:n + 1], t)
        Wf = W.rearrange("p a b -> p (a b)")
        tj = []
        for j in range(4):
            w = S[:, 2048 * j:2048 * j + 2048]
            t2 = k.v_ts(w, w, sc[:, 4 + n:5 + n], 1.0, ALU.mult, ALU.min, t)
            t2 = k.v_ts(w, w, -1.0, MAGIC, ALU.max, ALU.add, t2)
            t2 = k.v_ts(Wf[:, 2048 * j:2048 * j + 2048], w, MAGIC, None, ALU.subtract, None, t2)
            tj.append(t2)
        sfree[n % 2] = tj
        tw.append(tj)
    tstage = [x for y in sfree for x in y]
    k.off = keep
    XQ = Ring([k.alloc([512]) for _ in range(2)], tstage)
    XB = Ring([k.alloc([512], BF16) for _ in range(2)], tstage)
    XT = Ring([k.alloc([4, P], BF16) for _ in range(2)], tstage)
    IM = Ring([k.alloc([2048]) for _ in range(2)], tstage)
    IT = Ring([k.alloc([16, P]) for _ in range(1)], tstage)
    HA = Ring([k.alloc([2048]) for _ in range(2)], tstage)
    HB = Ring([k.alloc([2048]) for _ in range(2)], tstage)
    YB = Ring([k.alloc([2048], BF16) for _ in range(1)], tstage)
    YT = Ring([k.alloc([16, P], BF16) for _ in range(2)], tstage)
    SG = Ring([k.alloc([512]) for _ in range(3)], tstage)
    sm = k.alloc([NT, 12])
    st = [dict() for _ in range(NT)]
    HN = float(1.0 / np.sqrt(2048))

    def a(i):
        s, m = st[i], sm[:, i, :]
        x = XQ.take()
        t = k.v_red(m[:, 0:1], k.X[:, i, :], ALU.max, k.xtok[i], tstage, absolute=True)
        t = k.v_ts(m[:, 0:1], m[:, 0:1], 1e-5, 1.0 / 128, ALU.max, ALU.mult, t)
        tr = k.v_recip(m[:, 1:2], m[:, 0:1], t)
        s["tf"] = [k.v_ts(m[:, 2:3], m[:, 0:1], sc[:, 0:1], None, ALU.mult, None, tr),
                   k.v_ts(m[:, 3:4], m[:, 0:1], sc[:, 1:2], None, ALU.mult, None, tr)]
        t = k.v_ts(x.ap, k.X[:, i, :], m[:, 1:2], 127.0, ALU.mult, ALU.min, tr, x.free)
        t = k.v_ts(x.ap, x.ap, -128.0, MAGIC, ALU.max, ALU.add, t)
        xb = XB.take()
        t = k.v_ts(xb.ap, x.ap, MAGIC, None, ALU.subtract, None, t, xb.free)
        x.done(t)
        r = R.take()
        bb = r.ap.bitcast(BF16)[:, 0:512].rearrange("p (m n) -> p m n", m=4)
        for kk in range(4):
            t1 = k.tr(bb[:, kk, :], xb.ap[:, kk * P:kk * P + P], r.free, t, sig=(kk == 3))
        xb.done(t1)
        s["xt"] = XT.take()
        s["txt"] = k.acopy(s["xt"].ap, bb, t1, s["xt"].free)
        r.done(s["txt"])

    def b(i):
        s, m = st[i], sm[:, i, :]
        im = s["im"] = IM.take()
        s["tim"] = []
        for c in range(4):
            r, r2 = R.take(), R.take()
            for kk in range(4):
                t = k.mm(r.ap, s["xt"].ap[:, kk, :], WG[:, kk, 512 * c:512 * c + 512], kk == 0, kk == 3, r.free,
                         s["txt"], tw[0], sig=(kk == 3))
            for kk in range(4):
                t2 = k.mm(r2.ap, s["xt"].ap[:, kk, :], WU[:, kk, 512 * c:512 * c + 512], kk == 0, kk == 3, r2.free,
                          tw[1], sig=(kk == 3))
            g = SG.take()
            t = k.activ(g.ap, r.ap, ACT.Silu, t, s["tf"], g.free, scale=m[:, 2:3])
            r.done(t)
            t = k.v_stt(im.ap[:, 512 * c:512 * c + 512], r2.ap, m[:, 3:4], g.ap, ALU.mult, ALU.mult, t, t2, im.free)
            r2.done(t)
            g.done(t)
            s["tim"].append(t)
        s["xt"].done(k.pe.last)

    def c(i):
        s, m = st[i], sm[:, i, :]
        im, it = s["im"], IT.take()
        te = []
        for c in range(4):
            r = R.take()
            bb = r.ap.rearrange("p (m n) -> p m n", m=4)
            for j in range(4):
                t = k.tr(bb[:, j, :], im.ap[:, (4 * c + j) * P:(4 * c + j + 1) * P], r.free, s["tim"], sig=(j == 3))
            te.append(k.acopy(it.ap[:, 4 * c:4 * c + 4, :], bb, t, it.free))
            r.done(te[-1])
        im.done(t)
        ha, hb = HA.take(), HB.take()
        tc = []
        for c in range(4):
            r = R.take()
            for j in range(4):
                t = k.mm(r.ap[:, j * P:j * P + P], it.ap[:, 4 * c + j, :], H, True, True, r.free, te[c], th, sig=(j == 3))
            tc.append(k.acopy(ha.ap[:, 512 * c:512 * c + 512], r.ap, t, ha.free))
            r.done(tc[-1])
        it.done(t)
        cur, nxt, t = ha, hb, tc
        nfree = hb.free
        for lv in range(4):
            h = P << lv
            v = cur.ap.rearrange("p (a t n) -> p a t n", t=2, n=h)
            o = nxt.ap.rearrange("p (a t n) -> p a t n", t=2, n=h)
            f = k.v_tt if lv < 2 else k.g_tt
            t1 = f(o[:, :, 0, :], v[:, :, 0, :], v[:, :, 1, :], ALU.add, t, nfree)
            t2 = f(o[:, :, 1, :], v[:, :, 0, :], v[:, :, 1, :], ALU.subtract, t)
            cur, nxt, t, nfree = nxt, cur, [t1, t2], None
        s["ha"], s["hb"], s["th"] = ha, hb, t

    def d(i):
        s, m = st[i], sm[:, i, :]
        ha, hb = s["ha"], s["hb"]
        t = k.v_red(m[:, 4:5], ha.ap, ALU.max, s["th"], absolute=True)
        t = k.v_ts(m[:, 4:5], m[:, 4:5], HN, 1e-5, ALU.mult, ALU.max, t)
        t = k.v_ts(m[:, 4:5], m[:, 4:5], 1.0 / 128, None, ALU.mult, None, t)
        t = k.v_recip(m[:, 5:6], m[:, 4:5], t)
        t1 = k.v_ts(m[:, 5:6], m[:, 5:6], HN, None, ALU.mult, None, t)
        tf = k.v_ts(m[:, 6:7], m[:, 4:5], sc[:, 2:3], None, ALU.mult, None, t)
        t = k.v_ts(ha.ap, ha.ap, m[:, 5:6], 127.0, ALU.mult, ALU.min, t1)
        t = k.v_ts(ha.ap, ha.ap, -128.0, MAGIC, ALU.max, ALU.add, t)
        yb = YB.take()
        t = k.v_ts(yb.ap, ha.ap, MAGIC, None, ALU.subtract, None, t, yb.free)
        ha.done(t)
        hb.done(t, s["th"])
        yt = YT.take()
        te = []
        for c in range(2):
            r = R.take()
            bb = r.ap.bitcast(BF16).rearrange("p (m n) -> p m n", m=8)
            for j in range(8):
                t1 = k.tr(bb[:, j, :], yb.ap[:, (8 * c + j) * P:(8 * c + j + 1) * P], r.free, t, sig=(j == 7))
            te.append(k.acopy(yt.ap[:, 8 * c:8 * c + 8, :], bb, t1, yt.free))
            r.done(te[-1])
        yb.done(t1)
        r = R.take()
        for j in range(16):
            t1 = k.mm(r.ap, yt.ap[:, j, :], WD[:, j, :], j == 0, j == 15, r.free, te, tw[2], sig=(j == 15))
        yt.done(t1)

        def add(z, *w):
            t2 = k.v_stt(z, r.ap, m[:, 6:7], k.X[:, i, :], ALU.mult, ALU.add, tf, *w, k.xtok[i])
            r.done(t2)
            return t2
        k.ln(i, add, t1)

    pipeline(NT, [(0, a), (1, b), (2, c), (3, d)])
    k.ln_flush()


def l1_attn(k):
    nc = k.nc
    k.phase("l1attn")
    k.off = k.base
    ins = k.ins
    xt_off = k.off
    XT = k.alloc([4, 2048])
    YT1, YT2 = k.alloc([2, 2048]), k.alloc([2, 2048])
    BD = k.alloc([2, 192])
    BP = k.alloc([2, 256])
    PM = k.alloc([P])
    CW = k.alloc([2, 4, 8])
    LB = k.alloc([3, 512])
    mark = k.off
    Q = Ring([k.alloc([8, 8, 24]) for _ in range(2)])
    PR = Ring([k.alloc([4096]) for _ in range(2)])
    S = Ring([k.alloc([8, 8, 8]) for _ in range(2)])
    AA = Ring([k.alloc([8, 8, 8])])
    A2 = Ring([k.alloc([8, 16, 8]) for _ in range(1)])
    LE = Ring([k.alloc([2, 8, 8, 8]) for _ in range(1)])
    mz = Ring([k.alloc([3, 64]) for _ in range(2)])
    tc = [k.dma(BD, ins["L1_bd"]), k.dma(BP, ins["L1_bp"]), k.dma(CW, ins["L1_cw"]), k.dma(LB, ins["L1_lb"])]
    R = Ring([k.bank(j)[:, 0, :] for j in range(4)])
    R4 = Ring([k.bank(4, 4)])
    SCL = float(8) ** -0.5

    tpm = k.dma(PM, ins["c_perm"])
    XV = XT.rearrange("p k (l r) -> p (k l) r", l=4)
    for i in range(NT):
        r = R.take()
        for c in range(4):
            t = k.mm(r.ap[:, c * P:c * P + P], k.X[:, i, c * P:c * P + P], PM, True, True, r.free, k.xtok[i], tpm,
                     sig=(c == 3))
        col = 256 * (i // 8) + 64 * (i // 4 % 2) + 16 * (i % 4)
        dst = XV[:, :, col:col + 144].rearrange("p m (h n) -> p m h n", n=16)[:, :, 0:9:8]
        src = r.ap.rearrange("p (m h n) -> p m h n", h=2, n=16)
        t = (k.acopy if i % 2 else k.v_copy)(dst, src, t)
        r.done(t)
    txt = [k.act.last, k.dve.last]

    def group(sset, il):
        return 4 * (il % 4) + 2 * sset + il // 4

    def window(q, tq, dst, br, n):
        s, pr, mm = S.take(), PR.take(), mz.take()
        pv = pr.ap.rearrange("p (w i j c) -> p w i j c", w=8, i=8, j=8)
        tp = []
        for w in range(8):
            a = q[:, w, :, 0:8].unsqueeze(2).to_broadcast([P, 8, 8, 8])
            b = q[:, w, :, 8:16].unsqueeze(1).to_broadcast([P, 8, 8, 8])
            tp.append((k.v_tt if w % 3 else k.g_tt)(pv[:, w], a, b, ALU.mult, tq, pr.free))
        sf = s.ap.rearrange("p w i j -> p (w i) j")
        t = k.v_red(s.ap.rearrange("p w i j -> p (w i j)"), pr.ap.rearrange("p (s c) -> p s c", c=8), ALU.add, tp, s.free)
        m, z, r = (mm.ap[:, j, :] for j in range(3))
        t = k.v_red(m, sf, ALU.max, t, mm.free)
        t = k.v_tt(sf, sf, m.unsqueeze(2).to_broadcast([P, 64, 8]), ALU.subtract, t)
        te = k.activ(sf, sf, ACT.Exp, t, scale=SCL)
        t = k.v_red(z, sf, ALU.add, te)
        tr = k.v_recip(r, z, t)
        pv = pr.ap.rearrange("p (w i c j) -> p w i c j", w=8, i=8, c=8)
        tp = []
        for w in range(8):
            a = s.ap[:, w].unsqueeze(2).to_broadcast([P, 8, 8, 8])
            b = q[:, w, :, 16:24].rearrange("p j c -> p c j").unsqueeze(1).to_broadcast([P, 8, 8, 8])
            tp.append((k.v_tt if w % 3 else k.g_tt)(pv[:, w], a, b, ALU.mult, te, t))
        s.done(tr, tp)
        aa = AA.take()
        t = k.v_red(aa.ap.rearrange("p w i c -> p (w i c)"), pr.ap.rearrange("p (s c) -> p s c", c=8), ALU.add, tp, aa.free)
        pr.done(t)
        t = k.v_tt(aa.ap.rearrange("p w i c -> p (w i) c"), aa.ap.rearrange("p w i c -> p (w i) c"),
                   r.unsqueeze(2).to_broadcast([P, 64, 8]), ALU.mult, t, tr)
        mm.done(t)
        le = LE.take()
        l0, l1 = le.ap[:, 0], le.ap[:, 1]
        v = q[:, :, :, 16:24]

        def cw(j, ni):
            return CW[:, br, j, :].unsqueeze(1).unsqueeze(1).to_broadcast([P, 1, ni, 8])

        tl = []
        for w in range(8):
            t1 = k.g_tt(l0[:, w:w + 1], v[:, w:w + 1], cw(1, 8), ALU.mult, tq, le.free, tc)
        g = t1
        tl = []
        for w in range(8):
            tl.append(k.g_tt(l1[:, w:w + 1, 1:8], v[:, w:w + 1, 0:7], cw(0, 7), ALU.mult, tq, le.free))
        t1 = k.g_tt(l0[:, :, 1:8], l0[:, :, 1:8], l1[:, :, 1:8], ALU.add, tl, g)
        tl = []
        for w in range(8):
            tl.append(k.g_tt(l1[:, w:w + 1, 0:7], v[:, w:w + 1, 1:8], cw(2, 7), ALU.mult, t1))
        t1 = k.g_tt(l0[:, :, 0:7], l0[:, :, 0:7], l1[:, :, 0:7], ALU.add, tl, t1)
        for w in range(8):
            t2 = k.g_tt(l1[:, w:w + 1], aa.ap[:, w:w + 1], cw(3, 8), ALU.add, t, t1)
        aa.done(t2)
        t3 = k.g_tt(dst, l0 if n is None else l0.rearrange("p w i c -> p i w c"),
                    l1 if n is None else l1.rearrange("p w i c -> p i w c"), ALU.add, t2, t1)
        le.done(t3)
        return t3

    ty = []
    for u in range(8):
        q = Q.take()
        tq = []
        for t2 in range(2):
            i = 2 * u + t2
            for c2 in range(2):
                r = R.take()
                for c in range(2):
                    t = k.mm(r.ap[:, 192 * c:192 * c + 192], XT[:, 2 * c2 + c, i * P:i * P + P], BD[:, 0, :], True, True,
                             r.free, txt, tc, sig=(c == 1))
                w0 = 4 * t2 + 2 * c2
                tq.append(k.acopy(q.ap[:, w0:w0 + 2], r.ap[:, 0:384].rearrange("p (w i c) -> p w i c", w=2, i=8), t, q.free))
                r.done(tq[-1])
        a2 = A2.take()
        dst = a2.ap.rearrange("p a b c -> p (a b c)")[:, 0:512].rearrange("p (w i c) -> p w i c", w=8, i=8)
        td = window(q.ap, tq, dst, 0, None)
        q.done(td, k.dve.last)
        for t2 in range(2):
            i = 2 * u + t2
            r = R.take()
            for h in range(2):
                t = k.tr(r.ap[:, h * P:h * P + P], a2.ap.rearrange("p a b c -> p (a b c)")[:, 256 * t2 + 128 * h:256 * t2 + 128 * h + 128],
                         r.free, td, sig=(h == 1))
            te = k.acopy(YT1[:, :, i * P:i * P + P], r.ap[:, 0:256].rearrange("p (h n) -> p h n", h=2), t)
            r.done(te)
            ty.append(te)
        a2.done(t)
    for sset in range(2):
        for half in range(2):
            a2 = A2.take()
            for c2 in range(2):
                c = 2 * half + c2
                q = Q.take()
                r = R4.take()
                tq = []
                for il in range(8):
                    gi = group(sset, il) * P
                    col = XT[:, c, gi:gi + P]
                    t = k.mm(r.ap[:, il // 2, 192 * (il % 2):192 * (il % 2) + 192], col, BD[:, 1, :], True, True,
                             r.free, txt, tc, sig=(il % 2 == 1))
                    if il % 2:
                        src = r.ap[:, il // 2, 0:384].rearrange("p (i w c) -> p w i c", i=2, w=8)
                        tq.append(k.acopy(q.ap[:, :, il - 1:il + 1, :].rearrange("p w i c -> p i w c"),
                                          src.rearrange("p w i c -> p i w c"), t, q.free))
                r.done(*tq)
                dst = a2.ap[:, :, 8 * c2:8 * c2 + 8, :]
                td = window(q.ap, tq, dst, 1, 1)
                q.done(td, k.dve.last)
            for q4 in range(2):
                r = R.take()
                for j in range(4):
                    il = 4 * q4 + j
                    t = k.tr(r.ap[:, j * P:j * P + P], a2.ap[:, il].rearrange("p w c -> p (w c)"), r.free, td, sig=(j == 3))
                gi = group(sset, 4 * q4) * P
                te = k.acopy(YT2[:, half, :].rearrange("p (l n) -> p l n", l=4)[:, :, gi:gi + P],
                             r.ap.rearrange("p (l n) -> p l n", l=4), t)
                ty.append(te)
                r.done(te)
            a2.done(t)
    k.off = mark
    start = [k.dve.last, k.act.last, k.pool.last, k.pe.last]
    TN = k.alloc([16, 16, 32])
    Y = Ring([k.alloc([512]) for _ in range(3)], start)
    Z = Ring([k.alloc([512]) for _ in range(3)], start)
    sm = Ring([k.alloc([4, 32]) for _ in range(3)], start)
    RB = Ring([k.bank(j, 2) for j in (0, 2, 4, 6)])
    for s in RB.free:
        s.extend(start)
    tn = []
    st = [dict() for _ in range(16)]

    def a(rl):
        s = st[rl]
        r = s["r"] = RB.take()
        c0 = 512 * (rl // 4) + rl % 4
        c1 = c0 + 509
        for h in range(2):
            o = r.ap[:, 0, 256 * h:256 * h + 256]
            k.mm(o, YT1[:, h, c0:c1:4], BP[:, 0, :], True, False, r.free, ty)
            t = k.mm(o, YT2[:, h, c0:c1:4], BP[:, 1, :], False, True, sig=(h == 1))
        for c in range(4):
            tt = k.tr(r.ap[:, 1, c * P:c * P + P], XT[:, c, c0:c1:4], sig=(c == 3))
        y, z, m = Y.take(), Z.take(), sm.take()
        s["y"], s["z"], s["m"] = y, z, m
        y3 = y.ap.rearrange("p (x c) -> p x c", c=16)
        z3 = z.ap.rearrange("p (x c) -> p x c", c=16)
        t = k.v_tt(y.ap, r.ap[:, 0, :], LB[:, 0, :], ALU.add, t, y.free)
        t = k.v_red(m.ap[:, 0, :], y3, ALU.add, t, m.free)
        t = k.v_ts(m.ap[:, 0, :], m.ap[:, 0, :], 1.0 / 16, None, ALU.mult, None, t)
        t = k.v_tt(y3, y3, m.ap[:, 0, :].unsqueeze(2).to_broadcast([P, 32, 16]), ALU.subtract, t)
        t = k.activ(z.ap, y.ap, ACT.Square, t, z.free)
        t = k.v_red(m.ap[:, 1, :], z3, ALU.add, t)
        t = k.g_ts(m.ap[:, 2, :], m.ap[:, 1, :], 1.0 / 16, 1e-5, ALU.mult, ALU.add, t)
        s["t"] = k.g_tt(m.ap[:, 3, :], m.ap[:, 2, :], k.nhalf, ALU.pow, t)
        s["tt"] = tt

    def b(rl):
        s = st[rl]
        y, z, m, r = s["y"], s["z"], s["m"], s["r"]
        y3 = y.ap.rearrange("p (x c) -> p x c", c=16)
        t = k.v_tt(y3, y3, m.ap[:, 3, :].unsqueeze(2).to_broadcast([P, 32, 16]), ALU.mult, s["t"])
        m.done(t)
        t = k.g_tt(y.ap, y.ap, LB[:, 1, :], ALU.mult, t)
        t = k.g_tt(z.ap, y.ap, LB[:, 2, :], ALU.add, t)
        y.done(t)
        t = k.v_tt(TN[:, :, rl, :].rearrange("p c x -> p x c"), z.ap.rearrange("p (x c) -> p x c", c=16),
                   r.ap[:, 1, :].rearrange("p (x c) -> p x c", c=16), ALU.add, t, s["tt"])
        z.done(t)
        r.done(t)
        tn.append(t)

    pipeline(16, [(0, a), (1, b)])
    OUT = k.view(xt_off, [NT, 512])
    td = []
    for p8 in range(8):
        sset, lh, b2 = p8 // 4, p8 // 2 % 2, p8 % 2
        bb = 2 * sset + b2
        for c4 in range(4):
            src = TN[16 * p8:16 * p8 + 16].rearrange("p (t c) r x -> p c t (r x)", c=4)[:, c4]
            p0 = 32 * c4 + lh
            td.append(k.dma(OUT[p0:p0 + 31:2, 4 * bb:4 * bb + 4, :], src, tn, k.pe.last))
    for i in range(NT):
        k.ln(i, k.add_from(i, OUT[:, i, :], None), td)
    k.ln_flush()


def layout_rest(a, d, T, rep, f):
    for n in ("L0_ffn_up_w", "L0_ffn_down_w", "L0_ffn_expert_weight", "L0_ffn_gate_w", "L3_attn_Wq"):
        d[n] = np.asarray(a[n])
    d["L0_ffn_ln"] = rep(np.stack([np.asarray(a["L0_ffn_ln_gamma"]), np.asarray(a["L0_ffn_ln_beta"])]), P, 2, 512)
    d["L3_ffn_w1"], d["L3_ffn_w2"] = T(a["L3_ffn_w1"]), T(a["L3_ffn_w2"])
    d["L3_ffn_b1"] = T(np.asarray(a["L3_ffn_b1"]).reshape(16, P))
    d["L3_ffn_b2"] = rep(a["L3_ffn_b2"], P, 512)
    for n in ("gate", "up", "down"):
        d["L1_ffn_w_" + n] = T(a["L1_ffn_w_" + n])
    h = np.ones((1, 1), f)
    while len(h) < P:
        h = np.block([[h, h], [h, -h]]).astype(f)
    d["c_hadamard"] = h
    sel = np.zeros((P, 4, 4, P), f)
    for g in range(4):
        for r in range(3):
            for hg in range(4):
                sel[32 * g + 4 * r + hg, g, hg, :] = 1
    d["c_sel"] = sel
    for lab, names, tr in (("L2_attn", ("WQ", "WK", "WV", "WO"), True), ("L3_attn", ("q", "k", "v", "c"), False)):
        for n, o in zip(names, "qkvo"):
            w, b = (f"{lab}_{n}_w", f"{lab}_{n}_b") if tr else (f"{lab}_W{n}", f"{lab}_b{n}")
            d[f"{lab}_{o}"] = T(a[w]) if tr else np.asarray(a[w])
            d[f"{lab}_b{o}"] = T(np.asarray(a[b]).reshape(4, P)) if o in "qk" else rep(a[b], P, 512)
    d["L2_xattn_q"], d["L2_xattn_o"] = T(a["L2_xattn_Wq"]), T(a["L2_xattn_Wout"])
    kv = T(a["L2_xattn_Wkv_expand"])
    d["L2_xattn_k"], d["L2_xattn_v"] = kv[:, :512], kv[:, 512:]
    d["ctx_T"] = np.ascontiguousarray(np.asarray(a["ctx_512"]).transpose(2, 0, 1))
    d["L3_xattn_W_k"] = T(a["L3_xattn_W_k"])
    d["L3_xattn_b_k"] = np.asarray(a["L3_xattn_b_k"]).reshape(P, 1)
    d["L3_xattn_ln"] = rep(np.stack([np.asarray(a["L3_xattn_ln_gamma"]), np.asarray(a["L3_xattn_ln_beta"])]), P, 2, 512)
    d["L1_xattn_W"] = np.stack([T(a["L1_xattn_Wq"]), T(a["L1_xattn_Wk"])], 1)
    pm = np.zeros((P, P), f)
    q = np.arange(P)
    pm[q, 32 * (q // 4 % 4) + 16 * (q // 16 % 2) + 4 * (q // 32) + q % 4] = 1
    d["c_perm"] = pm
    d["L1_gamma"] = rep(np.asarray(a["L1_xattn_gamma_raw"]).reshape(1, 1), P, 1)
    w = np.asarray(a["L1_attn_qkv_w"])
    bd = np.zeros((8, 16, 2, 8, 24), f)
    pw = np.asarray(a["L1_attn_proj_w"])
    bp = np.zeros((16, 8, 2, 16, 16), f)
    for br in range(2):
        for x in range(8):
            for j in range(3):
                bd[x, :, br, x, 8 * j:8 * j + 8] = w[:, 16 * j + 8 * br:16 * j + 8 * br + 8]
        for x in range(16):
            bp[x, :, br, x, :] = pw[8 * br:8 * br + 8]
    d["L1_bd"] = bd.reshape(P, 2, 192)
    d["L1_bp"] = bp.reshape(P, 2, 256)
    c0, c1 = np.asarray(a["L1_attn_conv_w0"])[:, 0], np.asarray(a["L1_attn_conv_w1"])[:, 0]
    cw = np.stack([np.stack([c0[:, 1, 0], c0[:, 1, 1], c0[:, 1, 2], np.asarray(a["L1_attn_conv_b0"])]),
                   np.stack([c1[:, 0, 1], c1[:, 1, 1], c1[:, 2, 1], np.asarray(a["L1_attn_conv_b1"])])])
    d["L1_cw"] = rep(cw, P, 2, 4, 8)
    lb = np.stack([np.tile(np.asarray(a["L1_attn_" + n]), 32) for n in ("proj_b", "ln_w", "ln_b")])
    d["L1_lb"] = rep(lb, P, 3, 512)
    d["L2_ffn_gate_weight"] = T(a["L2_ffn_gate_weight"])
    gu = np.concatenate([np.asarray(a["L2_ffn_w_gate"]), np.asarray(a["L2_ffn_w_up"])], axis=2)
    d["L2_ffn_gu"] = gu.reshape(NE, 4, P, 384).transpose(0, 2, 1, 3).reshape(NE, P, 1536)
    d["L2_ffn_dn"] = np.asarray(a["L2_ffn_w_down"]).reshape(NE, 2, 96, 512).transpose(0, 2, 1, 3).reshape(NE, 96, 1024)
    sl = np.zeros((P, NB, 2), np.uint32)
    sl[:, :, 0] = 2048 + np.arange(P)[:, None]
    d["c_slots"] = sl.reshape(P, 2 * NB)
    d["c_tokens"] = (np.arange(P)[:, None] + P * np.arange(NT)[None, :]).astype(np.uint32)
    d["c_tri"] = np.stack([np.triu(np.ones((P, P), f), 1), np.ones((P, P), f)], 1)
    d["c_blocks"] = np.concatenate([np.arange(P)[:, None] + np.array([[0, P]]), rep(np.arange(16)[None] * 128, P, 16)],
                                   1).astype(f)
    for n in ("L3_attn_Wq",):
        d.pop(n)
NB = 191
NE = 64


def l2_ffn(k):
    nc = k.nc
    k.phase("l2ffn")
    k.off = k.base
    ins = k.ins
    XD = nc.dram_tensor("moe_x", [2176, 512], F32, kind="Internal").ap()
    YD = nc.dram_tensor("moe_y", [2176, 512], F32, kind="Internal").ap()
    TW = nc.dram_tensor("moe_slots", [P * NB, 2], U32, kind="Internal").ap()
    EB = nc.dram_tensor("moe_experts", [256], I32, kind="Internal").ap()
    TB = k.alloc([NB, 2])
    ER = k.alloc([256])
    GU = Ring([k.alloc([4, 384]) for _ in range(4)])
    DN = Ring([k.alloc([2, 512]) for _ in range(6)])
    XG = Ring([k.alloc([512]) for _ in range(4)])
    XT = Ring([k.alloc([4, P]) for _ in range(2)])
    SG = Ring([k.alloc([192]) for _ in range(2)])
    HH = Ring([k.alloc([192]) for _ in range(2)])
    HT = Ring([k.alloc([2, P]) for _ in range(2)])
    YG = Ring([k.alloc([512]) for _ in range(3)])
    end = k.off
    WR = k.alloc([4, NE])
    LX = k.alloc([4, P])
    RW = k.alloc([NT, NE])
    MM = k.alloc([NT, NE])
    C = k.alloc([NT + 1, NE])
    TRI = k.alloc([2, P])
    S8 = k.alloc([NT, 8])
    W8 = k.alloc([NT, 8])
    IX = k.alloc([3, NT * 8])
    PAY = k.alloc([NT * 8, 2])
    TOK = k.alloc([NT])
    SC = k.alloc([4, NE])
    sm = k.alloc([NT, 16])
    PF = k.alloc([3, NE])
    IO = k.alloc([2 + 16])
    BIG = k.alloc([NE, 16])
    EX = k.alloc([2, 2])
    ZERO = k.alloc([4, 512])
    R = Ring([k.bank(j)[:, 0, :] for j in range(8)])
    k.pool.wait()
    tz = k.pool.sig(nc.gpsimd.memset(ZERO, 0.0))
    tz2 = k.pool.sig(nc.gpsimd.memset(C[:, 0, :], 0.0))
    yv = YD.rearrange("(t p) d -> p t d", p=P)
    xv = XD.rearrange("(t p) d -> p t d", p=P)
    td = [k.dma(yv[:, 4 * j:min(4 * j + 4, 17), :], ZERO[:, 0:min(4, 17 - 4 * j), :], tz) for j in range(5)]
    tx = [k.dma(xv[:, 16, :], ZERO[:, 0, :], tz)]
    tx += [k.dma(xv[:, 4 * j:4 * j + 4, :], k.X[:, 4 * j:4 * j + 4, :], k.xtok) for j in range(4)]
    tt = k.dma(TW.rearrange("(p a) c -> p (a c)", p=P), ins["c_slots"])
    tc = [k.dma(WR, rows(ins["L2_ffn_gate_weight"])), k.dma(TRI, ins["c_tri"]), k.dma(IO, ins["c_blocks"]),
          k.dma(TOK.bitcast(U32), ins["c_tokens"])]
    for i in range(NT):
        tl = k.x_to_xt(i, R, LX, k.pe.last, eng=0)
        r = R.take()
        for kk in range(4):
            t = k.mm(r.ap[:, 0:NE], LX[:, kk, :], WR[:, kk, :], kk == 0, kk == 3, r.free, tl, tc, sig=(kk == 3))
        m = sm[:, i, :]
        t = k.v_red(m[:, 0:1], r.ap[:, 0:NE], ALU.max, t, negate=True)
        t = k.activ(SC[:, 0, :], r.ap[:, 0:NE], ACT.Exp, t, k.dve.last, bias=m[:, 0:1], accum=m[:, 1:2])
        r.done(t)
        t = k.v_recip(m[:, 2:3], m[:, 1:2], t)
        t = k.v_ts(SC[:, 1, :], SC[:, 0, :], m[:, 2:3], None, ALU.mult, None, t)
        k.dve.wait(t)
        t = k.dve.sig(nc.vector.max(m[:, 3:11], SC[:, 1, :]))
        k.dve.wait(t)
        t = k.dve.sig(nc.vector.match_replace(SC[:, 2, :], m[:, 3:11], SC[:, 1, :], -1.0))
        t = k.v_red(m[:, 11:12], m[:, 3:11], ALU.add, t)
        t = k.v_recip(m[:, 12:13], m[:, 11:12], t)
        tm = k.v_tt(MM[:, i, :], SC[:, 2, :], SC[:, 1, :], ALU.not_equal, t)
        trw = k.v_ts(RW[:, i, :], SC[:, 1, :], m[:, 12:13], None, ALU.mult, None, t)
        tcum = k.v_tt(C[:, i + 1, :], C[:, i, :], MM[:, i, :], ALU.add, tm, tz2, k.dve.last)

    r = R.take()
    t = k.mm(r.ap[:, 0:NE], TRI[:, 1, :], C[:, NT, :], True, True, r.free, tc, tcum, sig=True)
    lim = IO[:, 2:18].unsqueeze(1).to_broadcast([P, NE, 16])
    t = k.v_copy(PF[:, 0, :], r.ap[:, 0:NE], t)
    r.done(t)
    t = k.v_tt(BIG, PF[:, 0, :].unsqueeze(2).to_broadcast([P, NE, 16]), lim, ALU.is_gt, t, tc)
    t = k.v_red(PF[:, 1, :], BIG, ALU.add, t)
    r = R.take()
    t = k.tr(r.ap[0:NE, 0:P], PF[:, 1, :], r.free, t, sig=True)
    t = k.v_copy(BIG.rearrange("p a b -> p (a b)")[0:NE, 0:P], r.ap[0:NE, 0:P], t)
    r.done(t)
    r = R.take()
    t = k.mm(r.ap[:, 0:NE], BIG.rearrange("p a b -> p (a b)")[0:NE, 0:P], TRI[0:NE, 0, 0:NE], True, True, r.free, t,
             sig=True)
    t = k.v_copy(PF[:, 2, :], r.ap[:, 0:NE], t)
    r.done(t)
    for j in range(2):
        t1 = k.v_ts(BIG.rearrange("p a b -> p (a b)")[:, 0:NE], PF[:, 2, :], IO[:, j:j + 1], None, ALU.is_le, None, t,
                    k.dve.last, k.pe.last)
        t1 = k.v_red(EX[:, 0, j:j + 1], BIG.rearrange("p a b -> p (a b)")[:, 0:NE], ALU.add, t1)
    t1 = k.v_ts(EX[:, 1, :].bitcast(I32), EX[:, 0, :], -1.0, None, ALU.add, None, t1)
    t1 = k.dma(EB.rearrange("(p j) -> p j", p=P), EX[:, 1, :].bitcast(I32), t1)
    te = k.dma(ER[0:1].bitcast(I32), EB.rearrange("(a n) -> a n", a=1), t1)
    tp = k.v_ts(PF[:, 2, :], PF[:, 2, :], 128.0, 1.0, ALU.mult, ALU.add, t1)
    for i in range(NT):
        r = R.take()
        k.mm(r.ap[:, 0:NE], TRI[:, 0, :], MM[:, i, :], True, False, r.free, tcum)
        t = k.mm(r.ap[:, 0:NE], TRI[:, 1, :], C[:, i, :], False, True, sig=True)
        t = k.v_tt(SC[:, 0, :], r.ap[:, 0:NE], PF[:, 2, :], ALU.add, t, tp, k.dve.last)
        r.done(t)
        t = k.v_tt(SC[:, 1, :], SC[:, 0, :], MM[:, i, :], ALU.mult, t)
        k.dve.wait(t)
        t = k.dve.sig(nc.vector.max(S8[:, i, :], SC[:, 1, :]))
        b8 = BIG.rearrange("p a b -> p (a b)")[:, 0:8 * NE].rearrange("p (j e) -> p j e", e=NE)
        t = k.v_tt(b8, SC[:, 1, :].unsqueeze(1).to_broadcast([P, 8, NE]),
                   S8[:, i, :].unsqueeze(2).to_broadcast([P, 8, NE]), ALU.is_equal, t)
        t = k.v_tt(b8, b8, RW[:, i, :].unsqueeze(1).to_broadcast([P, 8, NE]), ALU.mult, t, trw)
        tw8 = k.v_red(W8[:, i, :], b8, ALU.add, t)
    s8 = S8.rearrange("p a b -> p (a b)")
    t = k.v_ts(IX[:, 0, :].bitcast(I32), s8, -1.0, None, ALU.add, None, tw8)
    t1 = k.v_ts(IX[:, 1, :].bitcast(I32), IX[:, 0, :].bitcast(I32), 127, None, ALU.bitwise_and, None, t)
    t2 = k.v_ts(IX[:, 2, :].bitcast(I32), IX[:, 0, :].bitcast(I32), 7, None, ALU.logical_shift_right, None, t)
    t = k.v_ts(IX[:, 0, :], IX[:, 1, :].bitcast(I32), float(NB), None, ALU.mult, None, t1, t2)
    t = k.v_tt(IX[:, 1, :].bitcast(U32), IX[:, 0, :], IX[:, 2, :].bitcast(I32), ALU.add, t)
    pw = PAY.rearrange("p (i j) c -> p i j c", j=8)
    t3 = k.v_copy(pw[:, :, :, 0].bitcast(U32), TOK.bitcast(U32).unsqueeze(2).to_broadcast([P, NT, 8]), tc)
    t4 = k.v_copy(PAY[:, :, 1], W8.rearrange("p a b -> p (a b)"))
    ng = 8
    gs = [nc.alloc_semaphore(f"moe_sc{j}") for j in range(ng)]
    k.pool.wait(tt, t, t3, t4)
    for n in range(NT * 8):
        s = gs[n % ng]
        if n >= ng:
            k.pool.wait((s, 16 * (n // ng)))
        nc.gpsimd.indirect_dma_start(TW, bass.IndirectOffsetOnAxis(ap=IX[:, 1, n:n + 1].bitcast(U32), axis=0),
                                     PAY[:, n, :].bitcast(U32), None).then_inc(s, 16)
    tsc = [(s, 16 * (NT * 8 // ng)) for s in gs]
    ttb = k.dma(TB.bitcast(U32), TW.rearrange("(p a) c -> p a c", p=P), tsc)

    wg = ins["L2_ffn_gu"]
    wd = ins["L2_ffn_dn"]
    xs = [nc.alloc_semaphore(f"moe_g{j}") for j in range(4)]
    ys = nc.alloc_semaphore("moe_y")
    st = [dict() for _ in range(NB)]
    k.sp.wait(te)

    def load(n):
        s = st[n]
        s["g"], s["d"] = GU.take(), DN.take()
        c = n % P * 2 + n // P
        e = nc.sync.value_load(ER[0:1, c:c + 1].bitcast(I32), min_val=0, max_val=NE - 1)
        s["tg"] = k.dma(s["g"].ap.rearrange("p a b -> p (a b)"), wg[bass.ds(e, 1)].rearrange("a p n -> p (a n)"), s["g"].free)
        s["td"] = k.dma(s["d"].ap[0:96].rearrange("p a b -> p (a b)"), wd[bass.ds(e, 1)].rearrange("a p n -> p (a n)"),
                        s["d"].free)

    def gather(n):
        s = st[n]
        x = s["x"] = XG.take()
        k.pool.wait(x.free, tx, ttb, (xs[n % 4], 16 * (n // 4)) if n >= 4 else None)
        nc.gpsimd.indirect_dma_start(x.ap, None, XD, bass.IndirectOffsetOnAxis(ap=TB[:, n, 0:1].bitcast(U32), axis=0)
                                     ).then_inc(xs[n % 4], 16)
        s["tx"] = (xs[n % 4], 16 * (n // 4 + 1))

    def a(n):
        s = st[n]
        r = R.take()
        bb = r.ap.rearrange("p (k n) -> p k n", k=4)
        for kk in range(4):
            t = k.tr(bb[:, kk, :], s["x"].ap[:, kk * P:kk * P + P], r.free, s["tx"], sig=(kk == 3))
        s["x"].done(t)
        x = s["xt"] = XT.take()
        s["txt"] = k.acopy(x.ap, bb, t, x.free)
        r.done(s["txt"])

    def up(n):
        s = st[n]
        r = R.take()
        for kk in range(4):
            t = k.mm(r.ap[:, 0:384], s["xt"].ap[:, kk, :], s["g"].ap[:, kk, :], kk == 0, kk == 3, r.free, s["txt"], s["tg"],
                     sig=(kk == 3))
        s["xt"].done(t)
        s["g"].done(t)
        g = SG.take()
        t1 = k.activ(g.ap, r.ap[:, 0:192], ACT.Silu, t, g.free)
        h = s["h"] = HH.take()
        s["th"] = k.v_stt(h.ap, r.ap[:, 192:384], TB[:, n, 1:2], g.ap, ALU.mult, ALU.mult, t1, h.free, ttb)
        g.done(s["th"])
        r.done(s["th"])

    def b(n):
        s = st[n]
        r = R.take()
        for c in range(2):
            t = k.tr(r.ap[0:96, c * P:c * P + P], s["h"].ap[:, 96 * c:96 * c + 96], r.free, s["th"], sig=(c == 1))
        s["h"].done(t)
        h = s["ht"] = HT.take()
        s["tht"] = k.v_copy(h.ap[0:96], r.ap[0:96, 0:256].rearrange("p (c n) -> p c n", c=2), t, h.free)
        r.done(s["tht"])

    def down(n):
        s = st[n]
        r = R.take()
        for c in range(2):
            t = k.mm(r.ap, s["ht"].ap[0:96, c, :], s["d"].ap[0:96, c, :], c == 0, c == 1, r.free, s["tht"], s["td"],
                     sig=(c == 1))
        s["ht"].done(t)
        s["d"].done(t)
        y = s["y"] = YG.take()
        s["ty"] = k.v_copy(y.ap, r.ap, t, y.free)
        r.done(s["ty"])

    def add(n):
        s = st[n]
        k.pool.wait(s["ty"], td, (ys, 16 * n) if n else None)
        nc.gpsimd.indirect_dma_start(YD, bass.IndirectOffsetOnAxis(ap=TB[:, n, 0:1].bitcast(U32), axis=0), s["y"].ap, None,
                                     compute_op=ALU.add).then_inc(ys, 16)
        s["y"].done((ys, 16 * n + 16))

    pipeline(NB, [(0, load), (1, gather), (2, a), (3, up), (4, b), (5, down), (6, add)])
    YL = Ring([k.view(end, [4, 512]), k.view(end + 2048, [4, 512])])
    for j in range(4):
        y = YL.take()
        t = k.dma(y.ap, yv[:, 4 * j:4 * j + 4, :], y.free, (ys, 16 * NB), k.pe.last, k.dve.last, k.act.last)
        for t4 in range(4):
            k.ln(4 * j + t4, k.add_from(4 * j + t4, y.ap[:, t4, :], None), t)
        k.ln_flush()
        y.done(k.dve.last)
def build(nc, ins, out, layers):
    k = K(nc, ins, out)
    k.start()
    table = [l0_attn, l0_xattn, l0_ffn, l1_attn, l1_xattn, l1_ffn, l2_attn, l2_xattn, l2_ffn,
             l3_attn, l3_xattn, l3_ffn]
    for n in layers:
        table[n](k)
    o = out.rearrange("b (t p) d -> p (b t) d", p=P)
    ts = [k.dma(o[:, 4 * b:4 * b + 4, :], k.X[:, 4 * b:4 * b + 4, :], k.xtok) for b in range(4)]
    k.sp.wait(ts)


def layout(a):
    f = np.float32

    def T(x):
        return np.ascontiguousarray(np.asarray(x).T)

    def rep(x, *shape):
        return np.ascontiguousarray(np.broadcast_to(np.asarray(x), shape))

    d = {}
    d["x"] = np.asarray(a["x"])
    d["ctx_512"] = np.asarray(a["ctx_512"])
    ident = np.eye(P, dtype=f)
    i, j = np.arange(P)[None, :], np.arange(P)[:, None]
    d["c_ident"] = ident
    d["c_masks"] = np.stack([ident, np.where(i > j, f(NEG), f(0)), np.where(j > i, f(NEG), f(0))], 1).astype(f)
    d["c_iota"] = np.stack([i + 1 + 0 * j, np.where(i >= j, i - j, 1e30), 127 - j + 0 * i], 1).astype(f)
    d["c_block"] = (i // 32 == j // 32).astype(f)
    s = np.asarray(a["L0_attn_slope_rate"]).reshape(16)
    d["slope_k"] = rep(s, P, 16)
    d["slope_q"] = np.ascontiguousarray(np.repeat(s.reshape(4, 4).T, 32, axis=0))
    for n in ("L0_attn_W_qkvu", "L0_attn_W_out"):
        d[n] = T(a[n])
    layout_rest(a, d, T, rep, f)
    return d


def kernel(**inputs):
    import concourse.bacc as _bacc
    from concourse.bass_utils import run_bass_kernel_spmd as _run

    nc = _bacc.Bacc("TRN2", target_bir_lowering=False, num_devices=1)
    arrays, ins = {}, {}
    for name, v in layout(inputs).items():
        v = np.ascontiguousarray(v)
        arrays[f"in_{name}"] = v
        ins[name] = nc.dram_tensor(f"in_{name}", v.shape, mybir.dt.from_np(v.dtype), kind="ExternalInput").ap()
    out = nc.dram_tensor("out_0", (4, 512, 512), F32, kind="ExternalOutput").ap()
    build(nc, ins, out, range(12))
    r = _run(nc, [arrays], core_ids=[0])
    return r.results[0]["out_0"]
```

```python
import numpy as np
import concourse.bass as bass
from concourse import mybir

F32 = mybir.dt.float32
BF16 = mybir.dt.bfloat16
F32R = mybir.dt.float32r
U32 = mybir.dt.uint32
I32 = mybir.dt.int32
ALU = mybir.AluOpType
ACT = mybir.ActivationFunctionType
AX = mybir.AxisListType
P = 128
NT = 16
D = 512
NEG = -1.0e30


class Eng:

    def __init__(self, nc, name, eng):
        self.nc, self.name, self.eng = nc, name, eng
        self.seen = {}
        self.last = None

    def phase(self, label):
        self.sem = self.nc.alloc_semaphore(f"{self.name}_{label}")
        self.count = 0

    def wait(self, *toks):
        for t in toks:
            if t is None:
                continue
            if isinstance(t, list):
                self.wait(*t)
                continue
            sem, val = t
            if self.seen.get(sem.name, 0) >= val:
                continue
            self.seen[sem.name] = val
            self.eng.wait_ge(sem, val)

    def sig(self, ins):
        ins.then_inc(self.sem, 1)
        self.count += 1
        self.last = (self.sem, self.count)
        return self.last


class Slot:
    def __init__(self, ring, i, ap, free):
        self.ring, self.i, self.ap, self.free = ring, i, ap, free

    def done(self, *toks):
        self.ring.free[self.i] = list(toks)
        self.ring.held[self.i] = False


class Ring:

    def __init__(self, bufs, free=None):
        self.bufs, self.n = bufs, 0
        self.free = [list(free or []) for _ in bufs]
        self.held = [False for _ in bufs]

    def take(self):
        i = self.n % len(self.bufs)
        self.n += 1
        assert not self.held[i], "a buffer is taken before its last user is named"
        self.held[i] = True
        return Slot(self, i, self.bufs[i], self.free[i])


class K:
    def __init__(self, nc, ins, out):
        self.nc, self.ins, self.out = nc, ins, out
        self.pe = Eng(nc, "pe", nc.tensor)
        self.act = Eng(nc, "act", nc.scalar)
        self.dve = Eng(nc, "dve", nc.vector)
        self.pool = Eng(nc, "pool", nc.gpsimd)
        self.sp = Eng(nc, "sp", nc.sync)
        self.NDS = 24
        self.dsem = [nc.alloc_semaphore(f"dma{i}") for i in range(self.NDS)]
        self.dcount = [0] * self.NDS
        self.dn = 0
        self.W = 51800
        self.arena_at = (nc.sbuf_base + 31) // 32 * 32
        self.arena = nc.alloc_sbuf_tensor("arena", [P, self.W], F32)
        self.ps = nc.alloc_psum_tensor("ps", [P, 8, 512], F32)
        self.off = 0
        self.nr = 0
        self.fence_toks = []

    def alloc(self, shape, dt=F32):
        n = int(np.prod(shape))
        words = (n + 1) // 2 if dt == BF16 else n
        o = self.off = (self.off + 7) // 8 * 8
        self.off += words
        assert self.off <= self.W, f"sbuf {self.off}"
        return self.view(o, shape, dt)

    def view(self, o, shape, dt=F32):
        n = int(np.prod(shape))
        words = n if dt != BF16 else n // 2
        a = self.arena[:, o:o + words]
        if dt != F32:
            a = a.bitcast(dt)
        if len(shape) > 1:
            names = "abcde"[:len(shape)]
            kw = {names[i]: shape[i] for i in range(1, len(shape))}
            a = a.rearrange(f"p ({' '.join(names)}) -> p {' '.join(names)}", **kw)
        return a

    def rview(self, o, shape):
        n = int(np.prod(shape))
        self.nr = self.nr + 1
        a = self.nc.alloc_sbuf_tensor_at(f"r{self.nr}", [P, n], F32R, offset=self.arena_at + 4 * o)[:, :]
        if len(shape) > 1:
            names = "abcde"[:len(shape)]
            kw = {names[i]: shape[i] for i in range(1, len(shape))}
            a = a.rearrange(f"p ({' '.join(names)}) -> p {' '.join(names)}", **kw)
        return a

    def ralloc(self, shape):
        self.alloc(shape)
        return self.rview(self.off - int(np.prod(shape)), shape)

    def bank(self, i, n=1):
        return self.ps[:, i:i + n, :]

    def phase(self, label):
        toks = [e.last for e in (self.pe, self.act, self.dve, self.pool) if e.last]
        for i in range(self.NDS):
            if self.dcount[i]:
                toks.append((self.dsem[i], 16 * self.dcount[i]))
        for e in (self.pe, self.act, self.dve, self.pool, self.sp):
            e.wait(*toks)
        for e in (self.pe, self.act, self.dve, self.pool):
            e.phase(label)

    def dma(self, out, in_, *w, eng=None, **kw):
        eng = eng or self.sp
        i = self.dn % self.NDS
        self.dn += 1
        if self.dcount[i]:
            eng.wait((self.dsem[i], 16 * self.dcount[i]))
        eng.wait(*w)
        eng.eng.dma_start(out, in_, **kw).then_inc(self.dsem[i], 16)
        self.dcount[i] += 1
        return (self.dsem[i], 16 * self.dcount[i])

    def mm(self, out, lhsT, rhs, start, stop, *w, sig=False, skip=True):
        self.pe.wait(*w)
        i = self.nc.tensor.matmul(out, lhsT, rhs, start=start, stop=stop, skip_group_check=skip)
        return self.pe.sig(i) if sig else None

    def tr(self, out, in_, *w, sig=False):
        self.pe.wait(*w)
        ident = self.idb if in_.dtype == BF16 else self.idf
        n = in_.shape[0]
        i = self.nc.tensor.transpose(out, in_, ident[0:n, 0:n])
        return self.pe.sig(i) if sig else None

    def activ(self, out, in_, func, *w, bias=None, scale=1.0, accum=None):
        self.act.wait(*w)
        kw = {}
        if bias is not None:
            kw["bias"] = bias
        if accum is not None:
            kw["accum_out"] = accum
        return self.act.sig(self.nc.scalar.activation(out, in_, func, scale=scale, **kw))

    def acopy(self, out, in_, *w):
        return self.activ(out, in_, ACT.Copy, *w)

    def v_copy(self, out, in_, *w):
        self.dve.wait(*w)
        return self.dve.sig(self.nc.vector.tensor_copy(out, in_))

    def v_tt(self, out, a, b, op, *w):
        self.dve.wait(*w)
        return self.dve.sig(self.nc.vector.tensor_tensor(out, a, b, op))

    def v_ts(self, out, a, s1, s2, op0, op1, *w, accum=None):
        self.dve.wait(*w)
        kw = {"accum_out": accum} if accum is not None else {}
        if op1 is None:
            return self.dve.sig(self.nc.vector.tensor_scalar(out, a, s1, None, op0))
        return self.dve.sig(self.nc.vector.tensor_scalar(out, a, s1, s2, op0, op1, **kw))

    def v_stt(self, out, a, s, b, op0, op1, *w):
        self.dve.wait(*w)
        return self.dve.sig(self.nc.vector.scalar_tensor_tensor(out=out, in0=a, scalar=s, in1=b, op0=op0, op1=op1))

    def v_red(self, out, a, op, *w, negate=False, absolute=False):
        self.dve.wait(*w)
        return self.dve.sig(self.nc.vector.tensor_reduce(out, a, AX.X, op, negate=negate,
                                                         apply_absolute_value=absolute))

    def v_recip(self, out, a, *w):
        self.dve.wait(*w)
        return self.dve.sig(self.nc.vector.reciprocal(out, a))

    def g_tt(self, out, a, b, op, *w):
        self.pool.wait(*w)
        return self.pool.sig(self.nc.gpsimd.tensor_tensor(out, a, b, op))

    def g_ts(self, out, a, s1, s2, op0, op1, *w):
        self.pool.wait(*w)
        if op1 is None:
            return self.pool.sig(self.nc.gpsimd.tensor_scalar(out, a, s1, None, op0))
        return self.pool.sig(self.nc.gpsimd.tensor_scalar(out, a, s1, s2, op0, op1))

    def g_copy(self, out, a, *w):
        self.pool.wait(*w)
        return self.pool.sig(self.nc.gpsimd.tensor_copy(out, a))

    def start(self):
        nc = self.nc
        self.X = self.alloc([NT, D])
        self.idf = self.alloc([P])
        self.idb = self.alloc([P], BF16)
        self.mq = self.alloc([P], BF16)
        self.mk = self.alloc([P], BF16)
        self.nhalf = self.alloc([32])
        self.st = self.alloc([4, 8])
        self.mv = self.alloc([4, 4])
        self.zb = Ring([self.alloc([D]) for _ in range(4)])
        self.thr = self.alloc([NT])
        self.base = self.off
        for e in (self.pe, self.act, self.dve, self.pool, self.sp):
            e.phase("start")
        c = self.ins["c_masks"]
        tc = [self.dma(self.idf, self.ins["c_ident"])]
        tmp = self.view(self.base, [3, P])
        t = self.dma(tmp, c)
        tc.append(self.v_copy(self.idb, tmp[:, 0, :], t))
        tc.append(self.v_copy(self.mq, tmp[:, 1, :], t))
        tc.append(self.v_copy(self.mk, tmp[:, 2, :], t))
        self.pool.wait()
        tc.append(self.pool.sig(nc.gpsimd.memset(self.nhalf, -0.5)))
        self.xtok = []
        self.load_x(0)
        self.ln_n = 0
        self.ln_pending = []
        self.bg = thresholds(self)
        self.early = None

    def load_x(self, b):
        t = self.dma(self.X[:, 4 * b:4 * b + 4, :], self.ins["x"][b].rearrange("(t p) d -> p t d", p=P))
        self.xtok += [t] * 4

    def background(self, n):
        for _ in range(n):
            next(self.bg, None)

    def ln_begin(self, i, add, *w):
        s = self.zb.take()
        n = self.ln_n % 4
        self.ln_n += 1
        tz = add(s.ap, *w, s.free)
        self.dve.wait(tz)
        tb = self.dve.sig(self.nc.vector.bn_stats(self.st[:, n, 0:6], s.ap))
        self.dve.wait(tb)
        ta = self.dve.sig(self.nc.vector.bn_aggr(self.mv[:, n, 0:2], self.st[:, n, 0:6]))
        t1 = self.g_ts(self.mv[:, n, 2:3], self.mv[:, n, 1:2], 1e-5, 1.0, ALU.add, ALU.mult, ta)
        t2 = self.g_tt(self.mv[:, n, 3:4], self.mv[:, n, 2:3], self.nhalf[:, 0:1], ALU.pow, t1)
        self.ln_pending.append((i, s, n, t2))

    def ln_end(self):
        i, s, n, t2 = self.ln_pending.pop(0)
        t = self.v_ts(self.X[:, i, :], s.ap, self.mv[:, n, 0:1], self.mv[:, n, 3:4],
                      ALU.subtract, ALU.mult, t2)
        s.done(t)
        self.xtok[i] = t
        return t

    def ln(self, i, add, *w, lag=1):
        self.ln_begin(i, add, *w)
        while len(self.ln_pending) > lag:
            self.ln_end()

    def ln_flush(self):
        while self.ln_pending:
            self.ln_end()

    def add_from(self, i, src, slot, *w):
        def add(z, *ww):
            t = self.v_tt(z, self.X[:, i, :], src, ALU.add, *ww, self.xtok[i])
            if slot is not None:
                slot.done(t)
            return t
        return add

    def x_to_xt(self, i, ring, dst, *w, eng=0):
        s = ring.take()
        b = s.ap.rearrange("p (k n) -> p k n", k=4)
        for k in range(4):
            t = self.tr(b[:, k, :], self.X[:, i, k * P:(k + 1) * P], s.free, self.xtok[i], sig=(k == 3))
        t = self.acopy(dst, b, t, *w) if eng == 0 else self.v_copy(dst, b, t, *w)
        s.done(t)
        return t


def pipeline(n, stages):
    top = max(lag for lag, _ in stages)
    for t in range(n + top):
        for lag, f in sorted(stages, key=lambda s: -s[0]):
            if 0 <= t - lag < n:
                f(t - lag)
def l0_attn(k):
    nc = k.nc
    k.phase("l0attn")
    k.off = k.base
    WQ = k.alloc([4, 2048])
    WO = k.alloc([4, 512])
    tw = [k.dma(WQ[:, :, 512 * j:512 * j + 512],
                k.ins["L0_attn_W_qkvu"].rearrange("(k p) n -> p k n", p=P)[:, :, 512 * j:512 * j + 512])
          for j in range(4)]
    two = k.dma(WO, k.ins["L0_attn_W_out"].rearrange("(k p) n -> p k n", p=P))
    SQ = k.alloc([4])
    SK = k.alloc([16])
    for b in range(1, 4):
        k.load_x(b)
    next(k.bg)
    IO = k.alloc([3, P])
    DT = k.alloc([16, P])
    QD = k.alloc([4, P])
    KD = k.alloc([512])
    KD16 = k.alloc([16])
    EB = k.alloc([4, P])
    BM = k.alloc([P])
    eb1 = k.alloc([4])
    ts = [k.dma(SQ, k.ins["slope_q"]), k.dma(SK, k.ins["slope_k"]), k.dma(IO, k.ins["c_iota"]),
          k.dma(BM, k.ins["c_block"])]
    for h in range(16):
        td = k.v_ts(DT[:, h, :], IO[:, 1, :], SK[:, h:h + 1], -1.0, ALU.mult, ALU.mult, ts)
    for hg in range(4):
        td = k.v_ts(QD[:, hg, :], IO[:, 0, :], SQ[:, hg:hg + 1], -1.0, ALU.mult, ALU.mult)
    td = k.v_ts(KD16, SK, IO[:, 2, 0:1], -1.0, ALU.mult, ALU.mult)
    td = k.v_ts(eb1, SQ, -128.0, None, ALU.mult, None)
    t1 = k.activ(DT, DT, ACT.Exp, td)
    t2 = k.activ(QD, QD, ACT.Exp)
    t3 = k.activ(KD16, KD16, ACT.Exp)
    t4 = k.activ(eb1, eb1, ACT.Exp)
    t5 = k.v_copy(KD.rearrange("p (h d) -> p h d", d=32), KD16.unsqueeze(2).to_broadcast([P, 16, 32]), t3, td)
    for hg in range(4):
        t6 = k.v_ts(EB[:, hg, :], BM, eb1[:, hg:hg + 1], None, ALU.mult, None, t4, td)
    dec = [t1, t2, t5, t6]

    R = Ring([k.bank(j)[:, 0, :] for j in range(3)])
    k.bgring = R
    S4 = Ring([k.bank(3 + j)[:, 0, :] for j in range(4)])
    OB = Ring([k.bank(7)[:, 0, :]])
    XT = Ring([k.alloc([4, P]) for _ in range(2)])
    Qr, Kr = (Ring([k.alloc([512]) for _ in range(1)]) for _ in range(2))
    Vr, Ur = (Ring([k.alloc([512]) for _ in range(3)]) for _ in range(2))
    QTr = Ring([k.alloc([4, 4, P]) for _ in range(2)])
    KTr = Ring([k.alloc([4, P]) for _ in range(2)])
    for b in QTr.bufs:
        k.pool.wait(k.pool.last)
        tqz = k.pool.sig(nc.gpsimd.memset(b, 0.0))
    QSr, KSr = (Ring([k.alloc([4, P]) for _ in range(3)]) for _ in range(2))
    PTr = Ring([k.alloc([16, P])])
    OTr = Ring([k.alloc([4, P]) for _ in range(2)])
    ONr = Ring([k.alloc([512]) for _ in range(2)])
    KV = k.alloc([4, P])
    KVt = k.alloc([4, P])
    rs = k.alloc([NT, 4])
    st = [dict() for _ in range(NT)]
    state = {"kv": None, "rd": None}

    def a0(i):
        s = st[i]
        s["xt"] = XT.take()
        s["txt"] = k.x_to_xt(i, R, s["xt"].ap, s["xt"].free, eng=i % 2)

    def a(i):
        s = st[i]
        for j, (name, ring) in enumerate((("q", Qr), ("k", Kr), ("v", Vr), ("u", Ur))):
            b = R.take()
            o = s[name] = ring.take()
            for kk in range(4):
                t = k.mm(b.ap, s["xt"].ap[:, kk, :], WQ[:, kk, 512 * j:512 * j + 512], kk == 0, kk == 3,
                         b.free, s["txt"], tw[j], sig=(kk == 3))
            if j < 2:
                t = k.activ(o.ap, b.ap, ACT.Silu, t, o.free)
            elif j == 2:
                t = k.v_copy(o.ap, b.ap, t, o.free)
            else:
                t = k.acopy(o.ap, b.ap, t, o.free)
            b.done(t)
            s["t" + name] = t
        s["xt"].done(k.pe.last)

    def b(i):
        s = st[i]
        for name, src, tsrc, ring in (("qt", s["q"], s["tq"], QTr), ("kt", s["k"], s["tk"], KTr)):
            bk = R.take()
            bb = bk.ap.rearrange("p (k n) -> p k n", k=4)
            o = s[name] = ring.take()
            for kk in range(4):
                t = k.tr(bb[:, kk, :], src.ap[:, kk * P:kk * P + P], bk.free, tsrc, sig=(kk == 3))
            if name == "qt":
                t = [(k.v_copy if g % 2 else k.acopy)(o.ap[32 * g:32 * g + 32, g], bb[32 * g:32 * g + 32], t, o.free, tqz)
                     for g in range(4)] + [tqz]
                s["qs"] = QSr.take()
                s["tqs"] = k.v_tt(s["qs"].ap, bb, QD, ALU.mult, t, s["qs"].free, dec)
                t.append(s["tqs"])
            else:
                t = [k.acopy(o.ap, bb, t, o.free)]
            bk.done(*t)
            s["t" + name] = t
            if name == "qt":
                s["q"].done(k.pe.last)
            else:
                tkt = k.pe.last
        o = s["ks"] = KSr.take()
        s["tks"] = k.g_tt(o.ap.rearrange("p a b -> p (a b)"), s["k"].ap, KD, ALU.mult, s["tk"], o.free, dec)
        s["k"].done(s["tks"], tkt)

    def c(i):
        s = st[i]
        first = i % 4 == 0
        pt = s["pt"] = PTr.take()
        banks = [S4.take() for _ in range(4)]
        for g in range(4):
            bb = banks[g].ap.rearrange("p (k n) -> p k n", k=4)
            for hg in range(4):
                t = k.mm(bb[:, hg, :], s["kt"].ap[:, hg, :], s["qt"].ap[:, g, hg, :],
                         True, True, banks[g].free, s["tqt"], s["tkt"], sig=(hg == 3))
            dv = DT.rearrange("p (hg g) n -> p g hg n", g=4)[:, g]
            pv = pt.ap.rearrange("p (hg g) n -> p g hg n", g=4)[:, g]
            t = k.v_tt(pv, bb, dv, ALU.mult, t, pt.free, dec)
            banks[g].done(t)
        s["tpt"] = t
        s["qt"].done(k.pe.last, s["tqs"])
        s["kt"].done(k.pe.last)

    def kvup(i):
        s = st[i]
        if i % 4 == 3:
            s["ks"].done(s["tks"])
            return
        bk = R.take()
        bb = bk.ap.rearrange("p (k n) -> p k n", k=4)
        for hg in range(4):
            t = k.mm(bb[:, hg, :], s["ks"].ap[:, hg, :], s["v"].ap[:, hg * P:hg * P + P], True, True,
                     bk.free, s["tks"], s["tv"], sig=(hg == 3))
        s["ks"].done(t)
        bm = BM.unsqueeze(1).to_broadcast([P, 4, P])
        if i % 4 == 0:
            t = t0 = k.v_tt(KV, bb, bm, ALU.mult, t, state["rd"])
        else:
            t0 = k.v_tt(KVt, bb, bm, ALU.mult, t, state["kv"])
            t1 = k.v_tt(KV, KV, EB, ALU.mult, state["kv"], state["rd"], t0)
            t = k.v_tt(KV, KV, KVt, ALU.add, t1)
        bk.done(t0)
        state["kv"] = t

    def dd(i):
        s = st[i]
        ob = OB.take()
        if i % 4:
            for hg in range(4):
                k.mm(ob.ap[:, hg * P:hg * P + P], s["qs"].ap[:, hg, :], KV[:, hg, :], hg == 0, False,
                     ob.free, s["tqs"], state["kv"], sig=(hg == 3))
            state["rd"] = k.pe.last
        kvup(i)
        s["qs"].done(k.pe.last, s["tqs"])
        for h in range(16):
            t = k.mm(ob.ap[:, h * 32:h * 32 + 32], s["pt"].ap[:, h, :], s["v"].ap[:, h * 32:h * 32 + 32],
                     i % 4 == 0 and h == 0, h == 15, ob.free, s["tpt"], s["tv"], sig=(h == 15))
        s["pt"].done(t)
        s["v"].done(t)
        on = s["on"] = ONr.take()
        t1 = k.activ(on.ap, ob.ap, ACT.Square, t, on.free, accum=rs[:, i, 0:1])
        t2 = k.g_ts(rs[:, i, 1:2], rs[:, i, 0:1], 1.0 / 512, 1e-6, ALU.mult, ALU.add, t1)
        t3 = k.g_tt(rs[:, i, 2:3], rs[:, i, 1:2], k.nhalf[:, 0:1], ALU.pow, t2)
        t4 = k.v_stt(on.ap, ob.ap, rs[:, i, 2:3], s["u"].ap, ALU.mult, ALU.mult, t3, s["tu"], t1)
        s["u"].done(t4)
        ob.done(t4)
        s["ton"] = t4

    def e(i):
        s = st[i]
        bk = R.take()
        bb = bk.ap.rearrange("p (k n) -> p k n", k=4)
        for kk in range(4):
            t = k.tr(bb[:, kk, :], s["on"].ap[:, kk * P:kk * P + P], bk.free, s["ton"], sig=(kk == 3))
        s["on"].done(t)
        ot = OTr.take()
        t = k.acopy(ot.ap, bb, t, ot.free)
        bk.done(t)
        b2 = R.take()
        for kk in range(4):
            t2 = k.mm(b2.ap, ot.ap[:, kk, :], WO[:, kk, :], kk == 0, kk == 3, b2.free, t, two, sig=(kk == 3))
        ot.done(t2)
        k.ln(i, k.add_from(i, b2.ap, b2), t2)

    def turn(i):
        a0(i)
        k.background(4)

    pipeline(NT, [(0, turn), (1, a), (2, b), (3, c), (4, dd), (5, e)])
    k.ln_flush()


def split3(k, parts, x, res, *w):
    t = k.v_copy(parts[0], x, *w)
    t = k.v_tt(res, x, parts[0], ALU.subtract, t, *w)
    t = k.v_copy(parts[1], res, t)
    t = k.v_tt(res, res, parts[1], ALU.subtract, t)
    return k.v_copy(parts[2], res, t)


def l0_xattn(k):
    nc = k.nc
    k.phase("l0xattn")
    k.off = k.base
    CX = k.alloc([NT, P])
    tcx = [k.dma(CX[:, 4 * b:4 * b + 4, :], k.ins["ctx_512"][b].rearrange("(t p) d -> p t d", p=P)) for b in range(4)]
    KS = Ring([k.alloc([8, 512], BF16) for _ in range(2)])
    VA = Ring([k.alloc([4, 8, 32]) for _ in range(2)])
    kst = [k.alloc([8, P], BF16) for _ in range(1)]
    kres = k.alloc([P])
    qst = Ring([k.alloc([32, 96], BF16) for _ in range(1)])
    qsc = k.alloc([512])
    qres = k.alloc([512])
    QS = Ring([k.alloc([32, P], BF16) for _ in range(3)])
    MX = k.alloc([2, 32])
    mres = k.alloc([32])
    ms = k.alloc([96], BF16)
    MT = Ring([k.alloc([P], BF16) for _ in range(2)])
    PT = Ring([k.alloc([4, 4, P]) for _ in range(3)])
    OT = Ring([k.alloc([4, P]) for _ in range(2)])
    rz = k.alloc([2, 32])
    oa = Ring([k.alloc([512]) for _ in range(2)])
    S1 = Ring([k.bank(0, 2), k.bank(2, 2)])
    S2 = Ring([k.bank(4)[:, 0, :], k.bank(5)[:, 0, :]])
    OB = Ring([k.bank(6)[:, 0, :], k.bank(7)[:, 0, :]])
    st = [dict() for _ in range(NT)]
    kb = [dict() for _ in range(4)]
    KORD = (0, 1, 0, 1, 2, 0)
    QORD = (0, 0, 1, 1, 0, 2)
    k.tkst = None

    for buf in VA.bufs:
        k.pool.wait()
        tva = k.pool.sig(nc.gpsimd.memset(buf[:, :, :, 16:32], 1.0))
    tks0 = k.pool.sig(nc.gpsimd.memset(kst[0][:, :, 96:128], 0.0))
    k.pool.wait(tks0)
    tks0 = k.pool.sig(nc.gpsimd.memset(kst[0][:, :, 96:99], 1.0))
    k.tkst = [tks0]
    for buf in QS.bufs:
        k.pool.wait(k.pool.last)
        tqz = k.pool.sig(nc.gpsimd.memset(buf[96:128, :, :], 0.0))
    k.pool.wait(tqz)

    def prep(b, t4):
        s = kb[b]
        if t4 == 0:
            s["ks"] = KS.take()
            s["va"] = VA.take()
            s["tk"] = [None] * 4
            s["tv"] = [None] * 4
        src = CX[:, 4 * b + t4, :].rearrange("p (h d) -> p h d", d=16)
        va = s["va"].ap
        s["tv"][t4] = k.g_copy(va[:, t4, :, 0:16], src, tcx, s["va"].free)
        s["tva"] = tva
        buf = kst[0]
        kv = buf[:, :, 0:96].rearrange("p h (r d) -> p h r d", d=16)
        part = [kv[:, :, 0, :], kv[:, :, 1, :], kv[:, :, 4, :]]
        rr = kres.rearrange("p (h d) -> p h d", d=16)
        t = split3(k, part, src, rr, tcx, k.tkst, tks0)
        ta = k.g_copy(kv[:, :, 2, :], kv[:, :, 0, :], t)
        tb = k.g_copy(kv[:, :, 3, :], kv[:, :, 1, :])
        tc = k.g_copy(kv[:, :, 5, :], kv[:, :, 0, :])
        s["tc"] = [tc, ta, tb]

    def prep2(b, t4):
        s, buf = kb[b], kst[0]
        s1 = S1.take()
        bb = s1.ap[:, 0, :].bitcast(BF16).rearrange("p (h n) -> p h n", n=P)
        for h in range(8):
            t = k.tr(bb[:, h, :], buf[:, h, :], s1.free, s["tc"], sig=(h == 7))
        k.tkst = [t]
        t = k.acopy(s["ks"].ap[:, :, t4 * P:t4 * P + P], bb, t, s["ks"].free)
        s1.done(t)
        s["tk"][t4] = t

    def qsplit(i):
        s = st[i]
        sc = qsc.rearrange("p (h d) -> p h d", d=16)
        b = s["qst"] = qst.take()
        qv = b.ap.rearrange("p h (r d) -> p h r d", d=16)
        t0 = k.v_ts(qsc, k.X[:, i, :], 0.25, None, ALU.mult, None, k.xtok[i], k.dve.last)
        rr = qres.rearrange("p (h d) -> p h d", d=16)
        t = split3(k, [qv[:, :, 0, :], qv[:, :, 2, :], qv[:, :, 5, :]], sc, rr, t0, b.free)
        for dst, src in ((1, 0), (3, 2), (4, 0)):
            t = k.g_copy(qv[:, :, dst, :], qv[:, :, src, :], t)
        s["tqv"] = t

    def qt(i, h4):
        s = st[i]
        if h4 == 0:
            s["q"] = QS.take()
            s["tq"] = []
        q, b = s["q"], s["qst"]
        s1 = S1.take()
        for j in range(2):
            bb = s1.ap[:, j, :].bitcast(BF16).rearrange("p (h n) -> p h n", n=P)
            for h in range(8):
                t1 = k.tr(bb[0:96, h, :], b.ap[:, 16 * h4 + 8 * j + h, :], s1.free, s["tqv"], sig=(h == 7))
            dst = q.ap[0:96, 16 * h4 + 8 * j:16 * h4 + 8 * j + 8, :]
            te = k.acopy(dst, bb[0:96], t1, q.free)
            s["tq"].append(te)
        s1.done(te)
        if h4 == 1:
            b.done(t1)

    def first(i, j):
        s = st[i]
        s1 = S1.take()
        for u in range(2):
            h = 2 * j + u
            t = k.mm(s1.ap[:, u, :], s["q"].ap[0:96, h, :], kb[i // 4]["ks"].ap[0:96, h // 4, :], True, True,
                     s1.free, s["tq"], kb[i // 4]["tk"], sig=(u == 1))
        t = k.v_red(MX[:, i % 2, 2 * j:2 * j + 2], s1.ap, ALU.max, t, s["mfree"], negate=True)
        s1.done(t)
        s["tmx"] = t

    def maxparts(i):
        parts = [ms.rearrange("p (r h) -> p r h", h=32)[:, r, :] for r in range(3)]
        st[i]["tms"] = split3(k, parts, MX[:, i % 2, :], mres, st[i]["tmx"], k.msfree)

    def maxrows(i):
        s = st[i]
        s1 = S1.take()
        bb = s1.ap[:, 0, 0:64].bitcast(BF16)
        t = k.tr(bb[0:96, :], ms, s1.free, s["tms"], sig=True)
        k.msfree = t
        m = MT.take()
        t = k.v_copy(m.ap[0:96, :], bb[0:96, :], t, m.free)
        s1.done(t)
        t = k.dma(s["q"].ap[96:99, :, :], m.ap[0:96, :], t, s["q"].free, tqz)
        m.done(t)
        s["tmr"] = t

    k.msfree = None

    def second(i, h):
        s = st[i]
        kk = kb[i // 4]
        s2 = S2.take()
        bb = s2.ap.rearrange("p (t n) -> p t n", t=4)
        for t4 in range(4):
            t = k.mm(bb[:, t4, :], kk["ks"].ap[:, h // 4, t4 * P:t4 * P + P], s["q"].ap[:, h, :], True, True,
                     s2.free, s["tmr"], s["tq"], kk["tk"], sig=(t4 == 3))
        if h % 4 == 0:
            s["pt"] = PT.take()
        p = s["pt"]
        t = k.activ(p.ap[:, :, h % 4, :], bb, ACT.Exp, t, p.free)
        s2.done(t)
        if h % 4 == 3:
            s["p"].append((h // 4, p, t))

    def pv(i):
        s = st[i]
        kv, p, t = s["p"].pop(0)
        kk = kb[i // 4]
        if kv % 4 == 0:
            s["ob"] = OB.take()
        ob = s["ob"]
        r0 = 32 * (kv % 4)
        for t4 in range(4):
            t2 = k.mm(ob.ap[r0:r0 + 32, :], kk["va"].ap[:, t4, kv, :], p.ap[:, t4].rearrange("p h n -> p (h n)"),
                      t4 == 0, t4 == 3, ob.free, t, kk["tv"], kk["tva"], sig=(t4 == 3))
        p.done(t2)
        if kv % 4 == 3:
            o = OT.take()
            t3 = k.acopy(o.ap.rearrange("p a b -> p (a b)"), ob.ap, t2, o.free)
            ob.done(t3)
            s["ot"].append((kv // 4, o, t3))
        if kv == 7:
            s["q"].done(t2, k.pe.last)
            if i % 4 == 3:
                kk["ks"].done(k.pe.last)
                kk["va"].done(k.pe.last)

    def back(i):
        s = st[i]
        half, o, t = s["ot"].pop(0)
        s1 = S1.take()
        bb = s1.ap[:, 0, :].rearrange("p (g n) -> p g n", g=4)
        for g in range(4):
            t2 = k.tr(bb[:, g, :], o.ap[:, g, :], s1.free, t, sig=(g == 3))
        o.done(t2)
        if half == 0:
            s["oa"] = oa.take()
            s["toa"] = []
        b4 = bb.rearrange("p g (v e) -> p v g e", e=32)
        r = rz[:, i % 2, 16 * half:16 * half + 16].rearrange("p (v g) -> p v g", g=4).unsqueeze(3)
        t3 = k.v_recip(r, b4[:, :, :, 16:17], t2, s["mfree"])
        dst = s["oa"].ap[:, 256 * half:256 * half + 256].rearrange("p (v g d) -> p v g d", g=4, d=16)
        for v in range(4):
            t4 = k.v_tt(dst[:, v], b4[:, v, :, 0:16], r[:, v].to_broadcast([P, 4, 16]), ALU.mult, t3, s["oa"].free)
        s1.done(t4)
        s["toa"].append(t4)
        if half == 1:
            def add(z, *w):
                t = k.v_tt(z, k.X[:, i, :], s["oa"].ap, ALU.add, s["toa"], *w, k.xtok[i])
                s["oa"].done(t)
                return t
            k.ln(i, add)

    for t4 in range(4):
        prep(0, t4)
        prep2(0, t4)
    LAG = 19


    qsplit(0)
    qt(0, 0)
    qt(0, 1)
    for n in range(16 * NT + LAG + 9):
        def at(lag, j=None):
            i, jj = divmod(n - lag, 16)
            return (i, jj) if 0 <= i < NT and (j is None or jj == j) else None
        v = at(0)
        if v:
            i, j = v
            if j == 0:
                st[i]["mfree"] = k.dve.last
                st[i]["p"], st[i]["ot"] = [], []
            first(i, j)
            if i + 1 < NT:
                if j == 3:
                    qsplit(i + 1)
                if j in (13, 14):
                    qt(i + 1, j - 13)
            if i % 4 >= 2 and i // 4 < 3 and j in (1, 7, 9, 15):
                (prep if j in (1, 9) else prep2)(i // 4 + 1, 2 * (i % 4 - 2) + j // 8)
            if j == 15:
                maxparts(i)
        if at(16, 0):
            maxrows(at(16, 0)[0])
        v = at(LAG)
        if v:
            second(v[0], 2 * v[1])
            second(v[0], 2 * v[1] + 1)
        v = at(LAG + 1)
        if v and v[1] % 2 == 1:
            pv(v[0])
        for lag, j in ((LAG + 3, 7), (LAG + 3, 15)):
            if at(lag, j):
                back(at(lag, j)[0])
    k.ln_flush()
def rows(ap):
    return ap.rearrange("(k p) n -> p k n", p=P)


def stats(k, z, st6, mv4, eps, *w):
    k.dve.wait(*w)
    t = k.dve.sig(k.nc.vector.bn_stats(st6, z))
    tr = t
    k.dve.wait(t)
    t = k.dve.sig(k.nc.vector.bn_aggr(mv4[:, 0:2], st6))
    t = k.g_ts(mv4[:, 2:3], mv4[:, 1:2], eps, 1.0, ALU.add, ALU.mult, t)
    return k.g_tt(mv4[:, 3:4], mv4[:, 2:3], k.nhalf[:, 0:1], ALU.pow, t), tr


def sims(k, R, CT, W, b, QK, s, tc):
    for j in range(2):
        r = R.take()
        t = k.mm(r.ap, W[:, j, :], CT[:, b, :], True, True, r.free, tc, sig=True)
        o = s[j] = QK[j].take()
        if j == 0:
            t = k.activ(o.ap, r.ap, ACT.Copy, t, o.free, scale=1.0 / (float(np.sqrt(np.float32(32))) * 4))
        else:
            t = k.acopy(o.ap, r.ap, t, o.free)
        r.done(t)
        s[2 + j] = t


def score(k, R, s, t4, o, done):
    r = R.take()
    t = k.mm(r.ap, s[0].ap[:, t4 * P:t4 * P + P], s[1].ap, True, True, r.free, s[2], s[3], sig=True)
    if done:
        s[0].done(t)
        s[1].done(t)
    t = k.acopy(o.ap, r.ap, t, o.free)
    r.done(t)
    return t


def thresholds(k):
    nc = k.nc
    o = k.W - 5000
    CT, W = k.view(o, [4, 512]), k.view(o + 2048, [2, P])
    QK = [Ring([k.view(o + 2304 + 512 * j, [512])]) for j in range(2)]
    SS = Ring([k.view(o + 3328 + 512 * j, [512]) for j in range(2)])
    w = k.view(o + 4352, [512])
    m8 = k.view(o + 4864, [8])
    tc = [k.dma(CT, k.ins["ctx_T"]), k.dma(W, k.ins["L1_xattn_W"])]
    yield
    s = {}
    t = None
    nxt = None
    for n in range(NT + 1):
        if n < NT:
            if n % 4 == 0:
                sims(k, k.bgring, CT, W, n // 4, QK, s, tc)
            o2 = SS.take()
            nxt, cur = (o2, score(k, k.bgring, s, n % 4, o2, n % 4 == 3)), nxt
        else:
            cur = nxt
        if cur is None:
            continue
        o, ts = cur
        k.dve.wait(ts, t)
        t = k.dve.sig(nc.vector.max(m8, o.ap))
        for j in range(19):
            k.dve.wait(t)
            t = k.dve.sig(nc.vector.match_replace(w, m8, o.ap if j == 0 else w, -3.0e38))
            k.dve.wait(t)
            t = k.dve.sig(nc.vector.max(m8, w))
            if j == 0:
                o.done(t)
            yield
        t = k.v_copy(k.thr[:, n - 1:n], m8[:, 0:1], t)


def l0_ffn(k):
    nc = k.nc
    k.phase("l0ffn")
    k.off = k.base
    W1 = k.alloc([4, 2048])
    W2 = k.alloc([16, 512])
    w1, w2 = rows(k.ins["L0_ffn_up_w"]), rows(k.ins["L0_ffn_down_w"])
    WE = k.alloc([4, 512])
    WG = k.alloc([4, 8])
    G = k.alloc([2, 512])
    tw1 = [k.dma(W1[:, kk, :], w1[:, kk, :]) for kk in range(4)]
    tc = [k.dma(WE, rows(k.ins["L0_ffn_expert_weight"])), k.dma(WG, rows(k.ins["L0_ffn_gate_w"])),
          k.dma(G, k.ins["L0_ffn_ln"])]
    tw2 = [k.dma(W2[:, 4 * j:4 * j + 4, :], w2[:, 4 * j:4 * j + 4, :]) for j in range(4)]
    XT = Ring([k.alloc([4, 512]) for _ in range(2)])
    HT = Ring([k.alloc([512]) for _ in range(4)])
    YS = Ring([k.alloc([512]) for _ in range(3)])
    ES = Ring([k.alloc([512]) for _ in range(4)])
    sm = k.alloc([NT, 24])
    YB = [k.bank(j)[:, 0, :] for j in range(4)]
    yfree = [[] for _ in range(4)]
    H = Ring([k.bank(4)[:, 0, :], k.bank(5)[:, 0, :]])
    R = Ring([k.bank(6)[:, 0, :], k.bank(7)[:, 0, :]])

    def xt(b):
        s = XT.take()
        s.toks = []
        for t4 in range(4):
            s.toks.append(k.x_to_xt(4 * b + t4, R, s.ap[:, :, t4 * P:t4 * P + P], s.free))
        return s

    k.bgring = R
    xs = {0: xt(0)}

    def up(b, m):
        h = H.take()
        for kk in range(4):
            t = k.mm(h.ap, W1[:, kk, m * P:m * P + P], xs[b].ap[:, kk, :], kk == 0, kk == 3, h.free, xs[b].toks,
                     tw1[kk], sig=(kk == 3))
        o = HT.take()
        t = k.activ(o.ap, h.ap, ACT.Relu, t, o.free)
        h.done(t)
        t = k.activ(o.ap, o.ap, ACT.Square, t)
        return o, t

    def down(b, m, ot):
        o, t = ot
        for t4 in range(4):
            td = k.mm(YB[t4], o.ap[:, t4 * P:t4 * P + P], W2[:, m, :], m == 0, m == 15, t, tw2[m // 4],
                      yfree[t4], sig=(m == 15 or t4 == 3))
            if m == 15:
                ydone[t4] = td
        o.done(td)

    def gate(i, t4):
        x = xs[i // 4]
        r = R.take()
        for kk in range(4):
            t = k.mm(r.ap[:, 0:8], x.ap[:, kk, t4 * P:t4 * P + P], WG[:, kk, :], kk == 0, kk == 3, r.free, x.toks, tc,
                     sig=(kk == 3))
        k.dve.wait(t)
        t = k.dve.sig(nc.vector.max(sm[:, i, 0:8], r.ap[:, 0:8]))
        r.done(t)
        ts = k.v_tt(sm[:, i, 8:9], sm[:, i, 0:1], sm[:, i, 1:2], ALU.add, t)
        r = R.take()
        for kk in range(4):
            t = k.mm(r.ap, x.ap[:, kk, t4 * P:t4 * P + P], WE[:, kk, :], kk == 0, kk == 3, r.free, sig=(kk == 3))
        e = ES.take()
        t = k.activ(e.ap, r.ap, ACT.Copy, t, ts, e.free, scale=sm[:, i, 8:9])
        r.done(t)
        return e, t

    def finish(i, t4):
        e, te = gates.pop(i)
        y = YS.take()
        ty = k.v_tt(y.ap, YB[t4], e.ap, ALU.add, ydone[t4], te, y.free)
        yfree[t4] = [ty]
        e.done(ty)
        ts, _ = stats(k, y.ap, sm[:, i, 9:15], sm[:, i, 16:20], 1e-5, ty)
        return y, ts, i

    def finish2(v):
        y, ts, i = v
        t = k.v_ts(y.ap, y.ap, sm[:, i, 16:17], sm[:, i, 19:20], ALU.subtract, ALU.mult, ts)
        t = k.g_tt(y.ap, y.ap, G[:, 0, :], ALU.mult, t, tc)
        t = k.g_tt(y.ap, y.ap, G[:, 1, :], ALU.add, t)

        def add(z, *w):
            t2 = k.v_tt(z, y.ap, k.X[:, i, :], ALU.add, t, *w, k.xtok[i])
            y.done(t2)
            return t2
        k.ln(i, add)

    ydone = [None] * 4
    pend = []
    gates = {}
    q = {}
    for n in range(64 + 2):
        b, m = divmod(n, 16)
        if n < 64:
            q[n] = up(b, m)
        if n >= 2:
            down((n - 2) // 16, (n - 2) % 16, q.pop(n - 2))
        if m == 1 and b:
            for t4 in range(4):
                pend.append(finish(4 * b - 4 + t4, t4))
                if len(pend) > 1:
                    finish2(pend.pop(0))
            xs[b - 1].done(k.pe.last)
        k.background(4)
        if m == 8 and b < 3:
            xs[b + 1] = xt(b + 1)
        if 10 <= m <= 13:
            gates[4 * b + m - 10] = gate(4 * b + m - 10, m - 10)
    while pend:
        finish2(pend.pop(0))
    k.background(400)
    k.ln_flush()


def attn(k, label, kind):
    nc = k.nc
    k.phase(label)
    k.off = k.base
    ins = k.ins
    lat = kind == 1
    SC = float(32) ** -0.5
    nk = 1 if lat else 4
    if kind == 2 and k.early:
        (WQ, WK, WV, WO), tw = k.early
        tw = list(tw)
    else:
        WQ, WK, WV, WO = (k.alloc([n, 512]) for n in (4, nk, nk, 4))
        tw = [k.dma(w, rows(ins[label + n])) for w, n in ((WQ, "_q"), (WK, "_k"), (WV, "_v"), (WO, "_o"))]
    XT = Ring([k.alloc([4, P]) for _ in range(2)])
    if lat:
        CT = k.alloc([4, 512])
        tw.append(k.dma(CT, ins["ctx_T"]))
    else:
        BQ, BK, BV, BO = k.alloc([4]), k.alloc([4]), k.alloc([512]), k.alloc([512])
        tw += [k.dma(w, ins[label + n]) for w, n in ((BQ, "_bq"), (BK, "_bk"), (BV, "_bv"), (BO, "_bo"))]
    QT = Ring([k.alloc([4, 4, P]) for _ in range(3)])
    for b in QT.bufs:
        k.pool.wait()
        tqz = k.pool.sig(nc.gpsimd.memset(b, 0.0))
    KT = Ring([k.alloc([4, 512]) for _ in range(2)])
    if kind == 2:
        V = Ring([k.alloc([512]) for _ in range(3)])
        JK = Ring([k.alloc([512]) for _ in range(2)])
        SM = k.alloc([2, 4, 16])
    else:
        VA = Ring([k.alloc([4, 8, 4, 32]) for _ in range(2)])
        k.pool.wait()
        for b in VA.bufs:
            tva = k.pool.sig(nc.gpsimd.memset(b[:, :, :, 1:3, :], 1.0))
        PT = Ring([k.alloc([2, 512]) for _ in range(4)])
        NS = k.alloc([4, 32], BF16)
        NM = Ring([k.alloc([P], BF16) for _ in range(2)])
        SEL = k.alloc([4, 4, P], BF16)
        stg = k.alloc([4, 4, P])
        t = k.dma(stg, ins["c_sel"])
        tsel = [k.v_copy(SEL, stg, t)]
        k.pool.wait()
        tsel.append(k.pool.sig(nc.gpsimd.memset(NS, 0.0)))
        mres = k.alloc([16])
        RZ = k.alloc([2, 2, P])
    MX = k.alloc([2, 4, 4])
    ON = Ring([k.alloc([512]) for _ in range(2)])
    OT = Ring([k.alloc([4, P]) for _ in range(2)])
    XB = Ring([k.alloc([512]) for _ in range(2)])
    A = Ring([k.bank(j, 2) for j in ((0, 2, 4, 6) if kind == 2 else (0, 2))])
    S2 = Ring([k.bank(4, 2)])
    OB = Ring([k.bank(j)[:, 0, :].rearrange("p (h g n) -> p h g n", h=2, g=2) for j in (6, 7)])
    LAG = 10
    st = [dict() for _ in range(NT)]
    kb = [dict() for _ in range(4)]
    free = {"mx": [None, None], "ns": None, "rz": [None, None]}
    fin = []

    def v4(ap):
        return ap.rearrange("p (m n) -> p m n", m=4)

    def xtile(i):
        a = A.take()
        xt = st[i]["xt"] = XT.take()
        bb = v4(a.ap[:, 0, :])
        for kk in range(4):
            t = k.tr(bb[:, kk, :], k.X[:, i, kk * P:kk * P + P], a.free, k.xtok[i], sig=(kk == 3))
        st[i]["txt"] = k.acopy(xt.ap, bb, t, xt.free)
        a.done(st[i]["txt"])

    def proj(i):
        s, b, t4 = st[i], kb[i // 4], i % 4
        xt, txt = s["xt"], s["txt"]
        if t4 == 0:
            b["kt"] = KT.take()
            b["tk"] = []
            if kind != 2:
                b["v"] = VA.take()
                b["tv"] = [tva]
        a = A.take()
        q = s["q"] = QT.take()
        bb = v4(a.ap[:, 0, :])
        for m in range(4):
            for kk in range(4):
                t = k.mm(bb[:, m, :], WQ[:, kk, m * P:m * P + P], xt.ap[:, kk, :], kk == 0, kk == 3, a.free, tw, txt,
                         sig=(kk == 3 and m == 3))
        s["tq"] = [tqz]
        for g in range(4):
            r = slice(32 * g, 32 * g + 32)
            if lat:
                t1 = k.acopy(q.ap[r, g], bb[r], t, q.free, tqz)
            else:
                t1 = k.v_tt(q.ap[r, g], bb[r], BQ[r].unsqueeze(2).to_broadcast([32, 4, P]), ALU.add, t, q.free, tqz)
            s["tq"].append(t1)
        bb = v4(a.ap[:, 1, :])
        for m in range(4):
            for kk in range(nk):
                r = CT[:, i // 4, t4 * P:t4 * P + P] if lat else xt.ap[:, kk, :]
                t = k.mm(bb[:, m, :], WK[:, kk, m * P:m * P + P], r, kk == 0, kk == nk - 1, sig=(kk == nk - 1 and m == 3))
        dst = b["kt"].ap[:, :, t4 * P:t4 * P + P]
        if lat:
            t2 = k.acopy(dst, bb, t, b["kt"].free)
        else:
            t2 = k.v_tt(dst, bb, BK.unsqueeze(2).to_broadcast([P, 4, P]), ALU.add, t, b["kt"].free)
        a.done(t1, t2)
        b["tk"].append(t2)
        a = A.take()
        for kk in range(nk):
            l = CT[:, i // 4, t4 * P:t4 * P + P] if lat else xt.ap[:, kk, :]
            t = k.mm(a.ap[:, 0, :], l, WV[:, kk, :], kk == 0, kk == nk - 1, a.free, sig=(kk == nk - 1))
        xt.done(t)
        src = a.ap[:, 0, :].rearrange("p (h w d) -> p h w d", w=2, d=32)
        if kind == 2:
            v = s["v"] = V.take()
            t = s["tv"] = k.v_tt(v.ap, a.ap[:, 0, :], BV, ALU.add, t, v.free)
        elif lat:
            t = k.acopy(b["v"].ap[:, t4, :, 0:4:3, :], src, t, b["v"].free)
            b["tv"].append(t)
        else:
            t = k.v_tt(b["v"].ap[:, t4, :, 0:4:3, :], src, BV.rearrange("p (h w d) -> p h w d", w=2, d=32), ALU.add, t,
                       b["v"].free)
            b["tv"].append(t)
        a.done(t)

    def first(i, hg, u):
        s, b, n = st[i], kb[i // 4], (i % 4 + 1) * P
        a = A.take()
        for g in range(2):
            k.mm(a.ap[:, g, 0:n], s["q"].ap[:, 2 * u + g, hg, :], b["kt"].ap[:, hg, 0:n], True, False,
                 a.free, s["tq"], b["tk"])
            t = k.mm(a.ap[:, g, n - P:n], k.idb, k.mq, False, True, sig=(g == 1))
        tm = k.v_red(MX[:, i % 2, 2 * u:2 * u + 2, hg], a.ap[:, :, 0:n], ALU.max, t, free["mx"][i % 2], negate=True)
        if kind == 2:
            for g in range(2):
                g4 = 2 * u + g
                j = JK.take()
                tb = k.v_ts(SM[:, i % 2, 0, 4 * hg + g4:4 * hg + g4 + 1], MX[:, i % 2, g4, hg:hg + 1], SC, None, ALU.mult,
                            None, tm, s["smfree"])
                t = k.activ(j.ap[:, 0:n], a.ap[:, g, 0:n], ACT.Exp, tb, j.free, s["smfree"],
                            bias=SM[:, i % 2, 0, 4 * hg + g4:4 * hg + g4 + 1], scale=SC,
                            accum=SM[:, i % 2, 1, 4 * hg + g4:4 * hg + g4 + 1])
                j.done(t)
            tm = t
        a.done(tm)
        s["tm"] = tm

    def maxparts(i):
        s = st[i]
        parts = [NS[:, :, 4 * r:4 * r + 4] for r in range(3)]
        t = split3(k, parts, MX[:, i % 2], mres.rearrange("p (a b) -> p a b", b=4), s["tm"], free["ns"], tsel)
        free["mx"][i % 2] = s["tns"] = t

    def maxrows(i):
        s = st[i]
        a = A.take()
        bb = a.ap[:, 0, 0:64].bitcast(BF16)
        t = free["ns"] = k.tr(bb, NS.rearrange("p a b -> p (a b)"), a.free, s["tns"], sig=True)
        m = s["nm"] = NM.take()
        s["tnm"] = k.v_copy(m.ap, bb, t, m.free)
        a.done(s["tnm"])

    def second(i, hg, u):
        s, b, n = st[i], kb[i // 4], i % 4 + 1
        a = S2.take()
        for g in range(2):
            for kt in range(n):
                o = a.ap[:, g, kt * P:kt * P + P]
                k.mm(o, b["kt"].ap[:, hg, kt * P:kt * P + P], s["q"].ap[:, 2 * u + g, hg, :], True, False,
                     a.free, s["tq"], b["tk"], s["tnm"])
                if kt == n - 1:
                    k.mm(o, k.idb, k.mk, False, False)
                t = k.mm(o, SEL[:, 2 * u + g, hg, :], s["nm"].ap, False, True, tsel,
                         sig=(g == 1 and kt == n - 1))
        p = PT.take()
        t = k.activ(p.ap[:, :, 0:n * P], a.ap[:, :, 0:n * P], ACT.Exp, t, p.free, scale=SC)
        a.done(t)
        s["p"].append((hg, u, p, t))

    def pv(i):
        s, b, n = st[i], kb[i // 4], i % 4 + 1
        hg, u, p, t = s["p"].pop(0)
        if hg % 2 == 0 and u == 0:
            s["ob"] = OB.take()
            if hg == 0:
                s["ot"] = OT.take()
                s["tot"] = []
        ob = s["ob"]
        for g in range(2):
            for kt in range(n):
                v = b["v"].ap[:, kt, 2 * hg + u, 2 * g:2 * g + 2, :].rearrange("p w d -> p (w d)")
                t2 = k.mm(ob.ap[64 * u:64 * u + 64, hg % 2, g, :], v, p.ap[:, g, kt * P:kt * P + P],
                          kt == 0, kt == n - 1, ob.free, t, b["tv"], sig=(g == 1 and kt == n - 1))
        p.done(t2)
        if hg % 2 == 1 and u == 1:
            o = s["ot"]

            def over(h2, last):
                hd = h2 % 2
                tz = k.v_recip(RZ[:, hd], ob.ap[:, hd], t2, free["rz"][hd])
                tt = []
                for g4 in range(4):
                    r0, z0, g = 32 * g4, 32 * (g4 ^ 1), g4 % 2
                    tt.append(k.v_tt(o.ap[r0:r0 + 32, h2, :], ob.ap[r0:r0 + 32, hd, g, :], RZ[z0:z0 + 32, hd, g, :],
                                     ALU.mult, tz, o.free))
                free["rz"][hd] = tt
                s["tot"] += tt
                if last:
                    ob.done(tt)
            fin.append(lambda: over(hg - 1, False))
            fin.append(lambda: over(hg, True))
            if hg == 3:
                s["q"].done(t2)
                s["nm"].done(t2)
                if i % 4 == 3:
                    b["kt"].done(t2)
                    b["v"].done(t2)

    def norm(i):
        s = st[i]
        if i % 4 == 3:
            kb[i // 4]["kt"].done(k.pe.last)
        s["q"].done(k.pe.last)
        on = s["on"] = ON.take()
        n, r, m = (SM[:, i % 2, j, :] for j in (1, 2, 3))
        t = k.v_recip(r, n, s["tm"])
        t = k.v_tt(m, n, r, ALU.mult, t)
        t = k.v_tt(on.ap.rearrange("p (h d) -> p h d", d=32), s["v"].ap.rearrange("p (h d) -> p h d", d=32),
                   m.unsqueeze(2).to_broadcast([P, 16, 32]), ALU.mult, t, s["tv"], on.free)
        s["v"].done(t)
        s["ton"] = [t]
        s["tsm"] = t

    def back(i):
        s = st[i]
        a = A.take()
        bb = v4(a.ap[:, 0, :])
        for kk in range(4):
            t = k.tr(bb[:, kk, :], s["on"].ap[:, kk * P:kk * P + P], a.free, s["ton"], sig=(kk == 3))
        s["on"].done(t)
        s["ot"] = OT.take()
        s["tot"] = k.acopy(s["ot"].ap, bb, t, s["ot"].free)
        a.done(s["tot"])

    def out(i):
        s = st[i]
        a = A.take()
        o, t = s["ot"], [s["tot"], a.free]
        for kk in range(4):
            t2 = k.mm(a.ap[:, 1, :], o.ap[:, kk, :], WO[:, kk, :], kk == 0, kk == 3, t, sig=(kk == 3))
        o.done(t2)
        if lat:
            k.ln(i, k.add_from(i, a.ap[:, 1, :], a), t2)
            return
        xb = XB.take()
        tb = k.g_tt(xb.ap, k.X[:, i, :], BO, ALU.add, k.xtok[i], xb.free, tw)

        def add(z, *w):
            t = k.v_tt(z, xb.ap, a.ap[:, 1, :], ALU.add, tb, *w)
            a.done(t)
            xb.done(t)
            return t
        k.ln(i, add, t2)

    xtile(0)
    proj(0)
    for n in range(8 * NT + 22):
        def at(lag, j=None):
            i, jj = divmod(n - lag, 8)
            return (i, jj) if 0 <= i < NT and (j is None or jj == j) else None
        v = at(0)
        if v:
            if v[1] == 0:
                st[v[0]]["p"] = []
                st[v[0]]["smfree"] = st[v[0] - 2]["tsm"] if kind == 2 and v[0] >= 2 else None
            first(v[0], v[1] // 2, v[1] % 2)
            if v[1] == 3 and v[0] + 1 < NT:
                xtile(v[0] + 1)
            if v[1] == 4 and v[0] + 1 < NT:
                proj(v[0] + 1)
        if kind == 2:
            for lag, f in ((1, norm), (4, back), (5, out)):
                if at(lag, 7):
                    f(at(lag, 7)[0])
            continue
        if at(0, 7):
            maxparts(at(0, 7)[0])
        if at(2, 7):
            maxrows(at(2, 7)[0])
        v = at(LAG)
        if v:
            second(v[0], v[1] // 2, v[1] % 2)
        v = at(LAG + 1)
        if v:
            pv(v[0])
        if fin:
            fin.pop(0)()
        if at(LAG + 4, 7):
            out(at(LAG + 4, 7)[0])
    k.ln_flush()


def l2_attn(k):
    attn(k, "L2_attn", 0)


def l2_xattn(k):
    attn(k, "L2_xattn", 1)


def l3_attn(k):
    attn(k, "L3_attn", 2)


def l3_xattn(k):
    nc = k.nc
    k.phase("l3xattn")
    k.off = k.base
    ins = k.ins
    k.off += 16384 + 256 + 4096
    CT = k.alloc([4, 512])
    WK = k.alloc([P])
    bk = k.alloc([1])
    GB = k.alloc([2, 512])
    KT = Ring([k.alloc([512]) for _ in range(2)])
    KV = Ring([k.alloc([4, P]) for _ in range(2)])
    XT = Ring([k.alloc([4, P]) for _ in range(2)])
    OT = Ring([k.alloc([P]) for _ in range(2)])
    ZZ = Ring([k.alloc([512]) for _ in range(4)])
    sm = k.alloc([NT, 16])
    R = Ring([k.bank(j)[:, 0, :] for j in range(8)])
    tc = [k.dma(CT, ins["ctx_T"]), k.dma(WK, ins["L3_xattn_W_k"]), k.dma(bk, ins["L3_xattn_b_k"]),
          k.dma(GB, ins["L3_xattn_ln"])]
    top, k.off = k.off, k.base
    tern = ternary(k, R, ins)
    next(tern)
    k.ternoff, k.off = k.off, top
    SC = float(512) ** -0.5
    kb = [dict() for _ in range(4)]
    st = [dict() for _ in range(NT)]

    def keys(b):
        s = kb[b]
        r = R.take()
        t = k.mm(r.ap, WK, CT[:, b, :], True, True, r.free, tc, sig=True)
        s["kt"], s["kv"] = KT.take(), KV.take()
        t = k.activ(s["kt"].ap, r.ap, ACT.Identity, t, s["kt"].free, bias=bk[:, 0:1])
        r.done(t)
        s["tk"] = t
        r = R.take()
        bb = r.ap.rearrange("p (m n) -> p m n", m=4)
        for m in range(4):
            t = k.tr(bb[:, m, :], s["kt"].ap[:, m * P:m * P + P], r.free, s["tk"], sig=(m == 3))
        s["tv"] = k.v_copy(s["kv"].ap, bb, t, s["kv"].free)
        r.done(s["tv"])

    def a(i):
        if i % 4 == 0:
            keys(i // 4)
        s = st[i]
        s["xt"] = XT.take()
        s["txt"] = k.x_to_xt(i, R, s["xt"].ap, s["xt"].free, eng=0)

    def b(i):
        s, b = st[i], kb[i // 4]
        r = R.take()
        for kk in range(4):
            t = k.mm(r.ap[:, 0:P], b["kv"].ap[:, kk, :], s["xt"].ap[:, kk, :], kk == 0, kk == 3, r.free, b["tv"], s["txt"],
                     sig=(kk == 3))
        s["xt"].done(t)
        o = OT.take()
        to = k.acopy(o.ap, r.ap[:, 0:P], t, o.free)
        r.done(to)
        r = R.take()
        t = k.mm(r.ap, o.ap, b["kt"].ap, True, True, r.free, to, b["tk"], sig=True)
        o.done(t)
        if i % 4 == 3:
            b["kt"].done(t)
            b["kv"].done(t)
        m = sm[:, i, :]
        k.dve.wait(t)
        t1 = k.dve.sig(nc.vector.bn_stats(m[:, 0:6], r.ap))
        k.dve.wait(t1)
        t1 = k.dve.sig(nc.vector.bn_aggr(m[:, 6:8], m[:, 0:6]))
        t1 = k.g_ts(m[:, 8:9], m[:, 7:8], SC * SC, 1e-6, ALU.mult, ALU.add, t1)
        t1 = k.g_tt(m[:, 9:10], m[:, 8:9], k.nhalf[:, 0:1], ALU.pow, t1)
        t1 = k.g_ts(m[:, 10:11], m[:, 9:10], SC, 1.0, ALU.mult, ALU.mult, t1)
        s["r"], s["t1"] = r, t1

    def c(i):
        s = st[i]
        m = sm[:, i, :]
        r = s["r"]
        z = ZZ.take()
        t = k.v_ts(z.ap, r.ap, m[:, 6:7], m[:, 10:11], ALU.subtract, ALU.mult, s["t1"], z.free)
        r.done(t)
        t = k.g_tt(z.ap, z.ap, GB[:, 0, :], ALU.mult, t, tc)
        s["tz"] = k.g_tt(z.ap, z.ap, GB[:, 1, :], ALU.add, t)
        s["z"] = z

    def d(i):
        s = st[i]
        m, z = sm[:, i, :], s["z"]
        t = k.v_red(m[:, 11:12], z.ap, ALU.max, s["tz"], negate=True)
        t = k.activ(z.ap, z.ap, ACT.Exp, t, bias=m[:, 11:12], accum=m[:, 12:13])
        t = k.v_recip(m[:, 13:14], m[:, 12:13], t)

        def add(zz, *w):
            t2 = k.v_stt(zz, z.ap, m[:, 13:14], k.X[:, i, :], ALU.mult, ALU.add, t, *w, k.xtok[i])
            z.done(t2)
            return t2
        k.ln(i, add)
        next(tern, None)

    pipeline(NT, [(0, a), (1, b), (2, c), (3, d)])
    k.ln_flush()
    for _ in tern:
        pass


def l1_xattn(k):
    nc = k.nc
    k.phase("l1xattn")
    k.off = k.base
    ins = k.ins
    R = Ring([k.bank(j)[:, 0, :] for j in range(8)])
    bits = bitweights(k, R)
    next(bits)
    CT = k.alloc([4, 512])
    W = k.alloc([2, P])
    gr = k.alloc([4])
    QT, KT = (Ring([k.alloc([512]) for _ in range(2)]) for _ in range(2))
    SS = Ring([k.alloc([512]) for _ in range(3)])
    WK = Ring([k.alloc([512]) for _ in range(2)])
    AL = Ring([k.alloc([4, 512]) for _ in range(2)])
    BB = Ring([k.alloc([512]) for _ in range(2)])
    XS = Ring([k.alloc([512]) for _ in range(2)])
    tc = [k.dma(CT, ins["ctx_T"]), k.dma(W, ins["L1_xattn_W"])]
    t = k.dma(gr[:, 0:1], ins["L1_gamma"])
    t = k.activ(gr[:, 1:2], gr[:, 0:1], ACT.Exp, t, scale=-1.0)
    t = k.v_ts(gr[:, 1:2], gr[:, 1:2], 1.0, None, ALU.add, None, t)
    t = k.v_recip(gr[:, 1:2], gr[:, 1:2], t)
    tg = [k.v_ts(gr[:, 2:3], gr[:, 1:2], -1.0, 2.0, ALU.mult, ALU.add, t),
          k.v_ts(gr[:, 3:4], gr[:, 1:2], 0.5, None, ALU.mult, None, t)]
    kb = [dict() for _ in range(4)]

    def learned(b, t4):
        s = kb[b]
        o, w = SS.take(), WK.take()
        t = score(k, R, s, t4, o, t4 == 3)
        te = k.activ(w.ap, o.ap, ACT.Sigmoid, t, w.free)
        al = s["al"]
        i = 4 * b + t4
        t = k.v_stt(al.ap[:, t4, :], o.ap, k.thr[:, i:i + 1], w.ap, ALU.is_ge, ALU.mult, te, al.free)
        w.done(t)
        o.done(t)
        s["ta"].append(t)

    def mix(i):
        s, t4 = kb[i // 4], i % 4
        al = s["al"]
        r = R.take()
        bb = r.ap.rearrange("p (m n) -> p m n", m=4)
        for m in range(4):
            t = k.tr(bb[:, m, :], al.ap[:, m, t4 * P:t4 * P + P], r.free, s["ta"], sig=(m == 3))
        o = BB.take()
        x = XS.take()
        tx = k.activ(x.ap, k.X[:, i, :], ACT.Copy, x.free, k.xtok[i], tg, scale=gr[:, 2:3])
        t = k.v_tt(o.ap, al.ap[:, t4, :], r.ap, ALU.add, t, o.free)
        r.done(t)
        if t4 == 3:
            al.done(t)

        def add(z, *w):
            t2 = k.v_stt(z, o.ap, gr[:, 3:4], x.ap, ALU.mult, ALU.add, t, tx, *w)
            o.done(t2)
            x.done(t2)
            return t2
        k.ln(i, add)

    def front(b):
        kb[b]["al"] = AL.take()
        kb[b]["ta"] = []
        sims(k, R, CT, W, b, [QT, KT], kb[b], tc)
        for t4 in range(4):
            learned(b, t4)
            next(bits, None)

    front(0)
    for b in range(4):
        if b < 3:
            front(b + 1)
        for t4 in range(4):
            mix(4 * b + t4)
            next(bits, None)
            next(bits, None)
    for _ in bits:
        pass
    k.ln_flush()


MAGIC = 12582912.0


def bitweights(k, R):
    nc, ins = k.nc, k.ins
    WG, WU = k.alloc([4, 2048], BF16), k.alloc([4, 2048], BF16)
    WD = k.alloc([16, 512], BF16)
    H = k.alloc([P])
    sc = k.alloc([8])
    k.bitoff = k.off
    part = k.alloc([16])
    ones = k.alloc([P])
    S = k.alloc([8192])
    th = k.dma(H, ins["c_hadamard"])
    to = k.pool.sig(nc.gpsimd.memset(ones, 1.0))
    cnt = 1.0 / (2048 * 512)
    tw, sfree = [], []
    yield
    for n, (name, W) in enumerate((("L1_ffn_w_gate", WG), ("L1_ffn_w_up", WU), ("L1_ffn_w_down", WD))):
        src = rows(ins[name])
        kk = src.shape[1] // 4
        tl = [k.dma(S[:, 2048 * j:2048 * j + 2048].rearrange("p (k n) -> p k n", k=kk),
                    src[:, kk * j:kk * j + kk, :], sfree) for j in range(4)]
        yield
        yield
        tp = []
        for j in range(4):
            tp.append(k.v_red(part[:, 4 * n + j:4 * n + j + 1], S[:, 2048 * j:2048 * j + 2048], ALU.add, tl[j],
                              absolute=True))
            yield
        t = k.v_red(sc[:, n:n + 1], part[:, 4 * n:4 * n + 4], ALU.add, tp)
        b = R.take()
        t = k.mm(b.ap[:, 0:1], ones, sc[:, n:n + 1], True, True, b.free, t, to, sig=True)
        t = k.v_ts(sc[:, n:n + 1], b.ap[:, 0:1], cnt, 1e-5, ALU.mult, ALU.max, t)
        b.done(t)
        t = k.v_recip(sc[:, 4 + n:5 + n], sc[:, n:n + 1], t)
        Wf = W.rearrange("p a b -> p (a b)")
        tj = []
        for j in range(4):
            w = S[:, 2048 * j:2048 * j + 2048]
            t2 = k.v_ts(w, w, sc[:, 4 + n:5 + n], 1.0, ALU.mult, ALU.min, t)
            t2 = k.v_ts(w, w, -1.0, MAGIC, ALU.max, ALU.add, t2)
            t2 = k.v_ts(Wf[:, 2048 * j:2048 * j + 2048], w, MAGIC, None, ALU.subtract, None, t2)
            tj.append(t2)
            yield
        sfree = tj
        tw.append(tj)
    k.bitw = (WG, WU, WD, H, sc, th, tw)
    yield


def l1_ffn(k):
    nc = k.nc
    k.phase("l1ffn")
    WG, WU, WD, H, sc, th, tw = k.bitw
    k.off = k.bitoff
    R = Ring([k.bank(j)[:, 0, :] for j in range(8)])
    tstage = None
    XQ = Ring([k.alloc([512]) for _ in range(2)], tstage)
    XB = Ring([k.alloc([512], BF16) for _ in range(2)], tstage)
    XT = Ring([k.alloc([4, P], BF16) for _ in range(2)], tstage)
    IM = Ring([k.alloc([2048]) for _ in range(2)], tstage)
    IT = Ring([k.alloc([16, P]) for _ in range(1)], tstage)
    HA = Ring([k.alloc([2048]) for _ in range(2)], tstage)
    HB = Ring([k.alloc([2048]) for _ in range(2)], tstage)
    YB = Ring([k.alloc([2048], BF16) for _ in range(2)], tstage)
    YT = Ring([k.alloc([16, P], BF16) for _ in range(2)], tstage)
    SG = Ring([k.alloc([512]) for _ in range(3)], tstage)
    sm = k.alloc([NT, 12])
    st = [dict() for _ in range(NT)]
    HN = float(1.0 / np.sqrt(2048))

    def a(i):
        s, m = st[i], sm[:, i, :]
        x = XQ.take()
        t = k.v_red(m[:, 0:1], k.X[:, i, :], ALU.max, k.xtok[i], tstage, absolute=True)
        t = k.v_ts(m[:, 0:1], m[:, 0:1], 1e-5, 1.0 / 128, ALU.max, ALU.mult, t)
        tr = k.v_recip(m[:, 1:2], m[:, 0:1], t)
        s["tf"] = [k.v_ts(m[:, 2:3], m[:, 0:1], sc[:, 0:1], None, ALU.mult, None, tr),
                   k.v_ts(m[:, 3:4], m[:, 0:1], sc[:, 1:2], None, ALU.mult, None, tr)]
        t = k.v_ts(x.ap, k.X[:, i, :], m[:, 1:2], 127.0, ALU.mult, ALU.min, tr, x.free)
        t = k.v_ts(x.ap, x.ap, -128.0, MAGIC, ALU.max, ALU.add, t)
        xb = XB.take()
        t = k.v_ts(xb.ap, x.ap, MAGIC, None, ALU.subtract, None, t, xb.free)
        x.done(t)
        s["xb"], s["txb"] = xb, t

    def a2(i):
        s = st[i]
        xb, t = s["xb"], s["txb"]
        r = R.take()
        bb = r.ap.bitcast(BF16)[:, 0:512].rearrange("p (m n) -> p m n", m=4)
        for kk in range(4):
            t1 = k.tr(bb[:, kk, :], xb.ap[:, kk * P:kk * P + P], r.free, t, sig=(kk == 3))
        xb.done(t1)
        s["xt"] = XT.take()
        s["txt"] = k.acopy(s["xt"].ap, bb, t1, s["xt"].free)
        r.done(s["txt"])

    def b(i):
        s, m = st[i], sm[:, i, :]
        im = s["im"] = IM.take()
        s["tim"] = []
        for c in range(4):
            r, r2 = R.take(), R.take()
            for kk in range(4):
                t = k.mm(r.ap, s["xt"].ap[:, kk, :], WG[:, kk, 512 * c:512 * c + 512], kk == 0, kk == 3, r.free,
                         s["txt"], tw[0], sig=(kk == 3))
            for kk in range(4):
                t2 = k.mm(r2.ap, s["xt"].ap[:, kk, :], WU[:, kk, 512 * c:512 * c + 512], kk == 0, kk == 3, r2.free,
                          tw[1], sig=(kk == 3))
            g = SG.take()
            t = k.activ(g.ap, r.ap, ACT.Silu, t, s["tf"], g.free, scale=m[:, 2:3])
            r.done(t)
            t = k.v_stt(im.ap[:, 512 * c:512 * c + 512], r2.ap, m[:, 3:4], g.ap, ALU.mult, ALU.mult, t, t2, im.free)
            r2.done(t)
            g.done(t)
            s["tim"].append(t)
        s["xt"].done(k.pe.last)

    def c(i):
        s, m = st[i], sm[:, i, :]
        im, it = s["im"], IT.take()
        te = []
        for c in range(4):
            r = R.take()
            bb = r.ap.rearrange("p (m n) -> p m n", m=4)
            for j in range(4):
                t = k.tr(bb[:, j, :], im.ap[:, (4 * c + j) * P:(4 * c + j + 1) * P], r.free, s["tim"], sig=(j == 3))
            te.append(k.acopy(it.ap[:, 4 * c:4 * c + 4, :], bb, t, it.free))
            r.done(te[-1])
        im.done(t)
        ha, hb = HA.take(), HB.take()
        tc = []
        for c in range(4):
            r = R.take()
            for j in range(4):
                t = k.mm(r.ap[:, j * P:j * P + P], it.ap[:, 4 * c + j, :], H, True, True, r.free, te[c], th, sig=(j == 3))
            tc.append(k.acopy(ha.ap[:, 512 * c:512 * c + 512], r.ap, t, ha.free))
            r.done(tc[-1])
        it.done(t)
        cur, nxt, t = ha, hb, tc
        nfree = hb.free
        for lv in range(4):
            h = P << lv
            v = cur.ap.rearrange("p (a t n) -> p a t n", t=2, n=h)
            o = nxt.ap.rearrange("p (a t n) -> p a t n", t=2, n=h)
            f = k.v_tt if lv < 2 else k.g_tt
            t1 = f(o[:, :, 0, :], v[:, :, 0, :], v[:, :, 1, :], ALU.add, t, nfree)
            t2 = f(o[:, :, 1, :], v[:, :, 0, :], v[:, :, 1, :], ALU.subtract, t)
            cur, nxt, t, nfree = nxt, cur, [t1, t2], None
        s["ha"], s["hb"], s["th"] = ha, hb, t

    def d(i):
        s, m = st[i], sm[:, i, :]
        ha, hb = s["ha"], s["hb"]
        t = k.v_red(m[:, 4:5], ha.ap, ALU.max, s["th"], absolute=True)
        t = k.v_ts(m[:, 4:5], m[:, 4:5], HN, 1e-5, ALU.mult, ALU.max, t)
        t = k.v_ts(m[:, 4:5], m[:, 4:5], 1.0 / 128, None, ALU.mult, None, t)
        t = k.v_recip(m[:, 5:6], m[:, 4:5], t)
        t1 = k.v_ts(m[:, 5:6], m[:, 5:6], HN, None, ALU.mult, None, t)
        tf = k.v_ts(m[:, 6:7], m[:, 4:5], sc[:, 2:3], None, ALU.mult, None, t)
        t = k.v_ts(ha.ap, ha.ap, m[:, 5:6], 127.0, ALU.mult, ALU.min, t1)
        t = k.v_ts(ha.ap, ha.ap, -128.0, MAGIC, ALU.max, ALU.add, t)
        yb = YB.take()
        t = k.v_ts(yb.ap, ha.ap, MAGIC, None, ALU.subtract, None, t, yb.free)
        ha.done(t)
        hb.done(t, s["th"])
        s["yb"], s["tyb"], s["tf2"] = yb, t, tf

    def d2(i):
        s, m = st[i], sm[:, i, :]
        yb, t, tf = s["yb"], s["tyb"], s["tf2"]
        yt = YT.take()
        te = []
        for c in range(2):
            r = R.take()
            bb = r.ap.bitcast(BF16).rearrange("p (m n) -> p m n", m=8)
            for j in range(8):
                t1 = k.tr(bb[:, j, :], yb.ap[:, (8 * c + j) * P:(8 * c + j + 1) * P], r.free, t, sig=(j == 7))
            te.append(k.acopy(yt.ap[:, 8 * c:8 * c + 8, :], bb, t1, yt.free))
            r.done(te[-1])
        yb.done(t1)
        r = R.take()
        for j in range(16):
            t1 = k.mm(r.ap, yt.ap[:, j, :], WD[:, j, :], j == 0, j == 15, r.free, te, tw[2], sig=(j == 15))
        yt.done(t1)

        def add(z, *w):
            t2 = k.v_stt(z, r.ap, m[:, 6:7], k.X[:, i, :], ALU.mult, ALU.add, tf, *w, k.xtok[i])
            r.done(t2)
            return t2
        k.ln(i, add, t1)

    pipeline(NT, [(0, a), (1, a2), (2, b), (3, c), (4, d), (5, d2)])
    k.ln_flush()


def l1_attn(k):
    nc = k.nc
    k.phase("l1attn")
    k.off = k.base
    ins = k.ins
    xt_off = k.off
    XT = k.alloc([4, 2048])
    YT1, YT2 = k.alloc([2, 2048]), k.alloc([2, 2048])
    BD = k.alloc([2, 256])
    BV = k.alloc([3, 64])
    BR = k.alloc([2, 64])
    ONE = k.alloc([P])
    BP = k.alloc([2, 256])
    PM = k.alloc([P])
    CW = k.alloc([2, 4, 8])
    LB = k.alloc([3, 512])
    mark = k.off
    Q = Ring([k.alloc([8, 8, 24]) for _ in range(3)])
    PR = Ring([k.alloc([4096]) for _ in range(2)])
    S = Ring([k.alloc([8, 8, 8]) for _ in range(2)])
    AA = Ring([k.alloc([8, 8, 8]) for _ in range(2)])
    A2 = Ring([k.alloc([8, 16, 8]) for _ in range(2)])
    LE = Ring([k.alloc([8, 8, 8]) for _ in range(3)])
    mz = Ring([k.alloc([3, 64]) for _ in range(2)])
    tc = [k.dma(BD[:, :, 0:192], ins["L1_bd"]), k.dma(BP, ins["L1_bp"]), k.dma(CW, ins["L1_cw"]), k.dma(LB, ins["L1_lb"])]
    k.pool.wait()
    tc.append(k.pool.sig(nc.gpsimd.memset(ONE, 1.0)))
    BD1 = BD[:, 1, 192:256].rearrange("p (x c) -> p x c", c=8)
    for br in range(2):
        t = k.v_copy(BR[:, br].rearrange("p (x c) -> p x c", c=8), CW[:, br, 3].unsqueeze(1).to_broadcast([P, 8, 8]), tc)
        tc.append(t)
        wv = BD[:, br, 0:192].rearrange("p (x c) -> p x c", c=24)[:, :, 16:24]
        for j in range(3):
            cj = CW[:, br, j].unsqueeze(1)
            if br == 1:
                tc.append(k.v_tt(BV[:, j].rearrange("p (x c) -> p x c", c=8), wv, cj.to_broadcast([P, 8, 8]), ALU.mult))
    wv = BD[:, 0, 0:192].rearrange("p (x c) -> p x c", c=24)[:, :, 16:24]
    l0 = BD[:, 0, 192:256].rearrange("p (x c) -> p x c", c=8)
    t = k.v_tt(l0, wv, CW[:, 0, 1].unsqueeze(1).to_broadcast([P, 8, 8]), ALU.mult)
    t1 = k.v_tt(BD1[:, 0:7], wv[:, 0:7], CW[:, 0, 0].unsqueeze(1).to_broadcast([P, 7, 8]), ALU.mult, t)
    t = k.v_tt(l0[:, 1:8], l0[:, 1:8], BD1[:, 0:7], ALU.add, t1)
    t1 = k.v_tt(BD1[:, 0:7], wv[:, 1:8], CW[:, 0, 2].unsqueeze(1).to_broadcast([P, 7, 8]), ALU.mult, t)
    tc.append(k.v_tt(l0[:, 0:7], l0[:, 0:7], BD1[:, 0:7], ALU.add, t1))
    R = Ring([k.bank(j)[:, 0, :] for j in range(4)])
    R4 = Ring([k.bank(4, 4)])
    SCL = float(8) ** -0.5

    tpm = k.dma(PM, ins["c_perm"])
    XV = XT.rearrange("p k (l r) -> p (k l) r", l=4)
    for i in range(NT):
        r = R.take()
        for c in range(4):
            t = k.mm(r.ap[:, c * P:c * P + P], k.X[:, i, c * P:c * P + P], PM, True, True, r.free, k.xtok[i], tpm,
                     sig=(c == 3))
        col = 256 * (i // 8) + 64 * (i // 4 % 2) + 16 * (i % 4)
        dst = XV[:, :, col:col + 144].rearrange("p m (h n) -> p m h n", n=16)[:, :, 0:9:8]
        src = r.ap.rearrange("p (m h n) -> p m h n", h=2, n=16)
        t = (k.acopy if i % 2 else k.v_copy)(dst, src, t)
        r.done(t)
    txt = [k.act.last, k.dve.last]

    def group(sset, il):
        return 4 * (il % 4) + 2 * sset + il // 4

    ty = []
    NJ = 16
    st = [dict() for _ in range(NJ)]
    hold = {}

    def front(n):
        s = st[n]
        q, le = s["q"], s["le"] = Q.take(), LE.take()
        s["tq"], s["tl"] = [], []
        if n < 8:
            for t2 in range(2):
                i = 2 * n + t2
                for c2 in range(2):
                    r = R.take()
                    for c in range(2):
                        l = XT[:, 2 * c2 + c, i * P:i * P + P]
                        k.mm(r.ap[:, 256 * c:256 * c + 256], l, BD[:, 0, :], True, False, r.free, txt, tc)
                        t = k.mm(r.ap[:, 256 * c + 192:256 * c + 256], ONE[0:1], BR[0:1, 0], False, True, sig=(c == 1))
                    w0 = 4 * t2 + 2 * c2
                    v = r.ap.rearrange("p (w n) -> p w n", w=2)
                    s["tq"].append(k.acopy(q.ap[:, w0:w0 + 2].rearrange("p w i c -> p w (i c)"), v[:, :, 0:192], t, q.free))
                    s["tl"].append(k.acopy(le.ap[:, w0:w0 + 2].rearrange("p w i c -> p w (i c)"), v[:, :, 192:256], t,
                                           le.free))
                    r.done(s["tl"][-1])
            return
        sset, c = (n - 8) // 4, (n - 8) % 4
        r = R4.take()

        def col(il):
            gi = group(sset, il) * P
            return XT[:, c, gi:gi + P]

        for il in range(8):
            t = k.mm(r.ap[:, il // 2, 192 * (il % 2):192 * (il % 2) + 192], col(il), BD[:, 1, 0:192], True, True,
                     r.free, txt, tc, sig=(il % 2 == 1))
            if il % 2:
                src = r.ap[:, il // 2, 0:384].rearrange("p (i w c) -> p w i c", i=2, w=8)
                s["tq"].append(k.acopy(q.ap[:, :, il - 1:il + 1, :].rearrange("p w i c -> p i w c"),
                                       src.rearrange("p w i c -> p i w c"), t, q.free))
        r.done(*s["tq"])
        r = R.take()
        for il in range(8):
            o = r.ap[:, 64 * il:64 * il + 64]
            k.mm(o, ONE[0:1], BR[0:1, 1], True, False, r.free)
            for j in range(3):
                if 0 <= il + j - 1 < 8:
                    last = j == 2 or il == 7 and j == 1
                    t = k.mm(o, col(il + j - 1), BV[:, j], False, last, sig=(il == 7 and last))
        t = k.acopy(le.ap.rearrange("p w i c -> p i w c"), r.ap.rearrange("p (i w c) -> p i w c", i=8, w=8), t, le.free)
        s["tl"].append(t)
        r.done(t)

    def qk(n):
        s = st[n]
        q = s["q"].ap
        s["s"], pr, s["mz"] = S.take(), PR.take(), mz.take()
        s["pr"] = pr
        pv = pr.ap.rearrange("p (w i j c) -> p w i j c", w=8, i=8, j=8)
        s["tp"] = []
        for w in range(8):
            a = q[:, w, :, 0:8].unsqueeze(2).to_broadcast([P, 8, 8, 8])
            b = q[:, w, :, 8:16].unsqueeze(1).to_broadcast([P, 8, 8, 8])
            s["tp"].append((k.v_tt if w % 2 else k.g_tt)(pv[:, w], a, b, ALU.mult, s["tq"], pr.free))

    def soft(n):
        s = st[n]
        pr, m = s["pr"], s["mz"].ap[:, 0, :]
        sf = s["s"].ap.rearrange("p w i j -> p (w i) j")
        s["tred"] = t = k.v_red(s["s"].ap.rearrange("p w i j -> p (w i j)"), pr.ap.rearrange("p (s c) -> p s c", c=8),
                                ALU.add, s["tp"], s["s"].free)
        t = k.v_red(m, sf, ALU.max, t, s["mz"].free)
        t = k.v_tt(sf, sf, m.unsqueeze(2).to_broadcast([P, 64, 8]), ALU.subtract, t)
        s["te"] = k.activ(sf, sf, ACT.Exp, t, scale=SCL)

    def av(n):
        s = st[n]
        q = s["q"].ap
        pv = s["pr"].ap.rearrange("p (w i c j) -> p w i c j", w=8, i=8, c=8)
        s["tp"] = []
        for w in range(8):
            a = s["s"].ap[:, w].unsqueeze(2).to_broadcast([P, 8, 8, 8])
            b = q[:, w, :, 16:24].rearrange("p j c -> p c j").unsqueeze(1).to_broadcast([P, 8, 8, 8])
            s["tp"].append((k.v_tt if w % 2 else k.g_tt)(pv[:, w], a, b, ALU.mult, s["te"], s["tred"]))

    def over(n):
        s = st[n]
        pr = s["pr"]
        z, r = s["mz"].ap[:, 1, :], s["mz"].ap[:, 2, :]
        sf = s["s"].ap.rearrange("p w i j -> p (w i) j")
        t = k.v_red(z, sf, ALU.add, s["te"])
        tr = k.v_recip(r, z, t)
        s["s"].done(t, s["tp"])
        aa = AA.take()
        t = k.v_red(aa.ap.rearrange("p w i c -> p (w i c)"), pr.ap.rearrange("p (s c) -> p s c", c=8), ALU.add, s["tp"],
                    aa.free)
        pr.done(t)
        s["q"].done(s["tp"])
        t = k.v_tt(aa.ap.rearrange("p w i c -> p (w i) c"), aa.ap.rearrange("p w i c -> p (w i) c"),
                   r.unsqueeze(2).to_broadcast([P, 64, 8]), ALU.mult, t, tr)
        s["mz"].done(t)
        if n < 8 or n % 2 == 0:
            hold["a2"] = A2.take()
            hold["t"] = []
        s["a2"] = a2 = hold["a2"]
        le = s["le"]
        if n < 8:
            dst = a2.ap.rearrange("p a b c -> p (a b c)")[:, 0:512].rearrange("p (w i c) -> p w i c", w=8, i=8)
            t3 = k.g_tt(dst, le.ap, aa.ap, ALU.add, t, s["tl"], a2.free)
        else:
            t3 = k.g_tt(a2.ap[:, :, 8 * (n % 2):8 * (n % 2) + 8, :], le.ap.rearrange("p w i c -> p i w c"),
                        aa.ap.rearrange("p w i c -> p i w c"), ALU.add, t, s["tl"], a2.free)
        aa.done(t3)
        le.done(t3)
        hold["t"].append(t3)
        s["td"] = list(hold["t"])

    def back(n):
        s = st[n]
        a2, td = s["a2"], s["td"]
        if n < 8:
            for t2 in range(2):
                i = 2 * n + t2
                r = R.take()
                for h in range(2):
                    c = 256 * t2 + 128 * h
                    t = k.tr(r.ap[:, h * P:h * P + P], a2.ap.rearrange("p a b c -> p (a b c)")[:, c:c + 128],
                             r.free, td, sig=(h == 1))
                te = k.acopy(YT1[:, :, i * P:i * P + P], r.ap[:, 0:256].rearrange("p (h n) -> p h n", h=2), t)
                r.done(te)
                ty.append(te)
            a2.done(t)
        elif n % 2:
            sset, half = (n - 8) // 4, (n - 8) // 2 % 2
            for q4 in range(2):
                r = R.take()
                for j in range(4):
                    il = 4 * q4 + j
                    t = k.tr(r.ap[:, j * P:j * P + P], a2.ap[:, il].rearrange("p w c -> p (w c)"), r.free, td, sig=(j == 3))
                gi = group(sset, 4 * q4) * P
                te = k.acopy(YT2[:, half, :].rearrange("p (l n) -> p l n", l=4)[:, :, gi:gi + P],
                             r.ap.rearrange("p (l n) -> p l n", l=4), t)
                ty.append(te)
                r.done(te)
            a2.done(t)

    front(0)
    for n in range(NJ + 2):
        if n < NJ:
            qk(n)
        if 1 <= n <= NJ:
            av(n - 1)
        if n < NJ:
            soft(n)
        if n + 1 < NJ:
            front(n + 1)
        if n >= 2:
            back(n - 2)
        if 1 <= n <= NJ:
            over(n - 1)
    k.off = mark
    start = [k.dve.last, k.act.last, k.pool.last, k.pe.last]
    TN = k.alloc([16, 16, 32])
    Y = Ring([k.alloc([512]) for _ in range(4)], start)
    Z = Ring([k.alloc([512]) for _ in range(4)], start)
    sm = Ring([k.alloc([4, 32]) for _ in range(4)], start)
    RB = Ring([k.bank(j, 2) for j in (0, 2, 4, 6)])
    for s in RB.free:
        s.extend(start)
    tn = []
    st = [dict() for _ in range(16)]

    def a(rl):
        s = st[rl]
        r = s["r"] = RB.take()
        c0 = 512 * (rl // 4) + rl % 4
        c1 = c0 + 509
        for h in range(2):
            o = r.ap[:, 0, 256 * h:256 * h + 256]
            k.mm(o, YT1[:, h, c0:c1:4], BP[:, 0, :], True, False, r.free, ty)
            t = k.mm(o, YT2[:, h, c0:c1:4], BP[:, 1, :], False, True, sig=(h == 1))
        for c in range(4):
            tt = k.tr(r.ap[:, 1, c * P:c * P + P], XT[:, c, c0:c1:4], sig=(c == 3))
        y, z, m = Y.take(), Z.take(), sm.take()
        s["y"], s["z"], s["m"] = y, z, m
        y3 = y.ap.rearrange("p (x c) -> p x c", c=16)
        z3 = z.ap.rearrange("p (x c) -> p x c", c=16)
        t = k.v_tt(y.ap, r.ap[:, 0, :], LB[:, 0, :], ALU.add, t, y.free)
        t = k.v_red(m.ap[:, 0, :], y3, ALU.add, t, m.free)
        t = k.v_ts(m.ap[:, 0, :], m.ap[:, 0, :], 1.0 / 16, None, ALU.mult, None, t)
        t = k.v_tt(y3, y3, m.ap[:, 0, :].unsqueeze(2).to_broadcast([P, 32, 16]), ALU.subtract, t)
        s["t"] = k.activ(z.ap, y.ap, ACT.Square, t, z.free)
        s["tt"] = tt

    def a2(rl):
        s = st[rl]
        z, m = s["z"], s["m"]
        t = k.v_red(m.ap[:, 1, :], z.ap.rearrange("p (x c) -> p x c", c=16), ALU.add, s["t"])
        t = k.g_ts(m.ap[:, 2, :], m.ap[:, 1, :], 1.0 / 16, 1e-5, ALU.mult, ALU.add, t)
        s["t"] = k.g_tt(m.ap[:, 3, :], m.ap[:, 2, :], k.nhalf, ALU.pow, t)

    def b(rl):
        s = st[rl]
        y, z, m, r = s["y"], s["z"], s["m"], s["r"]
        y3 = y.ap.rearrange("p (x c) -> p x c", c=16)
        t = k.v_tt(y3, y3, m.ap[:, 3, :].unsqueeze(2).to_broadcast([P, 32, 16]), ALU.mult, s["t"])
        m.done(t)
        s["t"] = k.g_tt(y.ap, y.ap, LB[:, 1, :], ALU.mult, t)

    def b2(rl):
        s = st[rl]
        y, z, r = s["y"], s["z"], s["r"]
        t = k.v_tt(z.ap, y.ap, LB[:, 2, :], ALU.add, s["t"])
        y.done(t)
        t = k.v_tt(TN[:, :, rl, :].rearrange("p c x -> p x c"), z.ap.rearrange("p (x c) -> p x c", c=16),
                   r.ap[:, 1, :].rearrange("p (x c) -> p x c", c=16), ALU.add, t, s["tt"])
        z.done(t)
        r.done(t)
        tn.append(t)

    pipeline(16, [(0, a), (1, a2), (2, b), (3, b2)])
    OUT = k.view(xt_off, [NT, 512])
    td = [[] for _ in range(4)]
    for p8 in (0, 2, 1, 3, 4, 6, 5, 7):
        sset, lh, b2 = p8 // 4, p8 // 2 % 2, p8 % 2
        bb = 2 * sset + b2
        for c4 in range(4):
            src = TN[16 * p8:16 * p8 + 16].rearrange("p (t c) r x -> p c t (r x)", c=4)[:, c4]
            p0 = 32 * c4 + lh
            td[bb].append(k.dma(OUT[p0:p0 + 31:2, 4 * bb:4 * bb + 4, :], src, tn, k.pe.last))
    for i in range(NT):
        k.ln(i, k.add_from(i, OUT[:, i, :], None), td[i // 4])
    k.ln_flush()


def layout_rest(a, d, T, rep, f):
    for n in ("L0_ffn_up_w", "L0_ffn_down_w", "L0_ffn_expert_weight", "L0_ffn_gate_w", "L3_attn_Wq"):
        d[n] = np.asarray(a[n])
    d["L0_ffn_ln"] = rep(np.stack([np.asarray(a["L0_ffn_ln_gamma"]), np.asarray(a["L0_ffn_ln_beta"])]), P, 2, 512)
    d["L3_ffn_w1"], d["L3_ffn_w2"] = T(a["L3_ffn_w1"]), T(a["L3_ffn_w2"])
    d["L3_ffn_b1"] = T(np.asarray(a["L3_ffn_b1"]).reshape(16, P))
    d["L3_ffn_b2"] = rep(a["L3_ffn_b2"], P, 512)
    for n in ("gate", "up", "down"):
        d["L1_ffn_w_" + n] = T(a["L1_ffn_w_" + n])
    h = np.ones((1, 1), f)
    while len(h) < P:
        h = np.block([[h, h], [h, -h]]).astype(f)
    d["c_hadamard"] = h
    sel = np.zeros((P, 4, 4, P), f)
    for g in range(4):
        for r in range(3):
            for hg in range(4):
                sel[32 * g + 4 * r + hg, g, hg, :] = 1
    d["c_sel"] = sel
    for lab, names, tr in (("L2_attn", ("WQ", "WK", "WV", "WO"), True), ("L3_attn", ("q", "k", "v", "c"), False)):
        for n, o in zip(names, "qkvo"):
            w, b = (f"{lab}_{n}_w", f"{lab}_{n}_b") if tr else (f"{lab}_W{n}", f"{lab}_b{n}")
            d[f"{lab}_{o}"] = T(a[w]) if tr else np.asarray(a[w])
            d[f"{lab}_b{o}"] = T(np.asarray(a[b]).reshape(4, P)) if o in "qk" else rep(a[b], P, 512)
    d["L2_xattn_q"], d["L2_xattn_o"] = T(a["L2_xattn_Wq"]), T(a["L2_xattn_Wout"])
    kv = T(a["L2_xattn_Wkv_expand"])
    d["L2_xattn_k"], d["L2_xattn_v"] = kv[:, :512], kv[:, 512:]
    d["ctx_T"] = np.ascontiguousarray(np.asarray(a["ctx_512"]).transpose(2, 0, 1))
    d["L3_xattn_W_k"] = T(a["L3_xattn_W_k"])
    d["L3_xattn_b_k"] = np.asarray(a["L3_xattn_b_k"]).reshape(P, 1)
    d["L3_xattn_ln"] = rep(np.stack([np.asarray(a["L3_xattn_ln_gamma"]), np.asarray(a["L3_xattn_ln_beta"])]), P, 2, 512)
    d["L1_xattn_W"] = np.stack([T(a["L1_xattn_Wq"]), T(a["L1_xattn_Wk"])], 1)
    pm = np.zeros((P, P), f)
    q = np.arange(P)
    pm[q, 32 * (q // 4 % 4) + 16 * (q // 16 % 2) + 4 * (q // 32) + q % 4] = 1
    d["c_perm"] = pm
    d["L1_gamma"] = rep(np.asarray(a["L1_xattn_gamma_raw"]).reshape(1, 1), P, 1)
    w = np.asarray(a["L1_attn_qkv_w"])
    bd = np.zeros((8, 16, 2, 8, 24), f)
    pw = np.asarray(a["L1_attn_proj_w"])
    bp = np.zeros((16, 8, 2, 16, 16), f)
    for br in range(2):
        for x in range(8):
            for j in range(3):
                bd[x, :, br, x, 8 * j:8 * j + 8] = w[:, 16 * j + 8 * br:16 * j + 8 * br + 8]
        for x in range(16):
            bp[x, :, br, x, :] = pw[8 * br:8 * br + 8]
    d["L1_bd"] = bd.reshape(P, 2, 192)
    d["L1_bp"] = bp.reshape(P, 2, 256)
    c0, c1 = np.asarray(a["L1_attn_conv_w0"])[:, 0], np.asarray(a["L1_attn_conv_w1"])[:, 0]
    cw = np.stack([np.stack([c0[:, 1, 0], c0[:, 1, 1], c0[:, 1, 2], np.asarray(a["L1_attn_conv_b0"])]),
                   np.stack([c1[:, 0, 1], c1[:, 1, 1], c1[:, 2, 1], np.asarray(a["L1_attn_conv_b1"])])])
    d["L1_cw"] = rep(cw, P, 2, 4, 8)
    lb = np.stack([np.tile(np.asarray(a["L1_attn_" + n]), 32) for n in ("proj_b", "ln_w", "ln_b")])
    d["L1_lb"] = rep(lb, P, 3, 512)
    d["L2_ffn_gate_weight"] = T(a["L2_ffn_gate_weight"])
    gu = np.concatenate([np.asarray(a["L2_ffn_w_gate"]), np.asarray(a["L2_ffn_w_up"])], axis=2)
    d["L2_ffn_gu"] = gu.reshape(NE, 4, P, 384).transpose(0, 2, 1, 3).reshape(NE, P, 1536)
    d["L2_ffn_dn"] = np.asarray(a["L2_ffn_w_down"]).reshape(NE, 2, 96, 512).transpose(0, 2, 1, 3).reshape(NE, 96, 1024)
    sl = np.zeros((P, NB, 2), np.uint32)
    sl[:, :, 0] = 2048 + np.arange(P)[:, None]
    d["c_slots"] = sl.reshape(P, 2 * NB)
    d["c_tokens"] = (np.arange(P)[:, None] + P * np.arange(NT)[None, :]).astype(np.uint32)
    d["c_tri"] = np.stack([np.triu(np.ones((P, P), f), 1), np.ones((P, P), f)], 1)
    d["c_blocks"] = np.concatenate([np.arange(P)[:, None] + np.array([[0, P]]), rep(np.arange(16)[None] * 128, P, 16)],
                                   1).astype(f)
    for n in ("L3_attn_Wq",):
        d.pop(n)
def ternary(k, R, ins):
    nc = k.nc
    k.off = (k.off + 7) // 8 * 8
    offs = [k.off, k.off + 8192]
    F1, F2 = k.alloc([4, 2048]), k.alloc([16, 512])
    W1, W2 = k.rview(offs[0], [4, 2048]), k.rview(offs[1], [16, 512])
    w1, w2 = rows(ins["L3_ffn_w1"]), rows(ins["L3_ffn_w2"])
    tw1 = [k.dma(F1[:, kk, :], w1[:, kk, :]) for kk in range(4)]
    tw2 = [k.dma(F2[:, 4 * j:4 * j + 4, :], w2[:, 4 * j:4 * j + 4, :]) for j in range(4)]
    part, thr, ones = k.alloc([8]), k.alloc([4]), k.alloc([P])
    tmp = Ring([k.alloc([2048]) for _ in range(2)])
    to = k.pool.sig(nc.gpsimd.memset(ones, 1.0))
    cnt = 1.0 / (2048 * 512)
    out = []
    yield
    for n, (F, W, tw) in enumerate(((F1, W1, tw1), (F2, W2, tw2))):
        F, W = F.rearrange("p a b -> p (a b)"), W.rearrange("p a b -> p (a b)")
        tp = []
        for j in range(4):
            tp.append(k.v_red(part[:, 4 * n + j:4 * n + j + 1], F[:, 2048 * j:2048 * j + 2048], ALU.add, tw[j],
                              absolute=True))
            yield
        t = k.v_red(thr[:, 2 * n:2 * n + 1], part[:, 4 * n:4 * n + 4], ALU.add, tp)
        b = R.take()
        t = k.mm(b.ap[:, 0:1], ones, thr[:, 2 * n:2 * n + 1], True, True, b.free, t, to, sig=True)
        t = k.v_ts(thr[:, 2 * n:2 * n + 1], b.ap[:, 0:1], cnt, 0.7, ALU.mult, ALU.mult, t)
        b.done(t)
        t = k.v_ts(thr[:, 2 * n + 1:2 * n + 2], thr[:, 2 * n:2 * n + 1], -1.0, None, ALU.mult, None, t)
        tj = []
        for j in range(4):
            s = tmp.take()
            c = slice(2048 * j, 2048 * j + 2048)
            t2 = k.v_ts(s.ap, F[:, c], thr[:, 2 * n + 1:2 * n + 2], None, ALU.is_le, None, t, s.free)
            t2 = k.v_stt(W[:, c], F[:, c], thr[:, 2 * n:2 * n + 1], s.ap, ALU.is_ge, ALU.subtract, t2)
            s.done(t2)
            tj.append(t2)
            yield
        out.append(tj)
    k.tern = (W1, out[0], W2, out[1])
    yield


def l3_ffn(k):
    nc = k.nc
    k.phase("l3ffn")
    W1, tw1, W2, tw2 = k.tern
    k.off = k.ternoff
    B1 = k.alloc([16])
    B2 = k.alloc([512])
    tc = [k.dma(B1, k.ins["L3_ffn_b1"]), k.dma(B2, k.ins["L3_ffn_b2"])]
    XH, XL = (Ring([k.ralloc([4, 512]) for _ in range(2)]) for _ in range(2))
    HF = Ring([k.alloc([512]) for _ in range(2)])
    HH, HL = (Ring([k.ralloc([512]) for _ in range(4)]) for _ in range(2))
    YS = Ring([k.alloc([512]) for _ in range(3)])
    YB = [k.bank(j)[:, 0, :] for j in range(4)]
    yfree = [[] for _ in range(4)]
    H = Ring([k.bank(4)[:, 0, :], k.bank(5)[:, 0, :]])
    R = Ring([k.bank(6)[:, 0, :], k.bank(7)[:, 0, :]])

    def xt(b):
        h, l = XH.take(), XL.take()
        toks = []
        for t4 in range(4):
            i = 4 * b + t4
            s = R.take()
            bb = s.ap.rearrange("p (k n) -> p k n", k=4)
            for kk in range(4):
                t = k.tr(bb[:, kk, :], k.X[:, i, kk * P:(kk + 1) * P], s.free, k.xtok[i], sig=(kk == 3))
            c = slice(t4 * P, t4 * P + P)
            t = k.acopy(h.ap[:, :, c], bb, t, h.free)
            t2 = k.v_tt(l.ap[:, :, c], bb, h.ap[:, :, c].bitcast(F32), ALU.subtract, t, l.free)
            s.done(t2)
            toks += [t, t2]
        return h, l, toks

    def up(b, m):
        xh, xl, tx = xs[b]
        h = H.take()
        for kk in range(4):
            w = W1[:, kk, m * P:m * P + P]
            k.mm(h.ap, w, xh.ap[:, kk, :], kk == 0, False, h.free, tx, tw1)
            t = k.mm(h.ap, w, xl.ap[:, kk, :], False, kk == 3, sig=(kk == 3))
        f, oh, ol = HF.take(), HH.take(), HL.take()
        t1 = k.activ(f.ap, h.ap, ACT.Gelu, t, f.free, tc, bias=B1[:, m:m + 1])
        t2 = k.activ(oh.ap, h.ap, ACT.Gelu, t, oh.free, tc, bias=B1[:, m:m + 1])
        h.done(t2)
        t3 = k.v_tt(ol.ap, f.ap, oh.ap.bitcast(F32), ALU.subtract, t1, t2, ol.free)
        f.done(t3)
        return oh, ol, [t2, t3]

    def down(b, m, o):
        oh, ol, t = o
        for t4 in range(4):
            c = slice(t4 * P, t4 * P + P)
            k.mm(YB[t4], oh.ap[:, c], W2[:, m, :], m == 0, False, t[0], tw2[m // 4], yfree[t4])
            td = k.mm(YB[t4], ol.ap[:, c], W2[:, m, :], False, m == 15, t[1], sig=(m == 15 or t4 == 3))
            if m == 15:
                ydone[t4] = td
        oh.done(td)
        ol.done(td)

    def finish(i, t4):
        y = YS.take()
        tx = k.g_tt(y.ap, k.X[:, i, :], B2, ALU.add, k.xtok[i], tc, y.free)

        def add(z, *w):
            t = k.v_tt(z, y.ap, YB[t4], ALU.add, tx, *w)
            yfree[t4] = [t]
            y.done(t)
            return t
        k.ln(i, add, ydone[t4])

    xs = {0: xt(0)}
    ydone = [None] * 4
    for b in range(4):
        q = []
        for m in range(16):
            q.append(up(b, m))
            if m >= 2:
                down(b, m - 2, q[m - 2])
            if m == 8 and b < 3:
                xs[b + 1] = xt(b + 1)
        down(b, 14, q[14])
        down(b, 15, q[15])
        for t4 in range(4):
            finish(4 * b + t4, t4)
        for s in xs[b][0:2]:
            s.done(k.pe.last)
    k.ln_flush()
NB = 191
NE = 64


def l2_ffn(k):
    nc = k.nc
    k.phase("l2ffn")
    k.off = k.base
    ins = k.ins
    XD = nc.dram_tensor("moe_x", [2176, 512], F32, kind="Internal").ap()
    YD = nc.dram_tensor("moe_y", [2176, 512], F32, kind="Internal").ap()
    TW = nc.dram_tensor("moe_slots", [P * NB, 2], U32, kind="Internal").ap()
    EB = nc.dram_tensor("moe_experts", [256], I32, kind="Internal").ap()
    TB = k.alloc([NB, 2])
    ER = k.alloc([256])
    TOT = k.alloc([1])
    GU = Ring([k.alloc([4, 384]) for _ in range(4)])
    DN = Ring([k.alloc([2, 512]) for _ in range(6)])
    XG = Ring([k.alloc([512]) for _ in range(4)])
    XT = Ring([k.alloc([4, P]) for _ in range(2)])
    SG = Ring([k.alloc([192]) for _ in range(2)])
    HH = Ring([k.alloc([192]) for _ in range(2)])
    HT = Ring([k.alloc([2, P]) for _ in range(2)])
    YG = Ring([k.alloc([512]) for _ in range(3)])
    end = k.off
    WR = k.alloc([4, NE])
    LX = Ring([k.alloc([4, P]) for _ in range(3)])
    EE = k.alloc([NT, NE])
    ER8 = k.alloc([NT, NE])
    RW = k.alloc([NT, NE])
    MM = k.alloc([NT, NE])
    C = k.alloc([NT + 1, NE])
    TRI = k.alloc([2, P])
    S8 = k.alloc([NT, 8])
    IX = k.alloc([3, NT * 8])
    PAY = k.alloc([NT * 8, 2])
    TOK = k.alloc([NT])
    SC = k.alloc([NT, NE])
    sm = k.alloc([NT, 16])
    m1, m2, m3, m4, m5 = (k.alloc([NT]) for _ in range(5))
    PF = k.alloc([3, NE])
    IO = k.alloc([2 + 16])
    BIG = k.alloc([NE, 16])
    EX = k.alloc([2, 2])
    ZERO = k.alloc([4, 512])
    R = Ring([k.bank(j)[:, 0, :] for j in range(8)])
    tc = [k.dma(WR, rows(ins["L2_ffn_gate_weight"])), k.dma(TRI, ins["c_tri"]), k.dma(IO, ins["c_blocks"]),
          k.dma(TOK.bitcast(U32), ins["c_tokens"])]
    k.pool.wait()
    tz = k.pool.sig(nc.gpsimd.memset(ZERO, 0.0))
    tz2 = k.pool.sig(nc.gpsimd.memset(C[:, 0, :], 0.0))
    yv = YD.rearrange("(t p) d -> p t d", p=P)
    xv = XD.rearrange("(t p) d -> p t d", p=P)
    td = [k.dma(yv[:, 4 * j:min(4 * j + 4, 17), :], ZERO[:, 0:min(4, 17 - 4 * j), :], tz) for j in range(5)]
    tx = [k.dma(xv[:, 16, :], ZERO[:, 0, :], tz)]
    tx += [k.dma(xv[:, 4 * j:4 * j + 4, :], k.X[:, 4 * j:4 * j + 4, :], k.xtok) for j in range(4)]
    tt = k.dma(TW.rearrange("(p a) c -> p (a c)", p=P), ins["c_slots"])
    lx = {}

    def turn(i):
        l = LX.take()
        lx[i] = l, k.x_to_xt(i, R, l.ap, l.free, eng=i % 2)

    def logits(i):
        l, tl = lx[i]
        r = R.take()
        for kk in range(4):
            t = k.mm(r.ap[:, 0:NE], l.ap[:, kk, :], WR[:, kk, :], kk == 0, kk == 3, r.free, tl, tc, sig=(kk == 3))
        l.done(t)
        te = (k.v_copy if i % 2 else k.acopy)(EE[:, i, :], r.ap[:, 0:NE], t)
        r.done(te)

    pipeline(NT, [(0, turn), (2, logits)])
    te = [k.act.last, k.dve.last]

    def wide(ap):
        return ap.unsqueeze(2).to_broadcast([P, NT, NE])

    t = k.v_red(m1, EE, ALU.max, te)
    t = k.v_tt(EE, EE, wide(m1), ALU.subtract, t)
    t = k.activ(EE, EE, ACT.Exp, t)
    t = k.v_red(m2, EE, ALU.add, t)
    t = k.v_recip(m3, m2, t)
    t = k.v_tt(EE, EE, wide(m3), ALU.mult, t)
    k.dve.wait(t)
    for i in range(NT):
        t = k.dve.sig(nc.vector.max(sm[:, i, 0:8], EE[:, i, :]))
    k.dve.wait(t)
    for i in range(NT):
        t = k.dve.sig(nc.vector.match_replace(ER8[:, i, :], sm[:, i, 0:8], EE[:, i, :], -1.0))
    t = tm = k.v_tt(MM, ER8, EE, ALU.not_equal, t)
    for i in range(NT):
        t = k.v_tt(C[:, i + 1, :], C[:, i, :], MM[:, i, :], ALU.add, t, tz2)
    tcum = t
    t = k.v_red(m4, sm[:, :, 0:8], ALU.add, tm)
    t = k.v_recip(m5, m4, t)
    trw = k.v_tt(RW, EE, wide(m5), ALU.mult, t)

    r = R.take()
    t = k.mm(r.ap[:, 0:NE], TRI[:, 1, :], C[:, NT, :], True, True, r.free, tc, tcum, sig=True)
    lim = IO[:, 2:18].unsqueeze(1).to_broadcast([P, NE, 16])
    t = k.v_copy(PF[:, 0, :], r.ap[:, 0:NE], t)
    r.done(t)
    t = k.v_tt(BIG, PF[:, 0, :].unsqueeze(2).to_broadcast([P, NE, 16]), lim, ALU.is_gt, t, tc)
    t = k.v_red(PF[:, 1, :], BIG, ALU.add, t)
    r = R.take()
    t = k.tr(r.ap[0:NE, 0:P], PF[:, 1, :], r.free, t, sig=True)
    t = k.v_copy(BIG.rearrange("p a b -> p (a b)")[0:NE, 0:P], r.ap[0:NE, 0:P], t)
    r.done(t)
    r = R.take()
    t = k.mm(r.ap[:, 0:NE], BIG.rearrange("p a b -> p (a b)")[0:NE, 0:P], TRI[0:NE, 0, 0:NE], True, True, r.free, t,
             sig=True)
    t = k.v_copy(PF[:, 2, :], r.ap[:, 0:NE], t)
    r.done(t)
    tt1 = k.v_red(EX[:, 0, 0:1], PF[:, 1, :], ALU.add, k.dve.last)
    ttot = k.v_copy(TOT.bitcast(I32), EX[:, 0, 0:1], tt1)
    for j in range(2):
        t1 = k.v_ts(BIG.rearrange("p a b -> p (a b)")[:, 0:NE], PF[:, 2, :], IO[:, j:j + 1], None, ALU.is_le, None, t,
                    k.dve.last, k.pe.last)
        t1 = k.v_red(EX[:, 0, j:j + 1], BIG.rearrange("p a b -> p (a b)")[:, 0:NE], ALU.add, t1)
    t1 = k.v_ts(EX[:, 1, :].bitcast(I32), EX[:, 0, :], -1.0, None, ALU.add, None, t1)
    t1 = k.dma(EB.rearrange("(p j) -> p j", p=P), EX[:, 1, :].bitcast(I32), t1)
    te = k.dma(ER[0:1].bitcast(I32), EB.rearrange("(a n) -> a n", a=1), t1)
    tp = k.v_ts(PF[:, 2, :], PF[:, 2, :], 128.0, 1.0, ALU.mult, ALU.add, t1)
    pw = PAY.rearrange("p (i j) c -> p i j c", j=8)
    t3 = k.v_copy(pw[:, :, :, 0].bitcast(U32), TOK.bitcast(U32).unsqueeze(2).to_broadcast([P, NT, 8]), tc)
    ng = 8
    gs = [nc.alloc_semaphore(f"moe_sc{j}") for j in range(ng)]
    B8 = Ring([k.alloc([8, NE]) for _ in range(2)])
    k.pool.wait(tt, t3)
    sl = [dict() for _ in range(NT)]

    def ranks(i):
        r = R.take()
        k.mm(r.ap[:, 0:NE], TRI[:, 0, :], MM[:, i, :], True, False, r.free, tcum)
        t = k.mm(r.ap[:, 0:NE], TRI[:, 1, :], C[:, i, :], False, True, sig=True)
        t = k.v_tt(SC[:, i, :], r.ap[:, 0:NE], PF[:, 2, :], ALU.add, t, tp)
        r.done(t)
        sl[i]["t"] = k.v_tt(SC[:, i, :], SC[:, i, :], MM[:, i, :], ALU.mult, t)

    def top(i):
        k.dve.wait(sl[i]["t"])
        t = k.dve.sig(nc.vector.max(S8[:, i, :], SC[:, i, :]))
        b8 = B8.take()
        te = k.v_tt(b8.ap, SC[:, i, :].unsqueeze(1).to_broadcast([P, 8, NE]),
                    S8[:, i, :].unsqueeze(2).to_broadcast([P, 8, NE]), ALU.is_equal, t, b8.free)
        c = slice(8 * i, 8 * i + 8)
        t = k.v_ts(IX[:, 0, c].bitcast(I32), S8[:, i, :], -1.0, None, ALU.add, None, t)
        te = k.v_tt(b8.ap, b8.ap, RW[:, i, :].unsqueeze(1).to_broadcast([P, 8, NE]), ALU.mult, te, trw)
        t1 = k.v_ts(IX[:, 1, c].bitcast(I32), IX[:, 0, c].bitcast(I32), 127, None, ALU.bitwise_and, None, t)
        t2 = k.v_ts(IX[:, 2, c].bitcast(I32), IX[:, 0, c].bitcast(I32), 7, None, ALU.logical_shift_right, None, t)
        tw = k.v_red(PAY[:, c, 1], b8.ap, ALU.add, te)
        b8.done(tw)
        t = k.v_ts(IX[:, 0, c], IX[:, 1, c].bitcast(I32), float(NB), None, ALU.mult, None, t1, t2)
        t = k.v_tt(IX[:, 1, c].bitcast(U32), IX[:, 0, c], IX[:, 2, c].bitcast(I32), ALU.add, t)
        sl[i]["s"] = [tw, t]

    def scatter(i):
        k.pool.wait(sl[i]["s"])
        for n in range(8 * i, 8 * i + 8):
            s = gs[n % ng]
            if n >= ng:
                k.pool.wait((s, 16 * (n // ng)))
            nc.gpsimd.indirect_dma_start(TW, bass.IndirectOffsetOnAxis(ap=IX[:, 1, n:n + 1].bitcast(U32), axis=0),
                                         PAY[:, n, :].bitcast(U32), None).then_inc(s, 16)

    pipeline(NT, [(0, ranks), (1, top), (2, scatter)])
    tsc = [(s, 16 * (NT * 8 // ng)) for s in gs]
    ttb = k.dma(TB.bitcast(U32), TW.rearrange("(p a) c -> p a c", p=P), tsc)

    wg = ins["L2_ffn_gu"]
    wd = ins["L2_ffn_dn"]
    xs = [nc.alloc_semaphore(f"moe_g{j}") for j in range(4)]
    ys = nc.alloc_semaphore("moe_y")
    st = [dict() for _ in range(NB)]
    k.sp.wait(te, ttot)
    total = nc.sync.value_load(TOT[0:1].bitcast(I32), min_val=P, max_val=NB)

    def load(n):
        s = st[n]
        s["g"], s["d"] = GU.take(), DN.take()
        c = n % P * 2 + n // P
        e = nc.sync.value_load(ER[0:1, c:c + 1].bitcast(I32), min_val=0, max_val=NE - 1)
        kw = dict(cond=total > n) if n >= P else {}
        s["tg"] = k.dma(s["g"].ap.rearrange("p a b -> p (a b)"), wg[bass.ds(e, 1)].rearrange("a p n -> p (a n)"), s["g"].free, **kw)
        s["td"] = k.dma(s["d"].ap[0:96].rearrange("p a b -> p (a b)"), wd[bass.ds(e, 1)].rearrange("a p n -> p (a n)"),
                        s["d"].free, **kw)

    def gather(n):
        s = st[n]
        x = s["x"] = XG.take()
        k.pool.wait(x.free, tx, ttb, (xs[n % 4], 16 * (n // 4)) if n >= 4 else None)
        nc.gpsimd.indirect_dma_start(x.ap, None, XD, bass.IndirectOffsetOnAxis(ap=TB[:, n, 0:1].bitcast(U32), axis=0)
                                     ).then_inc(xs[n % 4], 16)
        s["tx"] = (xs[n % 4], 16 * (n // 4 + 1))

    def a(n):
        s = st[n]
        r = R.take()
        bb = r.ap.rearrange("p (k n) -> p k n", k=4)
        for kk in range(4):
            t = k.tr(bb[:, kk, :], s["x"].ap[:, kk * P:kk * P + P], r.free, s["tx"], sig=(kk == 3))
        s["x"].done(t)
        x = s["xt"] = XT.take()
        s["txt"] = k.acopy(x.ap, bb, t, x.free)
        r.done(s["txt"])

    def up(n):
        s = st[n]
        r = R.take()
        for kk in range(4):
            t = k.mm(r.ap[:, 0:384], s["xt"].ap[:, kk, :], s["g"].ap[:, kk, :], kk == 0, kk == 3, r.free, s["txt"], s["tg"],
                     sig=(kk == 3))
        s["xt"].done(t)
        s["g"].done(t)
        g = SG.take()
        t1 = k.activ(g.ap, r.ap[:, 0:192], ACT.Silu, t, g.free)
        h = s["h"] = HH.take()
        s["th"] = k.v_stt(h.ap, r.ap[:, 192:384], TB[:, n, 1:2], g.ap, ALU.mult, ALU.mult, t1, h.free, ttb)
        g.done(s["th"])
        r.done(s["th"])

    def b(n):
        s = st[n]
        r = R.take()
        for c in range(2):
            t = k.tr(r.ap[0:96, c * P:c * P + P], s["h"].ap[:, 96 * c:96 * c + 96], r.free, s["th"], sig=(c == 1))
        s["h"].done(t)
        h = s["ht"] = HT.take()
        s["tht"] = k.v_copy(h.ap[0:96], r.ap[0:96, 0:256].rearrange("p (c n) -> p c n", c=2), t, h.free)
        r.done(s["tht"])

    def down(n):
        s = st[n]
        r = R.take()
        for c in range(2):
            t = k.mm(r.ap, s["ht"].ap[0:96, c, :], s["d"].ap[0:96, c, :], c == 0, c == 1, r.free, s["tht"], s["td"],
                     sig=(c == 1))
        s["ht"].done(t)
        s["d"].done(t)
        y = s["y"] = YG.take()
        s["ty"] = k.v_copy(y.ap, r.ap, t, y.free)
        r.done(s["ty"])

    def add(n):
        s = st[n]
        k.pool.wait(s["ty"], td, (ys, 16 * n) if n else None)
        nc.gpsimd.indirect_dma_start(YD, bass.IndirectOffsetOnAxis(ap=TB[:, n, 0:1].bitcast(U32), axis=0), s["y"].ap, None,
                                     compute_op=ALU.add).then_inc(ys, 16)
        s["y"].done((ys, 16 * n + 16))

    pipeline(NB, [(0, load), (1, gather), (2, a), (3, up), (4, b), (5, down), (6, add)])
    top = k.W - 8200
    assert k.off <= top
    w = [k.view(top + 2048 * j, [4, 512]) for j in range(4)]
    k.early = w, [k.dma(a, rows(ins["L3_attn" + n])) for a, n in zip(w, ("_q", "_k", "_v", "_o"))]
    YL = Ring([k.view(end, [4, 512]), k.view(end + 2048, [4, 512])])
    for j in range(4):
        y = YL.take()
        t = k.dma(y.ap, yv[:, 4 * j:4 * j + 4, :], y.free, (ys, 16 * NB), k.pe.last, k.dve.last, k.act.last)
        for t4 in range(4):
            k.ln(4 * j + t4, k.add_from(4 * j + t4, y.ap[:, t4, :], None), t)
        k.ln_flush()
        y.done(k.dve.last)
def build(nc, ins, out, layers):
    k = K(nc, ins, out)
    k.start()
    table = [l0_attn, l0_xattn, l0_ffn, l1_attn, l1_xattn, l1_ffn, l2_attn, l2_xattn, l2_ffn,
             l3_attn, l3_xattn, l3_ffn]
    for n in layers:
        table[n](k)
    o = out.rearrange("b (t p) d -> p (b t) d", p=P)
    ts = [k.dma(o[:, 4 * b:4 * b + 4, :], k.X[:, 4 * b:4 * b + 4, :], k.xtok) for b in range(4)]
    k.sp.wait(ts)


def layout(a):
    f = np.float32

    def T(x):
        return np.ascontiguousarray(np.asarray(x).T)

    def rep(x, *shape):
        return np.ascontiguousarray(np.broadcast_to(np.asarray(x), shape))

    d = {}
    d["x"] = np.asarray(a["x"])
    d["ctx_512"] = np.asarray(a["ctx_512"])
    ident = np.eye(P, dtype=f)
    i, j = np.arange(P)[None, :], np.arange(P)[:, None]
    d["c_ident"] = ident
    d["c_masks"] = np.stack([ident, np.where(i > j, f(NEG), f(0)), np.where(j > i, f(NEG), f(0))], 1).astype(f)
    d["c_iota"] = np.stack([i + 1 + 0 * j, np.where(i >= j, i - j, 1e30), 127 - j + 0 * i], 1).astype(f)
    d["c_block"] = (i // 32 == j // 32).astype(f)
    s = np.asarray(a["L0_attn_slope_rate"]).reshape(16)
    d["slope_k"] = rep(s, P, 16)
    d["slope_q"] = np.ascontiguousarray(np.repeat(s.reshape(4, 4).T, 32, axis=0))
    for n in ("L0_attn_W_qkvu", "L0_attn_W_out"):
        d[n] = T(a[n])
    layout_rest(a, d, T, rep, f)
    return d


def kernel(**inputs):
    import concourse.bacc as _bacc
    from concourse.bass_utils import run_bass_kernel_spmd as _run

    nc = _bacc.Bacc("TRN2", target_bir_lowering=False, num_devices=1)
    arrays, ins = {}, {}
    for name, v in layout(inputs).items():
        v = np.ascontiguousarray(v)
        arrays[f"in_{name}"] = v
        ins[name] = nc.dram_tensor(f"in_{name}", v.shape, mybir.dt.from_np(v.dtype), kind="ExternalInput").ap()
    out = nc.dram_tensor("out_0", (4, 512, 512), F32, kind="ExternalOutput").ap()
    build(nc, ins, out, range(12))
    r = _run(nc, [arrays], core_ids=[0])
    return r.results[0]["out_0"]
```
